# Optimizing a Trainium2 kernel written in Bass

```python
import numpy as np
import jax
import jax.numpy as jnp

def _softmax(x, axis=-1):
    return jax.nn.softmax(x, axis=axis)

def _gelu(x):
    return jax.nn.gelu(x, approximate=True)

def _silu(x):
    return jax.nn.silu(x)

def _sigmoid(x):
    return jax.nn.sigmoid(x)

def _layernorm(x, axis=-1, eps=1e-05):
    m = jnp.mean(x, axis=axis, keepdims=True)
    v = jnp.var(x, axis=axis, keepdims=True)
    return (x - m) / jnp.sqrt(v + eps)

def _scatter_add(tgt, idx, src, axis=0):
    return tgt.at[idx].add(src)

def _segment_sum(src, seg, n):
    return jax.ops.segment_sum(src, seg, n)
kernel_name = 'mk_gnn_resnorm_d4_gnn_r32_ca779d'

def setup_inputs(seed: int=0):
    np.random.seed(seed)
    _w = jnp.asarray

    def _rec_inputs():
        import jax
        import jax.numpy as jnp
        _gk = jax.random.key(seed)
        x = -0.000202 + 1 * jax.random.normal(jax.random.fold_in(_gk, 1), (3125, 64), jnp.float32)
        _s = jax.random.randint(jax.random.fold_in(_gk, 2), (50000,), 0, 3125, jnp.int32)
        _d = jax.random.randint(jax.random.fold_in(_gk, 3), (50000,), 0, 3125, jnp.int32)
        _loop = jnp.arange(3125, dtype=jnp.int32)
        src = jnp.concatenate([_s, _d, _loop])
        dst = jnp.concatenate([_d, _s, _loop])
        _o = jnp.argsort(dst, stable=True)
        src = src[_o]
        dst = dst[_o]
        edge_type_16 = jax.random.randint(jax.random.fold_in(_gk, 14), (103125,), 0, 16, jnp.int32)
        node_type_3 = jax.random.randint(jax.random.fold_in(_gk, 15), (3125,), 0, 3, jnp.int32)
        return (x, src, dst, edge_type_16, node_type_3)
    x, src, dst, edge_type_16, node_type_3 = _rec_inputs()

    def _L0_gnn_setup():
        import jax, jax.numpy as jnp
        import numpy as np
        N_NODES = 3125
        N_EDGES = 37500
        D_IN = 64
        D_OUT = 64
        key = jax.random.key(seed)
        ks = jax.random.split(key, 8)
        x = jax.random.normal(ks[0], (N_NODES, D_IN), dtype=jnp.float32)
        norm = jax.random.uniform(ks[1], (N_NODES,), dtype=jnp.float32)
        src = jax.random.randint(ks[2], (N_EDGES,), 0, N_NODES, dtype=jnp.int32)
        dst = jax.random.randint(ks[3], (N_EDGES,), 0, N_NODES, dtype=jnp.int32)
        limit = float(np.sqrt(6.0 / (D_IN + D_OUT)))
        W1 = jax.random.uniform(ks[4], (D_IN, D_OUT), minval=-limit, maxval=limit, dtype=jnp.float32)
        W2 = jax.random.uniform(ks[5], (D_IN, D_OUT), minval=-limit, maxval=limit, dtype=jnp.float32)
        b1 = jnp.zeros((D_OUT,), dtype=jnp.float32)
        b2 = jnp.zeros((D_OUT,), dtype=jnp.float32)
        return {'x': x, 'norm': norm, 'src': src, 'dst': dst, 'W1': W1, 'b1': b1, 'W2': W2, 'b2': b2}
    _L0_gnn_all = _L0_gnn_setup()
    _L0_gnn_in = {k: v for k, v in _L0_gnn_all.items() if k in ('W1', 'b1', 'W2', 'b2')}
    del _L0_gnn_all

    def _L1_gnn_setup():
        import jax, jax.numpy as jnp
        import numpy as np
        N_NODES = 3125
        LEAKY_ALPHA = 0.2
        L2_EPS = 1e-12
        key = jax.random.key(seed)
        ks = jax.random.split(key, 6)
        d = 64
        E = 50000
        x = jax.random.normal(ks[0], (N_NODES, d), dtype=jnp.float32)
        edge_index = jax.random.randint(ks[1], (2, E), 0, N_NODES, dtype=jnp.int32)
        s = 1.0 / np.sqrt(d)
        W_gcn = jax.random.normal(ks[2], (d, d), dtype=jnp.float32) * s
        b_gcn = jnp.zeros((d,), dtype=jnp.float32)
        W_int = jax.random.normal(ks[3], (d, d), dtype=jnp.float32) * s
        b_int = jnp.zeros((d,), dtype=jnp.float32)
        return {'x': x, 'edge_index': edge_index, 'W_gcn': W_gcn, 'b_gcn': b_gcn, 'W_int': W_int, 'b_int': b_int}
    _L1_gnn_all = _L1_gnn_setup()
    _L1_gnn_in = {k: v for k, v in _L1_gnn_all.items() if k in ('W_gcn', 'b_gcn', 'W_int', 'b_int')}
    del _L1_gnn_all

    def _L2_gnn_setup():
        import jax, jax.numpy as jnp
        import numpy as np
        N_NODES = 3125
        N_EDGES = 31250
        D_IN = 64
        D_OUT = 64
        N_RELS = 16
        key = jax.random.key(seed)
        k1, k2, k3, k4, k5 = jax.random.split(key, 5)
        feat = jax.random.normal(k1, (N_NODES, D_IN), dtype=jnp.float32)
        weight = jax.random.normal(k2, (N_RELS, D_IN, D_OUT), dtype=jnp.float32) * 0.05
        src = jax.random.randint(k3, (N_EDGES,), 0, N_NODES)
        dst = jax.random.randint(k4, (N_EDGES,), 0, N_NODES)
        etypes = jax.random.randint(k5, (N_EDGES,), 0, N_RELS)
        return {'feat': feat, 'weight': weight, 'src': src, 'dst': dst, 'etypes': etypes}
    _L2_gnn_all = _L2_gnn_setup()
    _L2_gnn_in = {k: v for k, v in _L2_gnn_all.items() if k in ('weight',)}
    del _L2_gnn_all

    def _L3_gnn_setup():
        import jax, jax.numpy as jnp
        import numpy as np
        N = 50000
        E = 25000
        F = 64
        HID = 64
        HEADS = 4
        NTYPES = 3

        def layer_norm(x, g, b, eps=1e-05):
            mu = x.mean(-1, keepdims=True)
            var = ((x - mu) ** 2).mean(-1, keepdims=True)
            return (x - mu) * jax.lax.rsqrt(var + eps) * g + b

        def gat_conv(x, src, dst, n, W, att_src, att_dst, bias, concat):
            H, C = att_src.shape
            xp = (x @ W).reshape(n, H, C)
            a_s = (xp * att_src).sum(-1)
            a_d = (xp * att_dst).sum(-1)
            e = jax.nn.leaky_relu(a_s[src] + a_d[dst], 0.2)
            m = jax.ops.segment_max(e, dst, num_segments=n)
            ex = jnp.exp(e - m[dst])
            denom = jax.ops.segment_sum(ex, dst, num_segments=n)
            alpha = ex / (denom[dst] + 1e-16)
            msg = xp[src] * alpha[:, :, None]
            out = jax.ops.segment_sum(msg, dst, num_segments=n)
            out = out.reshape(n, H * C) if concat else out.mean(1)
            return out + bias
        key = jax.random.key(seed)
        ks = jax.random.split(key, 12)
        f32 = jnp.float32
        return {'node_features': jax.random.normal(ks[0], (N, F), f32), 'node_types': jax.random.randint(ks[1], (N,), 0, NTYPES), 'edge_index': jax.random.randint(ks[2], (2, E), 0, N), 'type_emb': jax.random.normal(ks[3], (NTYPES, HID), f32) * 0.02, 'proj_W': jax.random.normal(ks[4], (F, HID), f32) / np.sqrt(F).astype(np.float32), 'proj_b': jnp.zeros((HID,), f32), 'W0': jax.random.normal(ks[5], (HID, HEADS * HID), f32) / np.sqrt(HID).astype(np.float32), 'att_src0': jax.random.normal(ks[6], (HEADS, HID), f32) * 0.1, 'att_dst0': jax.random.normal(ks[7], (HEADS, HID), f32) * 0.1, 'bias0': jnp.zeros((HEADS * HID,), f32), 'ln0_g': jnp.ones((HEADS * HID,), f32), 'ln0_b': jnp.zeros((HEADS * HID,), f32), 'W1': jax.random.normal(ks[8], (HEADS * HID, HEADS * HID), f32) / np.sqrt(HEADS * HID).astype(np.float32), 'att_src1': jax.random.normal(ks[9], (HEADS, HID), f32) * 0.1, 'att_dst1': jax.random.normal(ks[10], (HEADS, HID), f32) * 0.1, 'bias1': jnp.zeros((HID,), f32), 'ln1_g': jnp.ones((HID,), f32), 'ln1_b': jnp.zeros((HID,), f32)}
    _L3_gnn_all = _L3_gnn_setup()
    _L3_gnn_in = {k: v for k, v in _L3_gnn_all.items() if k in ('type_emb', 'proj_W', 'proj_b', 'W0', 'att_src0', 'att_dst0', 'bias0', 'ln0_g', 'ln0_b', 'W1', 'att_src1', 'att_dst1', 'bias1', 'ln1_g', 'ln1_b')}
    del _L3_gnn_all
    return {'x': x, 'src': src, 'dst': dst, 'edge_type_16': edge_type_16, 'node_type_3': node_type_3, 'L0_gnn_W1': _L0_gnn_in['W1'], 'L0_gnn_b1': _L0_gnn_in['b1'], 'L0_gnn_W2': _L0_gnn_in['W2'], 'L0_gnn_b2': _L0_gnn_in['b2'], 'L1_gnn_W_gcn': _L1_gnn_in['W_gcn'], 'L1_gnn_b_gcn': _L1_gnn_in['b_gcn'], 'L1_gnn_W_int': _L1_gnn_in['W_int'], 'L1_gnn_b_int': _L1_gnn_in['b_int'], 'L2_gnn_weight': _L2_gnn_in['weight'], 'L3_gnn_type_emb': _L3_gnn_in['type_emb'], 'L3_gnn_proj_W': _L3_gnn_in['proj_W'], 'L3_gnn_proj_b': _L3_gnn_in['proj_b'], 'L3_gnn_W0': _L3_gnn_in['W0'], 'L3_gnn_att_src0': _L3_gnn_in['att_src0'], 'L3_gnn_att_dst0': _L3_gnn_in['att_dst0'], 'L3_gnn_bias0': _L3_gnn_in['bias0'], 'L3_gnn_ln0_g': _L3_gnn_in['ln0_g'], 'L3_gnn_ln0_b': _L3_gnn_in['ln0_b'], 'L3_gnn_W1': _L3_gnn_in['W1'], 'L3_gnn_att_src1': _L3_gnn_in['att_src1'], 'L3_gnn_att_dst1': _L3_gnn_in['att_dst1'], 'L3_gnn_bias1': _L3_gnn_in['bias1'], 'L3_gnn_ln1_g': _L3_gnn_in['ln1_g'], 'L3_gnn_ln1_b': _L3_gnn_in['ln1_b']}

def reference(x, src, dst, edge_type_16, node_type_3, L0_gnn_W1, L0_gnn_b1, L0_gnn_W2, L0_gnn_b2, L1_gnn_W_gcn, L1_gnn_b_gcn, L1_gnn_W_int, L1_gnn_b_int, L2_gnn_weight, L3_gnn_type_emb, L3_gnn_proj_W, L3_gnn_proj_b, L3_gnn_W0, L3_gnn_att_src0, L3_gnn_att_dst0, L3_gnn_bias0, L3_gnn_ln0_g, L3_gnn_ln0_b, L3_gnn_W1, L3_gnn_att_src1, L3_gnn_att_dst1, L3_gnn_bias1, L3_gnn_ln1_g, L3_gnn_ln1_b):
    import jax
    import jax.numpy as jnp

    def _L0_gnn_ref(x, norm, src, dst, W1, b1, W2, b2):
        import jax, jax.numpy as jnp
        import numpy as np
        N_NODES = 3125
        N_EDGES = 37500
        D_IN = 64
        D_OUT = 64
        coef = (norm[src] * norm[dst])[:, None]
        x_src = x[src]
        x_dst = x[dst]
        m1 = x_src * coef
        m2 = x_src * x_dst * coef
        f1 = jax.ops.segment_sum(m1, dst, num_segments=N_NODES)
        f2 = jax.ops.segment_sum(m2, dst, num_segments=N_NODES)
        return f1 @ W1 + b1 + f2 @ W2 + b2

    def _L1_gnn_ref(x, edge_index, W_gcn, b_gcn, W_int, b_int):
        import jax, jax.numpy as jnp
        import numpy as np
        N_NODES = 3125
        LEAKY_ALPHA = 0.2
        L2_EPS = 1e-12
        row, col = (edge_index[0], edge_index[1])
        num_nodes = x.shape[0]
        ones = jnp.ones(row.shape, dtype=x.dtype)
        deg = jax.ops.segment_sum(ones, row, num_segments=num_nodes)
        inv_sqrt_deg = jnp.where(deg > 0, jax.lax.rsqrt(jnp.maximum(deg, 1.0)), 0.0)
        w = inv_sqrt_deg[row] * inv_sqrt_deg[col]
        msgs = w[:, None] * x[col]
        h = jax.ops.segment_sum(msgs, row, num_segments=num_nodes)
        gcn = jax.nn.leaky_relu(h @ W_gcn + b_gcn, negative_slope=LEAKY_ALPHA)
        inter = jax.nn.leaky_relu(x * h @ W_int + b_int, negative_slope=LEAKY_ALPHA)
        out = gcn + inter
        sq = jnp.sum(out * out, axis=-1, keepdims=True)
        out = out * jax.lax.rsqrt(jnp.maximum(sq, L2_EPS))
        return out

    def _L2_gnn_ref(feat, weight, src, dst, etypes):
        import jax, jax.numpy as jnp
        import numpy as np
        N_NODES = 3125
        N_EDGES = 31250
        D_IN = 64
        D_OUT = 64
        N_RELS = 16
        h = feat[src]
        n_rels = weight.shape[0]
        e, d_out = (h.shape[0], weight.shape[2])

        def step(m, rw):
            r, w_r = rw
            mask = jnp.where(etypes == r, 1.0, 0.0).astype(h.dtype)
            m = m + mask[:, None] * (h @ w_r)
            return (m, None)
        m0 = jnp.zeros((e, d_out), dtype=h.dtype)
        m, _ = jax.lax.scan(step, m0, (jnp.arange(n_rels), weight))
        out = jax.ops.segment_sum(m, dst, num_segments=feat.shape[0])
        return out

    def _L3_gnn_ref(node_features, node_types, edge_index, type_emb, proj_W, proj_b, W0, att_src0, att_dst0, bias0, ln0_g, ln0_b, W1, att_src1, att_dst1, bias1, ln1_g, ln1_b):
        import jax, jax.numpy as jnp
        import numpy as np
        N = 50000
        E = 25000
        F = 64
        HID = 64
        HEADS = 4
        NTYPES = 3

        def layer_norm(x, g, b, eps=1e-05):
            mu = x.mean(-1, keepdims=True)
            var = ((x - mu) ** 2).mean(-1, keepdims=True)
            return (x - mu) * jax.lax.rsqrt(var + eps) * g + b

        def gat_conv(x, src, dst, n, W, att_src, att_dst, bias, concat):
            H, C = att_src.shape
            xp = (x @ W).reshape(n, H, C)
            a_s = (xp * att_src).sum(-1)
            a_d = (xp * att_dst).sum(-1)
            e = jax.nn.leaky_relu(a_s[src] + a_d[dst], 0.2)
            m = jax.ops.segment_max(e, dst, num_segments=n)
            ex = jnp.exp(e - m[dst])
            denom = jax.ops.segment_sum(ex, dst, num_segments=n)
            alpha = ex / (denom[dst] + 1e-16)
            msg = xp[src] * alpha[:, :, None]
            out = jax.ops.segment_sum(msg, dst, num_segments=n)
            out = out.reshape(n, H * C) if concat else out.mean(1)
            return out + bias
        n = node_features.shape[0]
        loop = jnp.arange(n)
        src = jnp.concatenate([edge_index[0], loop])
        dst = jnp.concatenate([edge_index[1], loop])
        x = node_features @ proj_W + proj_b + type_emb[node_types]
        h = gat_conv(x, src, dst, n, W0, att_src0, att_dst0, bias0, True)
        h = jax.nn.relu(layer_norm(h, ln0_g, ln0_b))
        h2 = gat_conv(h, src, dst, n, W1, att_src1, att_dst1, bias1, False)
        h2 = jax.nn.relu(layer_norm(h2, ln1_g, ln1_b))
        return h2
    edge_index = jnp.stack([src, dst])
    deg = jnp.maximum(jax.ops.segment_sum(jnp.ones(dst.shape, jnp.float32), dst, num_segments=3125), 1.0)
    deg_isqrt = deg ** (-0.5)
    x = _layernorm(x + _L0_gnn_ref(x, deg_isqrt, src, dst, L0_gnn_W1, L0_gnn_b1, L0_gnn_W2, L0_gnn_b2), axis=-1)
    x = _layernorm(x + _L1_gnn_ref(x, edge_index, L1_gnn_W_gcn, L1_gnn_b_gcn, L1_gnn_W_int, L1_gnn_b_int), axis=-1)
    x = _layernorm(x + _L2_gnn_ref(x, L2_gnn_weight, src, dst, edge_type_16), axis=-1)
    x = _layernorm(x + _L3_gnn_ref(x, node_type_3, edge_index, L3_gnn_type_emb, L3_gnn_proj_W, L3_gnn_proj_b, L3_gnn_W0, L3_gnn_att_src0, L3_gnn_att_dst0, L3_gnn_bias0, L3_gnn_ln0_g, L3_gnn_ln0_b, L3_gnn_W1, L3_gnn_att_src1, L3_gnn_att_dst1, L3_gnn_bias1, L3_gnn_ln1_g, L3_gnn_ln1_b), axis=-1)
    return x

_drawn_inputs = setup_inputs


def setup_inputs(seed=0):
    import zlib

    import numpy as np

    out = dict(_drawn_inputs(seed))
    spreads = {'L0_gnn_b1': (0.0, 0.1),
     'L0_gnn_b2': (0.0, 0.1),
     'L1_gnn_b_gcn': (0.0, 0.1),
     'L1_gnn_b_int': (0.0, 0.1),
     'L3_gnn_proj_b': (0.0, 0.1),
     'L3_gnn_bias0': (0.0, 0.1),
     'L3_gnn_ln0_g': (1.0, 0.2),
     'L3_gnn_ln0_b': (0.0, 0.1),
     'L3_gnn_bias1': (0.0, 0.1),
     'L3_gnn_ln1_g': (1.0, 0.2),
     'L3_gnn_ln1_b': (0.0, 0.1)}
    factors = {'L3_gnn_type_emb': 3.506, 'L3_gnn_att_dst1': 5.498}
    for name, (base, spread) in spreads.items():
        noise = np.random.default_rng([zlib.crc32(name.encode()), seed]).standard_normal(out[name].shape)
        drawn = base * np.exp(spread * noise) if base else spread * noise
        out[name] = jnp.asarray(drawn.astype(out[name].dtype))
    for name, factor in factors.items():
        out[name] = (out[name] * factor).astype(out[name].dtype)
    return out
```

```python
from contextlib import ExitStack

import numpy as np

import concourse.bass as bass
from concourse import mybir

F32, BF16, I32, I16, U8 = (mybir.dt.float32, mybir.dt.bfloat16, mybir.dt.int32,
                           mybir.dt.int16, mybir.dt.uint8)
ALU = mybir.AluOpType
ACT = mybir.ActivationFunctionType
AX = mybir.AxisListType

P = 128
NODES, EDGES, D = 3125, 103125, 64
RELATIONS, HEADS, NODE_TYPES = 16, 4, 3
HD = HEADS * D
BLOCKS = -(-NODES // P)
PADDED = BLOCKS * P
TILES = -(-EDGES // P)
ITEMS = TILES + BLOCKS - 1
NO_NODE = 4095
BANK = 512
LN_EPS = 1e-5
CHUNKS = [(c, min(c + BANK, PADDED)) for c in range(0, PADDED, BANK)]


class Chain:

    def __init__(self, engine, semaphore):
        self.engine, self.semaphore, self.count = engine, semaphore, 0

    def __call__(self, instruction):
        instruction.then_inc(self.semaphore, 1)
        self.count += 1
        self.engine.wait_ge(self.semaphore, self.count)


class Core:

    def __init__(self, nc, ctx, ins, out):
        self.nc, self.ctx, self.ins, self.out = nc, ctx, ins, out
        sb = self.sb
        self.counts = sb("counts", [P, BLOCKS, PADDED], BF16)
        self.mask = self.counts[:, 0:BLOCKS // 2 + 1, :].rearrange("p b s -> p (b s)")\
            [:, 0:BLOCKS * PADDED // 2].bitcast(U8).rearrange("p (b s) -> p b s", b=BLOCKS)
        self.words = sb("item_words", [P, ITEMS], I32)
        self.dloc = sb("item_dst", [P, ITEMS], F32)
        self.block_of = sb("block_of", [1, ITEMS], I32)
        self.bounds = sb("item_bounds", [1, 32], I32)
        self.x = sb("x_nodes", [P, BLOCKS, D], F32)
        self.ident = sb("ident", [P, P], F32)
        self.ident16 = sb("ident16", [P, P], BF16)
        self.ones = sb("ones", [P, P], F32)
        self.ones16 = sb("ones16", [P, 1], BF16)
        self.iota = sb("iota128", [P, P], F32)
        self.eps = sb("eps", [P, 1], F32)
        self.deg = sb("deg", [P, BLOCKS, len(CHUNKS)], F32)
        self.stat = sb("stat", [P, 4, BLOCKS], F32)
        self.psum = ctx.enter_context(nc.psum_tensor("psum", [P, 8 * BANK], F32))

    def sb(self, name, shape, dtype, ctx=None):
        return (ctx or self.ctx).enter_context(self.nc.sbuf_tensor(name, shape, dtype))

    def tail_views(self, *wanted):
        flat = self.counts[:, :, :].rearrange("p b s -> p (b s)")
        at, views = BLOCKS * PADDED // 2, []
        for shape, dtype in wanted:
            size = int(np.prod(shape[1:]))
            cols = size * {F32: 4, I32: 4, BF16: 2}[dtype] // 2
            view = flat[:, at:at + cols].bitcast(dtype) if dtype is not BF16 else flat[:, at:at + cols]
            at += cols
            letters = "abc"[:len(shape) - 1]
            if len(letters) > 1:
                view = view.rearrange(f"p ({' '.join(letters)}) -> p {' '.join(letters)}",
                                      **dict(zip(letters[:-1], shape[1:-1])))
            views.append(view)
        assert at <= BLOCKS * PADDED
        return views

    def sem(self, name, ctx=None):
        return (ctx or self.ctx).enter_context(self.nc.semaphore(name))

    def bank(self, n, count=1):
        return self.psum[:, n * BANK:(n + count) * BANK]


def prepare(core):
    nc, ins = core.nc, core.ins
    with ExitStack() as stage:
        sb = lambda *a: core.sb(*a, stage)
        sem = lambda n: core.sem(n, stage)
        raw_src, raw_dst, raw_rel = (sb(n, [P, TILES], I32) for n in ("raw_src", "raw_dst", "raw_rel"))
        dst_f = core.counts[:, 0, 0:2 * TILES].bitcast(F32)
        below = core.counts[:, 1, 0:TILES]
        item_w = core.counts[:, 2, 0:2 * ITEMS].bitcast(F32)
        item_i = core.counts[:, 3, 0:2 * ITEMS].bitcast(I32)
        starts = sb("starts", [P, BLOCKS - 1], F32)
        start_col, start_row = sb("start_col", [P, 1], I32), sb("start_row", [1, BLOCKS - 1], I32)
        first_col = sb("first_col", [P, 1], F32)
        col_no, row_no = sb("col_no", [P, 1], F32), sb("row_no", [1, BLOCKS - 1], F32)
        reached = core.counts[:, 4, 0:2 * ITEMS].bitcast(F32)
        block_f = core.counts[:, 5, 0:2 * ITEMS].bitcast(F32)
        item_words = core.counts[:, 6, 0:2 * ITEMS].bitcast(I32)
        mask = core.counts[:, 7, 0:2 * TILES].bitcast(I32)
        loaded, constant, step = sem("p_loaded"), sem("p_constant"), sem("p_step")
        counted, summed = sem("p_counted"), sem("p_summed")
        reach_ready, blocks_ready = sem("p_reach"), sem("p_blocks")
        with nc.Block() as block:
            @block.sync
            def _(sp):
                sp.dma_start(raw_dst[:, :], ins["dst"]).then_inc(loaded, 16)
                sp.dma_start(raw_src[:, :], ins["src"]).then_inc(loaded, 16)
                sp.dma_start(raw_rel[:, :], ins["rel"]).then_inc(loaded, 16)
                sp.dma_start(core.x[:, :, :], ins["x"]).then_inc(loaded, 16)
                sp.wait_ge(loaded, 64)

            @block.gpsimd
            def _(pool):
                chain = Chain(pool, constant)
                chain(pool.memset(core.ident[:, :], 0.0))
                chain(pool.affine_select(out=core.ident[:, :], in_=core.ident[:, :], compare_op=ALU.not_equal,
                                         fill=1.0, base=0, pattern=[[-1, P]], channel_multiplier=1))
                pool.tensor_copy(core.ident16[:, :], core.ident[:, :]).then_inc(constant, 1)
                pool.memset(core.ones[:, :], 1.0).then_inc(constant, 1)
                pool.memset(core.ones16[:, :], 1.0).then_inc(constant, 1)
                pool.memset(core.eps[:, :], LN_EPS).then_inc(constant, 1)
                for tile, pattern, base, by_partition in (
                        (core.iota[:, :], [[1, P]], 0, 0), (item_w, [[1, ITEMS]], 0, 0),
                        (col_no[:, :], [[1, 1]], 1, 1), (row_no[:, :], [[1, BLOCKS - 1]], 1, 0)):
                    pool.iota(tile, pattern, base=base, channel_multiplier=by_partition,
                              allow_small_or_imprecise_dtypes=True).then_inc(constant, 1)

            @block.vector
            def _(dve):
                chain = Chain(dve, step)
                dve.wait_ge(loaded, 64)
                dve.wait_ge(constant, 10)
                chain(nc.vector.tensor_copy(dst_f, raw_dst[:, :]))
                for k in range(BLOCKS - 1):
                    chain(nc.vector.tensor_scalar(below, dst_f, float(P * (k + 1)), 0.0, ALU.is_lt, ALU.add,
                                                  accum_out=starts[:, k:k + 1]))
                nc.vector.memset(core.bounds[:, :], 0).then_inc(counted, 1)
                dve.wait_ge(summed, 1)
                chain(nc.vector.tensor_copy(start_col[0:BLOCKS - 1, :], core.psum[0:BLOCKS - 1, 0:1]))
                chain(nc.vector.tensor_copy(start_row[:, :], core.psum[0:1, BANK:BANK + BLOCKS - 1]))
                chain(nc.vector.tensor_scalar(start_col[0:BLOCKS - 1, :], start_col[0:BLOCKS - 1, :], 7, None,
                                              ALU.arith_shift_right))
                chain(nc.vector.tensor_scalar(start_row[:, :], start_row[:, :], 7, None, ALU.arith_shift_right))
                chain(nc.vector.tensor_tensor(first_col[0:BLOCKS - 1, :], start_col[0:BLOCKS - 1, :],
                                              col_no[0:BLOCKS - 1, :], ALU.add))
                chain(nc.vector.tensor_tensor(core.bounds[:, 1:BLOCKS], start_row[:, :], row_no[:, :], ALU.add))
                chain(nc.vector.memset(core.bounds[:, BLOCKS:BLOCKS + 1], ITEMS))
                nc.vector.tensor_scalar(reached[0:BLOCKS - 1, :], item_w[0:BLOCKS - 1, :],
                                        first_col[0:BLOCKS - 1, 0:1], None, ALU.is_ge).then_inc(reach_ready, 1)
                dve.wait_ge(blocks_ready, 1)
                chain(nc.vector.tensor_copy(block_f, core.psum[:, 2 * BANK:2 * BANK + ITEMS]))
                chain(nc.vector.tensor_copy(core.block_of[:, :], block_f[0:1, :]))
                chain(nc.vector.scalar_tensor_tensor(raw_src[:, :], raw_src[:, :], float(RELATIONS), raw_rel[:, :],
                                                     ALU.mult, ALU.add))
                chain(nc.vector.tensor_scalar(raw_dst[:, :], raw_dst[:, :], 16, None, ALU.logical_shift_left))
                chain(nc.vector.tensor_tensor(raw_dst[:, :], raw_dst[:, :], raw_src[:, :], ALU.bitwise_or))
                chain(nc.vector.tensor_copy(item_words[:, 0:TILES], raw_dst[:, :]))
                for b in range(1, BLOCKS):
                    window = slice(b, b + TILES)
                    chain(nc.vector.tensor_scalar(mask, block_f[:, window], float(b), None, ALU.is_ge))
                    chain(nc.vector.copy_predicated(item_words[:, window], mask, raw_dst[:, :]))
                chain(nc.vector.tensor_scalar(core.words[:, :], item_words, 0xFFFF, None, ALU.bitwise_and))
                chain(nc.vector.tensor_scalar(item_i, item_words, 16, None, ALU.logical_shift_right))
                chain(nc.vector.scalar_tensor_tensor(core.dloc[:, :], block_f, float(-P), item_i,
                                                     ALU.mult, ALU.add))

            @block.tensor
            def _(pe):
                pe.wait_ge(constant, 10)
                pe.wait_ge(counted, 1)
                nc.tensor.matmul(core.psum[0:BLOCKS - 1, 0:1], starts[:, :], core.ones[:, 0:1],
                                 start=True, stop=True)
                nc.tensor.matmul(core.psum[0:1, BANK:BANK + BLOCKS - 1], core.ones[:, 0:1], starts[:, :],
                                 start=True, stop=True).then_inc(summed, 1)
                pe.wait_ge(reach_ready, 1)
                for at in (0, BANK):
                    end = min(at + BANK, ITEMS)
                    last = nc.tensor.matmul(core.psum[:, 2 * BANK + at:2 * BANK + end], core.ones[0:BLOCKS - 1, :],
                                            reached[0:BLOCKS - 1, at:end], start=True, stop=True)
                last.then_inc(blocks_ready, 1)


def count_edges(core):
    nc = core.nc
    with ExitStack() as stage:
        sb = lambda *a: core.sb(*a, stage)
        sem = lambda n: core.sem(n, stage)
        source_no = sb("source_no", [P, PADDED], I16)
        source = sb("item_source", [P, ITEMS], F32)
        src_hot = sb("src_hot", [P, 2, PADDED], BF16)
        dst_hot = sb("dst_hot", [P, 2, P], BF16)
        zeros = sb("zeros16", [P, BANK], BF16)
        iota_ready, source_ready = sem("c_iota"), sem("c_source")
        zeros_ready = sem("c_zeros")
        hots_ready, items_added, banks_stored = sem("c_hots"), sem("c_added"), sem("c_stored")
        banks = len(CHUNKS)
        with nc.Block() as block:
            @block.gpsimd
            def _(pool):
                pool.iota(source_no[:, :], [[1, PADDED]], base=0, channel_multiplier=0).then_inc(iota_ready, 1)
                pool.memset(zeros[:, :], 0.0).then_inc(zeros_ready, 1)

            @block.vector
            def _(dve):
                words = source[:, :].bitcast(I32)
                chain = Chain(dve, source_ready)
                chain(nc.vector.tensor_scalar(words, core.words[:, :], 4, None, ALU.logical_shift_right))
                chain(nc.vector.tensor_copy(source[:, :], words))
                dve.wait_ge(iota_ready, 1)

                def one_hots(slot, w):
                    col = slice(w, w + 1) if isinstance(w, int) else bass.ds(w, 1)
                    nc.vector.tensor_scalar(dst_hot[:, slot, :], core.iota[:, :], core.dloc[:, col], None,
                                            ALU.is_equal)
                    nc.vector.tensor_scalar(src_hot[:, slot, :], source_no[:, :], source[:, col], None,
                                            ALU.is_equal).then_inc(hots_ready, 1)

                one_hots(0, 0)
                one_hots(1, 1)
                with dve.Fori(1, ITEMS // 2) as pair:
                    for slot in range(2):
                        dve.wait_ge(items_added, pair * 2 - 1 + slot)
                        one_hots(slot, pair * 2 + slot)

            @block.tensor
            def _(pe):
                pe.wait_ge(zeros_ready, 1)

                def block_counts(b):
                    first = pe.value_load(core.bounds[0:1, bass.ds(b, 1)], min_val=0, max_val=ITEMS - 1)
                    end = pe.value_load(core.bounds[0:1, bass.ds(b + 1, 1)], min_val=1, max_val=ITEMS)
                    for n, (lo, hi) in enumerate(CHUNKS):
                        if not isinstance(b, int):
                            pe.wait_ge(banks_stored, b * banks - (banks - 1 - n))
                        nc.tensor.matmul(core.psum[:, lo:hi], zeros[:, 0:P], zeros[:, 0:hi - lo],
                                         start=True, stop=True, skip_group_check=True)
                    with pe.Fori(first, end) as w:
                        pe.wait_ge(hots_ready, w + 1)
                        for lo, hi in CHUNKS:
                            last = nc.tensor.matmul(core.psum[:, lo:hi], dst_hot[:, bass.ds(w % 2, 1), :],
                                                    src_hot[:, bass.ds(w % 2, 1), lo:hi],
                                                    start=False, stop=True, skip_group_check=True)
                        last.then_inc(items_added, 1)

                block_counts(0)
                with pe.Fori(1, BLOCKS) as b:
                    block_counts(b)

            @block.scalar
            def _(act):
                with act.Fori(0, BLOCKS) as b:
                    end = act.value_load(core.bounds[0:1, bass.ds(b + 1, 1)], min_val=1, max_val=ITEMS)
                    act.wait_ge(items_added, end)
                    for n, (lo, hi) in enumerate(CHUNKS):
                        nc.scalar.activation(core.counts[:, bass.ds(b, 1), lo:hi], core.psum[:, lo:hi], ACT.Copy,
                                             accum_out=core.deg[:, bass.ds(b, 1), n:n + 1])\
                          .then_inc(banks_stored, 1)


def transposed_nodes(core, banks_ready, src, width, dst, copied, first_bank=0):
    nc = core.nc

    def on_tensor(pe):
        for b in range(BLOCKS):
            last = nc.tensor.transpose(core.psum[0:width, b * P:(b + 1) * P], src[:, b, :], core.ident[:, :])
            if b % 4 == 3 or b == BLOCKS - 1:
                last.then_inc(banks_ready, 1)

    def on_scalar(act):
        for n, (lo, hi) in enumerate(CHUNKS):
            act.wait_ge(banks_ready, n + 1)
            nc.scalar.activation(dst[0:width, lo:hi], core.psum[0:width, lo:hi], ACT.Copy).then_inc(copied, 1)

    return on_tensor, on_scalar


def bcast(ap, shape):
    return ap.to_broadcast(shape)


def layernorm(core, chain, act_turn, dve_turn, x, work, stat):
    nc = core.nc
    total, var = stat[:, 0, :], stat[:, 1, :]
    width = x.shape[2]
    chain(nc.vector.tensor_reduce(total, x, AX.X, ALU.add))
    chain(nc.vector.tensor_scalar(total, total, 1.0 / width, None, ALU.mult))
    chain(nc.vector.tensor_tensor(x, x, total.unsqueeze(2).to_broadcast(x.shape), ALU.subtract))
    chain(nc.vector.tensor_tensor(work, x, x, ALU.mult))
    nc.vector.tensor_reduce(var, work, AX.X, ALU.add).then_inc(dve_turn, 1)
    chain.engine.wait_ge(act_turn, 1)
    chain(nc.vector.reciprocal(total, stat[:, 2, :]))
    chain(nc.vector.tensor_tensor(x, x, total.unsqueeze(2).to_broadcast(x.shape), ALU.mult))


def layernorm_root(core, act, dve_turn, act_turn, stat, width):
    act.wait_ge(dve_turn, 1)
    core.nc.scalar.activation(stat[:, 2, :], stat[:, 1, :], ACT.Sqrt, bias=core.eps[:, 0:1],
                              scale=1.0 / width).then_inc(act_turn, 1)


def split_parts(nc, chain, value, parts):
    hi, mid, lo = (parts[:, :, k * D:(k + 1) * D] for k in range(3))
    chain(nc.vector.tensor_copy(hi, value))
    chain(nc.vector.tensor_tensor(value, value, hi, ALU.subtract))
    chain(nc.vector.tensor_copy(mid, value))
    chain(nc.vector.tensor_tensor(lo, value, mid, ALU.subtract))


def bilinear_layer(core):
    nc, ins = core.nc, core.ins
    with ExitStack() as stage:
        sb = lambda *a: core.sb(*a, stage)
        sem = lambda n: core.sem(n, stage)
        stack = sb("b_stack", [P, BLOCKS, 2 * D], F32)
        wide = sb("b_wide", [P, PADDED], F32)
        parts = wide[:, 0:BLOCKS * 3 * D // 2].bitcast(BF16).rearrange("p (b k) -> p b k", b=BLOCKS)
        turned = sb("b_turned", [P, 2, 7, P], BF16)
        weights = sb("b_weights", [P, D], F32)
        bias = sb("b_bias", [P, 2, D], F32)
        norm = core.stat[:, 3, :]
        loaded, step, root_of, rooted = sem("b_loaded"), sem("b_step"), sem("b_rootof"), sem("b_rooted")
        parts_ready, turned_in_psum, turned_ready = sem("b_parts"), sem("b_tpsum"), [sem("b_turned0"), sem("b_turned1")]
        turned_used, sums_stored = sem("b_used"), sem("b_sumstored")
        stack_ready, banks_ready, copied, products = sem("b_stack_s"), sem("b_banks"), sem("b_copied"), sem("b_prod")
        ln_var, ln_root = sem("b_lnvar"), sem("b_lnroot")
        groups = [range(0, 7), range(7, 13), range(13, 19), range(19, 25)]
        turned_psum = [core.bank(k).bitcast(BF16).rearrange("p (t d) -> p t d", d=P) for k in (0, 1)]
        sums = core.bank(2)[:, 0:3 * D]
        on_tensor, on_scalar = transposed_nodes(core, banks_ready, stack, P, wide, copied)
        with nc.Block() as block:
            @block.sync
            def _(sp):
                sp.dma_start(weights[0:D, :], ins["w_f"]).then_inc(loaded, 16)
                sp.dma_start(weights[D:P, :], ins["w_xf"]).then_inc(loaded, 16)
                for k, name in enumerate(("b_f", "b_xf")):
                    sp.dma_start(bias[:, k, :], ins[name].to_broadcast([P, D])).then_inc(loaded, 16)

            @block.vector
            def _(dve):
                chain = Chain(dve, step)
                dve.sem_inc(sums_stored, 1)
                chain(nc.vector.tensor_reduce(norm, core.deg[:, :, :], AX.X, ALU.add))
                nc.vector.tensor_scalar(norm, norm, 1.0, None, ALU.max).then_inc(root_of, 1)
                dve.wait_ge(rooted, 1)
                chain(nc.vector.reciprocal(norm, core.stat[:, 2, :]))
                value = stack[:, :, 0:D]
                per_node = norm.unsqueeze(2).to_broadcast([P, BLOCKS, D])
                chain(nc.vector.tensor_tensor(value, core.x[:, :, :], per_node, ALU.mult))
                split_parts(nc, chain, value, parts)
                nc.vector.memset(core.stat[:, 0, :], 0.0).then_inc(parts_ready, 1)
                with dve.Fori(0, BLOCKS) as b:
                    for n, group in enumerate(groups):
                        if n % 2:
                            dve.wait_ge(turned_in_psum, b * 4 + (n + 1))
                            dve.wait_ge(turned_used, b * 4 + (n + 1))
                            nc.vector.tensor_copy(turned[:, 1, 0:len(group), :],
                                                  turned_psum[1][:, 0:len(group), :]).then_inc(turned_ready[1], 1)
                    dve.wait_ge(turned_used, b * 4 + 6)
                    nc.vector.tensor_reduce(stack[:, bass.ds(b, 1), 0:D], sums.rearrange("p (k f) -> p f k", k=3),
                                            AX.X, ALU.add).then_inc(sums_stored, 1)
                dve.wait_ge(sums_stored, BLOCKS + 1)
                chain(nc.vector.tensor_tensor(value, value, per_node, ALU.mult))
                nc.vector.tensor_tensor(stack[:, :, D:2 * D], value, core.x[:, :, :], ALU.mult).then_inc(stack_ready, 1)
                dve.wait_ge(loaded, 64)
                chain(nc.vector.tensor_tensor(bias[:, 0, :], bias[:, 0, :], bias[:, 1, :], ALU.add))
                chain(nc.vector.tensor_tensor(core.x[:, :, :], core.x[:, :, :],
                                              bias[:, 0:1, :].to_broadcast([P, BLOCKS, D]), ALU.add))
                dve.wait_ge(products, 1)
                chain(nc.vector.tensor_tensor(core.x[:, :, :], core.x[:, :, :],
                                              core.psum[:, 0:BLOCKS * D].rearrange("p (b f) -> p b f", f=D), ALU.add))
                layernorm(core, chain, ln_root, ln_var, core.x[:, :, :], stack[:, :, 0:D], core.stat)

            @block.scalar
            def _(act):
                act.wait_ge(root_of, 1)
                nc.scalar.activation(core.stat[:, 2, :], norm, ACT.Sqrt).then_inc(rooted, 1)
                with act.Fori(0, BLOCKS) as b:
                    for n, group in enumerate(groups):
                        if n % 2 == 0:
                            act.wait_ge(turned_in_psum, b * 4 + (n + 1))
                            act.wait_ge(turned_used, b * 4 + (n + 1))
                            nc.scalar.activation(turned[:, 0, 0:len(group), :], turned_psum[0][:, 0:len(group), :],
                                                 ACT.Copy).then_inc(turned_ready[0], 1)
                on_scalar(act)
                layernorm_root(core, act, ln_var, ln_root, core.stat, D)

            @block.tensor
            def _(pe):
                pe.sem_inc(turned_used, 2)
                pe.wait_ge(parts_ready, 1)

                def turn(b, n):
                    for t, j in enumerate(groups[n]):
                        last = nc.tensor.transpose(turned_psum[n % 2][:, t, :],
                                                   core.counts[:, bass.ds(b, 1), j * P:(j + 1) * P],
                                                   core.ident16[:, :])
                    last.then_inc(turned_in_psum, 1)

                with pe.Fori(0, BLOCKS) as b:
                    turn(b, 0)
                    turn(b, 1)
                    pe.wait_ge(sums_stored, b + 1)
                    for n, group in enumerate(groups):
                        pe.wait_ge(turned_ready[n % 2], b * 2 + (n // 2 + 1))
                        for t, j in enumerate(group):
                            last = nc.tensor.matmul(sums, turned[:, n % 2, t, :], parts[:, j, :],
                                                    start=(j == 0), stop=(j == BLOCKS - 1))
                        last.then_inc(turned_used, 1)
                        if n < 2:
                            turn(b, n + 2)
                pe.wait_ge(stack_ready, 1)
                on_tensor(pe)
                pe.wait_ge(copied, len(CHUNKS))
                pe.wait_ge(loaded, 64)
                for b in range(BLOCKS):
                    last = nc.tensor.matmul(core.psum[:, b * D:(b + 1) * D], wide[:, b * P:(b + 1) * P],
                                            weights[:, :], start=True, stop=True)
                last.then_inc(products, 1)


def interaction_layer(core):
    nc, ins = core.nc, core.ins
    with ExitStack() as stage:
        sb = lambda *a: core.sb(*a, stage)
        sem = lambda n: core.sem(n, stage)
        stack = sb("i_stack", [P, BLOCKS, 2 * D], F32)
        wide = sb("i_wide", [P, PADDED], F32)
        parts = wide[:, 0:BLOCKS * 3 * D // 2].bitcast(BF16).rearrange("p (b k) -> p b k", b=BLOCKS)
        weights = sb("i_weights", [P, 2 * D], F32)
        bias = sb("i_bias", [P, 1, 2 * D], F32)
        norm, root = core.stat[:, 3, :], core.stat[:, 2, :]
        has_edges = core.stat[:, 0, :]
        loaded, cleared, step = sem("i_loaded"), sem("i_cleared"), sem("i_step")
        degrees, root_of, rooted = sem("i_degrees"), sem("i_rootof"), sem("i_rooted")
        norm_of, normed = sem("i_normof"), sem("i_normed")
        parts_ready, sums_ready, sums_stored = sem("i_parts"), sem("i_sums"), sem("i_stored")
        stack_ready, banks_ready, copied, products = sem("i_stack_s"), sem("i_banks"), sem("i_copied"), sem("i_prod")
        ln_var, ln_root = sem("i_lnvar"), sem("i_lnroot")
        sums = [core.bank(k)[:, 0:3 * D] for k in (0, 1)]
        on_tensor, on_scalar = transposed_nodes(core, banks_ready, stack, P, wide, copied)
        with nc.Block() as block:
            @block.gpsimd
            def _(pool):
                pool.memset(weights[:, :], 0.0).then_inc(cleared, 1)

            @block.sync
            def _(sp):
                sp.wait_ge(cleared, 1)
                sp.dma_start(weights[0:D, 0:D], ins["w_gcn"]).then_inc(loaded, 16)
                sp.dma_start(weights[D:P, D:2 * D], ins["w_int"]).then_inc(loaded, 16)
                sp.dma_start(bias[:, 0, 0:D], ins["b_gcn"].to_broadcast([P, D])).then_inc(loaded, 16)
                sp.dma_start(bias[:, 0, D:2 * D], ins["b_int"].to_broadcast([P, D])).then_inc(loaded, 16)

            @block.tensor
            def _(pe):
                with pe.Fori(0, BLOCKS) as j:
                    for b in range(BLOCKS):
                        last = nc.tensor.matmul(core.bank(7)[:, bass.ds(j, 1)],
                                                core.counts[:, b, bass.ds(j * P, P)], core.ones16[:, :],
                                                start=(b == 0), stop=(b == BLOCKS - 1))
                    last.then_inc(degrees, 1)
                pe.wait_ge(parts_ready, 1)

                def gather_sources(j, slot, turn):
                    pe.wait_ge(sums_stored, turn)
                    for b in range(BLOCKS):
                        last = nc.tensor.matmul(sums[slot], core.counts[:, b, bass.ds(j * P, P)], parts[:, b, :],
                                                start=(b == 0), stop=(b == BLOCKS - 1))
                    last.then_inc(sums_ready, 1)

                with pe.Fori(0, BLOCKS // 2) as pair:
                    for slot in range(2):
                        gather_sources(pair * 2 + slot, slot, pair * 2 + (slot + 1))
                gather_sources(BLOCKS - 1, 0, BLOCKS)
                pe.wait_ge(stack_ready, 1)
                on_tensor(pe)
                pe.wait_ge(copied, len(CHUNKS))
                pe.wait_ge(loaded, 64)
                for b in range(BLOCKS):
                    last = nc.tensor.matmul(core.psum[:, b * P:(b + 1) * P], wide[:, b * P:(b + 1) * P],
                                            weights[:, :], start=True, stop=True)
                last.then_inc(products, 1)

            @block.scalar
            def _(act):
                act.wait_ge(root_of, 1)
                nc.scalar.activation(root, norm, ACT.Sqrt).then_inc(rooted, 1)
                on_scalar(act)
                act.wait_ge(norm_of, 1)
                nc.scalar.activation(root, norm, ACT.Sqrt).then_inc(normed, 1)
                layernorm_root(core, act, ln_var, ln_root, core.stat, D)

            @block.vector
            def _(dve):
                chain = Chain(dve, step)
                dve.sem_inc(sums_stored, 2)
                dve.wait_ge(degrees, BLOCKS)
                degree = core.bank(7)[:, 0:BLOCKS]
                chain(nc.vector.tensor_scalar(has_edges, degree, 0.0, None, ALU.is_gt))
                nc.vector.tensor_scalar(norm, degree, 1.0, None, ALU.max).then_inc(root_of, 1)
                dve.wait_ge(rooted, 1)
                chain(nc.vector.reciprocal(norm, root))
                chain(nc.vector.tensor_tensor(norm, norm, has_edges, ALU.mult))
                value = stack[:, :, 0:D]
                per_node = norm.unsqueeze(2).to_broadcast([P, BLOCKS, D])
                chain(nc.vector.tensor_tensor(value, core.x[:, :, :], per_node, ALU.mult))
                split_parts(nc, chain, value, parts)
                nc.vector.memset(has_edges, 0.0).then_inc(parts_ready, 1)

                def store(j, slot, turn):
                    dve.wait_ge(sums_ready, turn)
                    nc.vector.tensor_reduce(stack[:, bass.ds(j, 1), 0:D],
                                            sums[slot].rearrange("p (k f) -> p f k", k=3),
                                            AX.X, ALU.add).then_inc(sums_stored, 1)

                with dve.Fori(0, BLOCKS // 2) as pair:
                    for slot in range(2):
                        store(pair * 2 + slot, slot, pair * 2 + (slot + 1))
                store(BLOCKS - 1, 0, BLOCKS)
                dve.wait_ge(sums_stored, BLOCKS + 2)
                chain(nc.vector.tensor_tensor(value, value, per_node, ALU.mult))
                nc.vector.tensor_tensor(stack[:, :, D:2 * D], value, core.x[:, :, :], ALU.mult).then_inc(stack_ready, 1)
                dve.wait_ge(loaded, 64)
                dve.wait_ge(products, 1)
                chain(nc.vector.tensor_tensor(stack[:, :, :], core.psum[:, 0:PADDED].rearrange("p (b f) -> p b f", f=P),
                                              bias[:, :, :].to_broadcast([P, BLOCKS, 2 * D]), ALU.add))
                chain(nc.vector.scalar_tensor_tensor(stack[:, :, :], stack[:, :, :], 0.2, stack[:, :, :],
                                                     ALU.mult, ALU.max))
                u, square = stack[:, :, 0:D], stack[:, :, D:2 * D]
                chain(nc.vector.tensor_tensor(u, u, square, ALU.add))
                chain(nc.vector.tensor_tensor(square, u, u, ALU.mult))
                chain(nc.vector.tensor_reduce(norm, square, AX.X, ALU.add))
                nc.vector.tensor_scalar(norm, norm, 1e-12, None, ALU.max).then_inc(norm_of, 1)
                dve.wait_ge(normed, 1)
                chain(nc.vector.reciprocal(norm, root))
                chain(nc.vector.tensor_tensor(u, u, per_node, ALU.mult))
                chain(nc.vector.tensor_tensor(core.x[:, :, :], core.x[:, :, :], u, ALU.add))
                layernorm(core, chain, ln_root, ln_var, core.x[:, :, :], u, core.stat)


HALF = 5
ROUNDS = ITEMS // (2 * HALF)
assert ROUNDS * 2 * HALF == ITEMS


def gather_rows(core, pool, table, index, staged, rows, free, staged_ready, started, gathered):
    nc = core.nc
    with pool.Fori(0, ROUNDS) as r:
        for k in range(2):
            pool.wait_ge(free[k], r + 1)
            nc.gpsimd.tensor_copy(staged[:, k, :], index[:, bass.ds(r * (2 * HALF) + k * HALF, HALF)])\
              .then_inc(staged_ready, 1)
            pool.wait_ge(staged_ready, r * 2 + (k + 1))
            pool.sem_inc(started, 1)
            for u in range(HALF):
                nc.gpsimd.indirect_dma_start(
                    out=rows[:, k, u, :], out_offset=None, in_=table,
                    in_offset=bass.IndirectOffsetOnAxis(ap=staged[:, k, u:u + 1], axis=0)).then_inc(gathered[k], 16)


def destination_hots(core, hots, k, r):
    at = r * (2 * HALF) + k * HALF
    return core.nc.vector.tensor_tensor(
        hots[:, k, :, :], core.iota[:, :].unsqueeze(1).to_broadcast([P, HALF, P]),
        core.dloc[:, bass.ds(at, HALF)].unsqueeze(2).to_broadcast([P, HALF, P]), ALU.is_equal)


def relation_layer(core):
    nc, ins = core.nc, core.ins
    with ExitStack() as stage:
        sem = lambda n: core.sem(n, stage)
        weights, x_t, made, rows, hots, staged = core.tail_views(
            ([P, RELATIONS, D], F32), ([P, PADDED], F32), ([P, 2, RELATIONS * D], F32),
            ([P, 2, HALF, D], F32), ([P, 2, HALF, P], F32), ([P, 2, HALF], I32))
        mask0 = core.sb("r_mask0", [P, PADDED], U8, stage)
        zeros = core.tail_views(([P, RELATIONS, D], F32), ([P, BANK], F32))[1]
        table = nc.dram_tensor("relation_table", [PADDED * RELATIONS, D], F32).ap()
        table_rows = table.rearrange("(n r) f -> n (r f)", r=RELATIONS)
        masked, loaded, step = sem("r_masked"), sem("r_loaded"), sem("r_step")
        banks_ready, copied = sem("r_banks"), sem("r_copied")
        multiplied, evacuated = sem("r_multiplied"), [sem("r_evac0"), sem("r_evac1")]
        written = [sem("r_written0"), sem("r_written1")]
        free, gathered = [sem("r_free0"), sem("r_free1")], [sem("r_gath0"), sem("r_gath1")]
        started = sem("r_started")
        staged_ready, hots_ready, zeros_ready = sem("r_staged"), sem("r_hots"), sem("r_zeros")
        summed, ln_var, ln_root = sem("r_summed"), sem("r_lnvar"), sem("r_lnroot")
        on_tensor, on_scalar = transposed_nodes(core, banks_ready, core.x, D, x_t, copied)
        sums = core.psum[:, 0:BLOCKS * D]
        with nc.Block() as block:
            @block.sync
            def _(sp):
                sp.wait_ge(masked, BLOCKS)
                sp.dma_start(weights[0:D, :, :], ins["w_rel"].rearrange("r i o -> i r o")).then_inc(loaded, 16)
                for b in range(BLOCKS):
                    sp.wait_ge(evacuated[b % 2], b // 2 + 1)
                    sp.dma_start(table_rows[b * P:(b + 1) * P, :], made[:, b % 2, :]).then_inc(written[b % 2], 16)

            @block.gpsimd
            def _(pool):
                pool.wait_ge(masked, BLOCKS)
                pool.wait_ge(written[0], 16 * (BLOCKS - BLOCKS // 2))
                pool.wait_ge(written[1], 16 * (BLOCKS // 2))
                gather_rows(core, pool, table, core.words, staged, rows, free, staged_ready, started, gathered)

            @block.vector
            def _(dve):
                for b in range(BLOCKS):
                    nc.vector.tensor_scalar(core.mask[:, b, :] if b else mask0[:, :], core.counts[:, b, :], 0.0, None,
                                            ALU.is_gt).then_inc(masked, 1)
                    dve.wait_ge(masked, b + 1)
                nc.vector.tensor_copy(core.mask[:, 0, :], mask0[:, :])
                for b in range(1, BLOCKS, 2):
                    dve.wait_ge(multiplied, b + 1)
                    if b > 2:
                        dve.wait_ge(written[1], 16 * (b // 2))
                    nc.vector.tensor_copy(made[:, 1, :], core.bank(2 * (b % 4), 2)).then_inc(evacuated[1], 1)
                dve.wait_ge(written[0], 16 * (BLOCKS - BLOCKS // 2))
                dve.wait_ge(copied, len(CHUNKS))
                dve.wait_ge(multiplied, BLOCKS)
                nc.vector.memset(zeros, 0.0).then_inc(zeros_ready, 1)
                with dve.Fori(0, ROUNDS) as r:
                    for k in range(2):
                        dve.wait_ge(free[k], r + 1)
                        destination_hots(core, hots, k, r).then_inc(hots_ready, 1)
                chain = Chain(dve, step)
                dve.wait_ge(summed, 1)
                chain(nc.vector.tensor_tensor(core.x[:, :, :], core.x[:, :, :],
                                              sums.rearrange("p (b f) -> p b f", f=D), ALU.add))
                chain(nc.vector.tensor_scalar(core.words[:, :], core.words[:, :], 4, None, ALU.logical_shift_right))
                work = x_t[:, 0:BLOCKS * D].rearrange("p (b f) -> p b f", f=D)
                layernorm(core, chain, ln_root, ln_var, core.x[:, :, :], work, core.stat)

            @block.scalar
            def _(act):
                act.wait_ge(masked, BLOCKS)
                on_scalar(act)
                for b in range(0, BLOCKS, 2):
                    act.wait_ge(multiplied, b + 1)
                    if b > 1:
                        act.wait_ge(written[0], 16 * (b // 2))
                    nc.scalar.activation(made[:, 0, :], core.bank(2 * (b % 4), 2), ACT.Copy)\
                      .then_inc(evacuated[0], 1)
                layernorm_root(core, act, ln_var, ln_root, core.stat, D)

            @block.tensor
            def _(pe):
                pe.sem_inc(free[0], 1)
                pe.sem_inc(free[1], 1)
                on_tensor(pe)
                pe.wait_ge(copied, len(CHUNKS))
                pe.wait_ge(loaded, 16)
                flat = weights[0:D, :, :].rearrange("p r f -> p (r f)")
                for b in range(BLOCKS):
                    if b >= 4:
                        pe.wait_ge(evacuated[b % 2], (b - 4) // 2 + 1)
                    for n in range(2):
                        last = nc.tensor.matmul(core.bank(2 * (b % 4) + n), x_t[0:D, b * P:(b + 1) * P],
                                                flat[:, n * BANK:(n + 1) * BANK], start=True, stop=True)
                    last.then_inc(multiplied, 1)
                pe.wait_ge(evacuated[0], BLOCKS - BLOCKS // 2)
                pe.wait_ge(evacuated[1], BLOCKS // 2)
                pe.wait_ge(zeros_ready, 1)
                for n in range(4):
                    nc.tensor.matmul(core.bank(n), zeros[:, 0:P], zeros, start=True, stop=True,
                                     skip_group_check=True)
                with pe.Fori(0, ROUNDS) as r:
                    for k in range(2):
                        pe.wait_ge(hots_ready, r * 2 + (k + 1))
                        pe.wait_ge(gathered[k], r * (16 * HALF) + 16 * HALF)
                        for u in range(HALF):
                            b = pe.value_load(core.block_of[0:1, bass.ds(r * (2 * HALF) + (k * HALF + u), 1)],
                                              min_val=0, max_val=BLOCKS - 1)
                            last = nc.tensor.matmul(core.psum[:, bass.ds(b * D, D)], hots[:, k, u, :],
                                                    rows[:, k, u, :], start=False, stop=True, skip_group_check=True)
                        last.then_inc(free[k], 1)
                pe.wait_ge(free[1], ROUNDS + 1)
                pe.sem_inc(summed, 1)


ROW = HD + HEADS
WIDE = HD + 2 * HEADS


def attention_layer(core, acc, layer):
    nc, ins = core.nc, core.ins
    depth = D if layer == 0 else HD
    halves = -(-depth // P)
    rows_used = min(depth, P)
    with ExitStack() as stage:
        sb = lambda *a: core.sb(*a, stage)
        sem = lambda n: core.sem(f"a{layer}_{n}", stage)
        weights, vectors, product, repeated, turned = core.tail_views(
            ([P, 2, WIDE], F32), ([P, 2, HD], F32), ([P, HD], F32), ([P, 2, HEADS, P], F32), ([P, 2, PADDED], F32))
        before = ([P, 2, WIDE], F32), ([P, 2, HD], F32), ([P, HD], F32), ([P, 2, HEADS, P], F32), ([P, 2, PADDED], F32)
        level, masked_out = core.tail_views(*before, ([P, 2, PADDED], F32), ([P, PADDED], BF16))[-2:]
        rows, hots, hots_t = core.tail_views(*before, ([P, 2, HALF, ROW], F32), ([P, 2, HALF, P], F32),
                                             ([P, 2, HALF, P], F32))[-3:]
        logits = sb(f"a{layer}_logits", [P, 2, HALF, HEADS], F32)
        staged = sb(f"a{layer}_staged", [P, 2, HALF], I32)
        at_dst = sb(f"a{layer}_at_dst", [P, BLOCKS, 2 * HEADS], F32)
        own = sb(f"a{layer}_own", [P, BLOCKS, HEADS], F32)
        best = sb(f"a{layer}_best", [P, BLOCKS, HEADS], F32)
        least = sb(f"a{layer}_least", [P, HEADS], F32)
        table = nc.dram_tensor(f"attention_table{layer}", [PADDED, ROW], F32).ap()
        loaded, step = sem("loaded"), sem("step")
        weights_ready, projected, evacuated, written = (sem(n) for n in ("weights", "projected", "evac", "written"))
        levels_in_psum, levels_ready, level_used = sem("lpsum"), sem("levels"), sem("lused")
        node_logits, self_ready = sem("nlogits"), sem("self")
        self_of, pass_ready = sem("self_of"), sem("pass_ready")
        free, gathered = [sem("free0"), sem("free1")], [sem("gath0"), sem("gath1")]
        staged_ready, started, hots_ready = sem("staged_s"), sem("started"), sem("hots_s")
        turned_in_psum, turned_ready, fetched = sem("tpsum"), sem("turned"), sem("fetched")
        logits_ready, exps_ready, messages_ready = sem("logits_s"), sem("exps"), sem("messages")
        added_up, stored, logit_steps = sem("added"), sem("stored"), sem("lsteps")
        half_psum = [core.psum[:, 0:BANK], core.psum[:, BANK:BANK + P]]
        hots_psum = core.psum[:, 0:HALF * P].rearrange("p (u e) -> p u e", u=HALF)
        fetch_psum = [core.psum[:, 2 * BANK + k * 64:2 * BANK + k * 64 + HALF * 2 * HEADS]
                      .rearrange("p (u h) -> p u h", u=HALF) for k in (0, 1)]
        with nc.Block() as block:
            @block.sync
            def _(sp):
                w = ins[f"w_gat{layer}"]
                for n in range(halves):
                    sp.dma_start(weights[0:rows_used, n, 0:HD], w[n * P:n * P + rows_used, :]).then_inc(loaded, 16)
                for n, name in enumerate(("att_src", "att_dst")):
                    sp.dma_start(vectors[:, n, :], ins[f"{name}{layer}"].to_broadcast([P, HD])).then_inc(loaded, 16)
                sp.wait_ge(evacuated, BLOCKS)
                sp.dma_start(table.rearrange("(b p) c -> p b c", p=P), acc[:, :, 0:ROW]).then_inc(written, 16)

            @block.gpsimd
            def _(pool):
                pool.wait_ge(written, 16)
                pool.wait_ge(pass_ready, 1)
                gather_rows(core, pool, table, core.words, staged, rows, free, staged_ready, started, gathered)

            @block.tensor
            def _(pe):
                pe.wait_ge(weights_ready, 1)
                for b in range(BLOCKS):
                    if b >= 8:
                        pe.wait_ge(evacuated, b - 7)
                    for n in range(halves):
                        last = nc.tensor.matmul(core.bank(b % 8)[:, 0:WIDE],
                                                turned[0:rows_used, n, b * P:(b + 1) * P], weights[0:rows_used, n, :],
                                                start=(n == 0), stop=(n == halves - 1))
                    last.then_inc(projected, 1)
                pe.wait_ge(evacuated, BLOCKS)
                for h in range(HEADS):
                    for c, (lo, hi) in enumerate(CHUNKS):
                        if h:
                            pe.wait_ge(levels_ready, (h - 1) * len(CHUNKS) + c + 1)
                        for n in range(halves):
                            last = nc.tensor.matmul(core.psum[:, lo:hi], repeated[0:rows_used, n, h, :],
                                                    turned[0:rows_used, n, lo:hi],
                                                    start=(n == 0), stop=(n == halves - 1))
                        last.then_inc(levels_in_psum, 1)
                pe.wait_ge(levels_ready, HEADS * len(CHUNKS))
                pe.sem_inc(free[0], 1)
                pe.sem_inc(free[1], 1)
                pe.wait_ge(pass_ready, 1)

                def registers(r, k):
                    return [pe.value_load(core.block_of[0:1, bass.ds(r * (2 * HALF) + (k * HALF + u), 1)],
                                          min_val=0, max_val=BLOCKS - 1) for u in range(HALF)]

                with pe.Fori(0, ROUNDS) as r:
                    for k in range(2):
                        turn = r * 2 + (k + 1)
                        pe.wait_ge(turned_ready, turn)
                        pe.wait_ge(hots_ready, turn)
                        for u in range(HALF):
                            last = nc.tensor.transpose(hots_psum[:, u, :], hots[:, k, u, :], core.ident[:, :])
                        last.then_inc(turned_in_psum, 1)
                        pe.wait_ge(turned_ready, turn + 1)
                        for u, b in enumerate(registers(r, k)):
                            last = nc.tensor.matmul(fetch_psum[k][:, u, :], hots_t[:, k, u, :],
                                                    at_dst[:, bass.ds(b, 1), :], start=True, stop=True)
                        last.then_inc(fetched, 1)
                        pe.wait_ge(messages_ready, turn)
                        for u in range(HALF):
                            pe.wait_ge(stored, r * (2 * HALF) + (k * HALF + u + 1))
                            last = nc.tensor.matmul(core.bank(3 + u)[:, 0:ROW], hots[:, k, u, :], rows[:, k, u, :],
                                                    start=True, stop=True)
                            if u < HALF - 1:
                                last.then_inc(added_up, 1)
                        last.then_inc(free[k], 1)

            @block.scalar
            def _(act):
                for b in range(BLOCKS):
                    act.wait_ge(projected, b + 1)
                    nc.scalar.activation(acc[:, b, :], core.bank(b % 8)[:, 0:WIDE], ACT.Copy).then_inc(evacuated, 1)
                for h in range(HEADS):
                    if h >= 2:
                        act.wait_ge(level_used, h - 1)
                    for c, (lo, hi) in enumerate(CHUNKS):
                        act.wait_ge(levels_in_psum, h * len(CHUNKS) + c + 1)
                        nc.scalar.activation(level[:, h % 2, lo:hi], core.psum[:, lo:hi], ACT.Copy)\
                          .then_inc(levels_ready, 1)
                act.wait_ge(node_logits, 1)
                nc.scalar.activation(own[:, :, :], own[:, :, :], ACT.Exp).then_inc(self_ready, 1)
                act.wait_ge(pass_ready, 1)
                act.sem_inc(turned_ready, 1)
                with act.Fori(0, ROUNDS) as r:
                    for k in range(2):
                        turn = r * 2 + (k + 1)
                        act.wait_ge(turned_in_psum, turn)
                        nc.scalar.activation(hots_t[:, k, :, :], hots_psum, ACT.Copy).then_inc(turned_ready, 1)
                        act.wait_ge(logits_ready, turn)
                        nc.scalar.activation(rows[:, k, :, HD:ROW], logits[:, k, :, :], ACT.Exp).then_inc(exps_ready, 1)

            @block.vector
            def _(dve):
                chain = Chain(dve, step)
                dve.wait_ge(loaded, 16 * (halves + 2))
                for n in range(halves):
                    for which in range(2):
                        chain(nc.vector.tensor_tensor(product[0:rows_used, :], weights[0:rows_used, n, 0:HD],
                                                      vectors[0:rows_used, which, :], ALU.mult))
                        at = HD + which * HEADS
                        chain(nc.vector.tensor_reduce(weights[0:rows_used, n, at:at + HEADS],
                                                      product[0:rows_used, :].rearrange("p (h c) -> p h c", h=HEADS),
                                                      AX.X, ALU.add))
                    chain(nc.vector.tensor_copy(repeated[0:rows_used, n, :, :],
                                                weights[0:rows_used, n, HD:HD + HEADS].unsqueeze(2)
                                                .to_broadcast([rows_used, HEADS, P])))
                dve.sem_inc(weights_ready, 1)
                for h in range(HEADS):
                    dve.wait_ge(levels_ready, (h + 1) * len(CHUNKS))
                    chain(nc.vector.tensor_reduce(least[:, h:h + 1], level[:, h % 2, :], AX.X, ALU.min))
                    chain(nc.vector.tensor_scalar(level[:, h % 2, :], level[:, h % 2, :], least[:, h:h + 1], None,
                                                  ALU.subtract))
                    for b in range(BLOCKS):
                        chain(nc.vector.tensor_tensor_reduce(
                            out=masked_out, in0=core.mask[:, b, :], in1=level[:, h % 2, :], scale=1.0, scalar=0.0,
                            op0=ALU.mult, op1=ALU.max, accum_out=best[:, b, h:h + 1]))
                    dve.sem_inc(level_used, 1)
                a_src, a_dst = acc[:, :, HD:ROW], acc[:, :, ROW:WIDE]
                highest = at_dst[:, :, HEADS:2 * HEADS]
                chain(nc.vector.tensor_tensor(best[:, :, :], best[:, :, :],
                                              least[:, :].unsqueeze(1).to_broadcast([P, BLOCKS, HEADS]), ALU.add))
                chain(nc.vector.tensor_tensor(best[:, :, :], best[:, :, :], a_src, ALU.max))
                chain(nc.vector.tensor_tensor(best[:, :, :], best[:, :, :], a_dst, ALU.add))
                chain(nc.vector.scalar_tensor_tensor(highest, best[:, :, :], 0.2, best[:, :, :], ALU.mult, ALU.max))
                chain(nc.vector.tensor_copy(at_dst[:, :, 0:HEADS], a_dst))
                chain(nc.vector.tensor_tensor(own[:, :, :], a_src, a_dst, ALU.add))
                chain(nc.vector.scalar_tensor_tensor(own[:, :, :], own[:, :, :], 0.2, own[:, :, :],
                                                     ALU.mult, ALU.max))
                nc.vector.tensor_tensor(own[:, :, :], own[:, :, :], highest, ALU.subtract).then_inc(node_logits, 1)
                dve.wait_ge(self_ready, 1)
                dve.wait_ge(written, 16)
                by_head = acc[:, :, 0:HD].rearrange("p b (h c) -> p b h c", h=HEADS)
                chain(nc.vector.tensor_tensor(by_head, by_head,
                                              own[:, :, :].unsqueeze(3).to_broadcast([P, BLOCKS, HEADS, D]), ALU.mult))
                chain(nc.vector.tensor_copy(a_src, own[:, :, :]))
                dve.sem_inc(pass_ready, 1)
                dve.sem_inc(stored, HALF)

                def store(r, k, first):
                    for u in range(HALF):
                        b = dve.value_load(core.block_of[0:1, bass.ds(first + u, 1)],
                                           min_val=0, max_val=BLOCKS - 1)
                        if u < HALF - 1:
                            dve.wait_ge(added_up, r * (2 * (HALF - 1)) + (k * (HALF - 1) + u + 1))
                        else:
                            dve.wait_ge(free[k], r + 2)
                        nc.vector.tensor_tensor(acc[:, bass.ds(b, 1), 0:ROW], acc[:, bass.ds(b, 1), 0:ROW],
                                                core.bank(3 + u)[:, 0:ROW].unsqueeze(1), ALU.add).then_inc(stored, 1)
                        dve.wait_ge(stored, first + (HALF + u + 1))

                with dve.Fori(0, ROUNDS) as r:
                    for k in range(2):
                        turn = r * 2 + (k + 1)
                        dve.wait_ge(free[k], r + 1)
                        destination_hots(core, hots, k, r).then_inc(hots_ready, 1)
                        dve.wait_ge(fetched, turn)
                        dve.wait_ge(gathered[k], r * (16 * HALF) + 16 * HALF)
                        e = logits[:, k, :, :]
                        base = r * 6 + k * 3
                        nc.vector.tensor_tensor(e, rows[:, k, :, HD:ROW], fetch_psum[k][:, :, 0:HEADS],
                                                ALU.add).then_inc(logit_steps, 1)
                        dve.wait_ge(logit_steps, base + 1)
                        nc.vector.scalar_tensor_tensor(e, e, 0.2, e, ALU.mult, ALU.max).then_inc(logit_steps, 1)
                        dve.wait_ge(logit_steps, base + 2)
                        nc.vector.tensor_tensor(e, e, fetch_psum[k][:, :, HEADS:2 * HEADS],
                                                ALU.subtract).then_inc(logit_steps, 1)
                        dve.wait_ge(logit_steps, base + 3)
                        nc.vector.tensor_scalar(e, e, 0.0, None, ALU.min).then_inc(logits_ready, 1)
                        dve.wait_ge(exps_ready, turn)
                        message = rows[:, k, :, 0:HD].rearrange("p u (h c) -> p u h c", h=HEADS)
                        nc.vector.tensor_tensor(message, message,
                                                rows[:, k, :, HD:ROW].unsqueeze(3).to_broadcast([P, HALF, HEADS, D]),
                                                ALU.mult).then_inc(messages_ready, 1)
                        store(r, k, r * (2 * HALF) + k * HALF)


def attention_layers(core):
    nc, ins = core.nc, core.ins
    before = ([P, 2, WIDE], F32), ([P, 2, HD], F32), ([P, HD], F32), ([P, 2, HEADS, P], F32)
    turned, across = core.tail_views(*before, ([P, 2, PADDED], F32), ([P, PADDED], F32))[-2:]
    acc = core.sb("acc", [P, BLOCKS, WIDE], F32)
    head_affine = core.sb("head_affine", [P, 3, HD], F32)
    with ExitStack() as stage:
        sem = lambda n: core.sem(n, stage)
        weights = core.sb("p_weights", [P, D], F32, stage)
        types, types_f = core.sb("type_of", [P, BLOCKS], I32, stage), core.sb("type_of_f", [P, BLOCKS], F32, stage)
        depth = D + NODE_TYPES + 1
        given, loaded, step = sem("j_given"), sem("j_loaded"), sem("j_step")
        banks_ready, copied, products, turned_out = sem("j_banks"), sem("j_copied"), sem("j_products"), sem("j_out")
        on_tensor, on_scalar = transposed_nodes(core, banks_ready, acc[:, :, 0:depth], depth, across, copied)
        with nc.Block() as block:
            @block.sync
            def _(sp):
                sp.dma_start(types[:, :], ins["types"]).then_inc(loaded, 16)
                sp.dma_start(weights[0:D, :], ins["w_proj"]).then_inc(loaded, 16)
                sp.dma_start(weights[D:D + NODE_TYPES, :], ins["type_emb"]).then_inc(loaded, 16)
                sp.dma_start(weights[depth - 1:depth, :], ins["b_proj"]).then_inc(loaded, 16)
                for n, name in enumerate(("bias0", "gain0", "shift0")):
                    sp.dma_start(head_affine[:, n, :], ins[name].to_broadcast([P, HD])).then_inc(loaded, 16)
                sp.wait_ge(loaded, 16 * 7)

            @block.vector
            def _(dve):
                chain = Chain(dve, step)
                chain(nc.vector.tensor_copy(acc[:, :, 0:D], core.x[:, :, :]))
                dve.wait_ge(loaded, 16 * 7)
                chain(nc.vector.tensor_copy(types_f[:, :], types[:, :]))
                for t in range(NODE_TYPES):
                    chain(nc.vector.tensor_scalar(acc[:, :, D + t:D + t + 1], types_f[:, :].unsqueeze(2), float(t),
                                                  None, ALU.is_equal))
                nc.vector.memset(acc[:, :, depth - 1:depth], 1.0).then_inc(given, 1)

            @block.tensor
            def _(pe):
                pe.wait_ge(given, 1)
                on_tensor(pe)
                pe.wait_ge(copied, len(CHUNKS))
                for lo, hi in CHUNKS:
                    nc.tensor.matmul(core.psum[0:D, lo:hi], weights[0:depth, :], across[0:depth, lo:hi],
                                     start=True, stop=True).then_inc(products, 1)

            @block.scalar
            def _(act):
                on_scalar(act)
                for n, (lo, hi) in enumerate(CHUNKS):
                    act.wait_ge(products, n + 1)
                    nc.scalar.activation(turned[0:D, 0, lo:hi], core.psum[0:D, lo:hi], ACT.Copy)\
                      .then_inc(turned_out, 1)
    attention_layer(core, acc, 0)

    with ExitStack() as stage:
        sem = lambda n: core.sem(n, stage)
        share = core.sb("m_share", [P, BLOCKS, HEADS], F32, stage)
        work = core.tail_views(([P, BLOCKS, HD], F32))[0]
        step, ln_var, ln_root, normed, relued = (sem(f"m_{n}") for n in ("step", "var", "root", "normed", "relued"))
        banks_ready, copied = sem("m_banks"), sem("m_copied")
        hidden = acc[:, :, 0:HD]
        by_head = hidden.rearrange("p b (h c) -> p b h c", h=HEADS)
        with nc.Block() as block:
            @block.vector
            def _(dve):
                chain = Chain(dve, step)
                chain(nc.vector.tensor_scalar(share[:, :, :], acc[:, :, HD:ROW], 1e-16, None, ALU.add))
                chain(nc.vector.reciprocal(share[:, :, :], share[:, :, :]))
                chain(nc.vector.tensor_tensor(by_head, by_head,
                                              share[:, :, :].unsqueeze(3).to_broadcast([P, BLOCKS, HEADS, D]), ALU.mult))
                rows = lambda n: head_affine[:, n:n + 1, :].to_broadcast([P, BLOCKS, HD])
                chain(nc.vector.tensor_tensor(hidden, hidden, rows(0), ALU.add))
                layernorm(core, chain, ln_root, ln_var, hidden, work, core.stat)
                chain(nc.vector.tensor_tensor(hidden, hidden, rows(1), ALU.mult))
                nc.vector.tensor_tensor(hidden, hidden, rows(2), ALU.add).then_inc(normed, 1)

            @block.scalar
            def _(act):
                layernorm_root(core, act, ln_var, ln_root, core.stat, HD)
                act.wait_ge(normed, 1)
                nc.scalar.activation(hidden, hidden, ACT.Relu).then_inc(relued, 1)
                for half in range(2):
                    for n, (lo, hi) in enumerate(CHUNKS):
                        act.wait_ge(banks_ready, half * len(CHUNKS) + n + 1)
                        nc.scalar.activation(turned[:, half, lo:hi], core.psum[:, lo:hi], ACT.Copy).then_inc(copied, 1)

            @block.tensor
            def _(pe):
                pe.wait_ge(relued, 1)
                for half in range(2):
                    for b in range(BLOCKS):
                        if half and b % 4 == 0:
                            pe.wait_ge(copied, b // 4 + 1)
                        last = nc.tensor.transpose(core.psum[:, b * P:(b + 1) * P],
                                                   acc[:, b, half * P:(half + 1) * P], core.ident[:, :])
                        if b % 4 == 3 or b == BLOCKS - 1:
                            last.then_inc(banks_ready, 1)
    attention_layer(core, acc, 1)

    with ExitStack() as stage:
        sem = lambda n: core.sem(n, stage)
        share = core.sb("f_share", [P, BLOCKS, HEADS], F32, stage)
        affine = core.sb("f_affine", [P, 3, D], F32, stage)
        work = core.tail_views(([P, BLOCKS, D], F32))[0]
        mean = acc[:, :, 0:D]
        loaded, step, done, stored = (sem(f"f_{n}") for n in ("loaded", "step", "done", "stored"))
        turns = [(sem(f"f_var{n}"), sem(f"f_root{n}")) for n in range(2)]
        hidden = acc[:, :, 0:HD]
        by_head = hidden.rearrange("p b (h c) -> p b h c", h=HEADS)
        with nc.Block() as block:
            @block.sync
            def _(sp):
                for n, name in enumerate(("bias1", "gain1", "shift1")):
                    sp.dma_start(affine[:, n, :], ins[name].to_broadcast([P, D])).then_inc(loaded, 16)
                sp.wait_ge(done, 1)
                sp.dma_start(core.out, core.x[:, :, :]).then_inc(stored, 16)
                sp.wait_ge(stored, 16)

            @block.vector
            def _(dve):
                chain = Chain(dve, step)
                chain(nc.vector.tensor_scalar(share[:, :, :], acc[:, :, HD:ROW], 1e-16, None, ALU.add))
                chain(nc.vector.reciprocal(share[:, :, :], share[:, :, :]))
                chain(nc.vector.tensor_tensor(by_head, by_head,
                                              share[:, :, :].unsqueeze(3).to_broadcast([P, BLOCKS, HEADS, D]), ALU.mult))
                for h in range(1, HEADS):
                    chain(nc.vector.tensor_tensor(mean, mean, acc[:, :, h * D:(h + 1) * D], ALU.add))
                rows = lambda n: affine[:, n:n + 1, :].to_broadcast([P, BLOCKS, D])
                dve.wait_ge(loaded, 48)
                chain(nc.vector.tensor_scalar(mean, mean, 1.0 / HEADS, None, ALU.mult))
                chain(nc.vector.tensor_tensor(mean, mean, rows(0), ALU.add))
                layernorm(core, chain, turns[0][1], turns[0][0], mean, work, core.stat)
                chain(nc.vector.tensor_tensor(mean, mean, rows(1), ALU.mult))
                chain(nc.vector.tensor_tensor(mean, mean, rows(2), ALU.add))
                chain(nc.vector.scalar_tensor_tensor(core.x[:, :, :], mean, 0.0, core.x[:, :, :], ALU.max, ALU.add))
                layernorm(core, chain, turns[1][1], turns[1][0], core.x[:, :, :], work, core.stat)
                dve.sem_inc(done, 1)

            @block.scalar
            def _(act):
                for variance, root in turns:
                    layernorm_root(core, act, variance, root, core.stat, D)


def build(nc, ins, out, debug=None):
    with ExitStack() as ctx:
        core = Core(nc, ctx, ins, out)
        prepare(core)
        count_edges(core)
        bilinear_layer(core)
        interaction_layer(core)
        relation_layer(core)
        attention_layers(core)
        if debug:
            debug(core)


_VECTORS = {"b_f": "L0_gnn_b1", "b_xf": "L0_gnn_b2", "b_gcn": "L1_gnn_b_gcn", "b_int": "L1_gnn_b_int",
            "b_proj": "L3_gnn_proj_b", "bias0": "L3_gnn_bias0", "gain0": "L3_gnn_ln0_g", "shift0": "L3_gnn_ln0_b",
            "bias1": "L3_gnn_bias1", "gain1": "L3_gnn_ln1_g", "shift1": "L3_gnn_ln1_b",
            "att_src0": "L3_gnn_att_src0", "att_dst0": "L3_gnn_att_dst0",
            "att_src1": "L3_gnn_att_src1", "att_dst1": "L3_gnn_att_dst1"}
_MATRICES = {"w_f": "L0_gnn_W1", "w_xf": "L0_gnn_W2", "w_gcn": "L1_gnn_W_gcn", "w_int": "L1_gnn_W_int",
             "w_rel": "L2_gnn_weight", "w_proj": "L3_gnn_proj_W", "type_emb": "L3_gnn_type_emb",
             "w_gat0": "L3_gnn_W0", "w_gat1": "L3_gnn_W1"}


def laid_out(inputs):
    def edges(name, fill):
        a = np.asarray(inputs[name])
        a = np.concatenate([a, np.full(TILES * P - a.size, fill, a.dtype)])
        return np.ascontiguousarray(a.reshape(TILES, P).T)

    x = np.asarray(inputs["x"])
    x = np.concatenate([x, np.zeros((PADDED - NODES, D), x.dtype)]).reshape(BLOCKS, P, D)
    types = np.asarray(inputs["node_type_3"])
    types = np.concatenate([types, np.zeros(PADDED - NODES, types.dtype)]).reshape(BLOCKS, P).T
    arrays = {"src": edges("src", 0), "dst": edges("dst", NO_NODE), "rel": edges("edge_type_16", 0),
              "x": np.ascontiguousarray(x.transpose(1, 0, 2)), "types": np.ascontiguousarray(types)}
    arrays |= {n: np.asarray(inputs[k]).reshape(1, -1) for n, k in _VECTORS.items()}
    arrays |= {n: np.asarray(inputs[k]) for n, k in _MATRICES.items()}
    return arrays


def kernel(**inputs):
    import concourse.bacc as bacc
    from concourse.bass_utils import run_bass_kernel_spmd

    nc = bacc.Bacc("TRN2", target_bir_lowering=False, num_devices=1)
    arrays = laid_out(inputs)
    ins = {name: nc.dram_tensor(f"in_{name}", a.shape, mybir.dt.from_np(a.dtype), kind="ExternalInput").ap()
           for name, a in arrays.items()}
    out = nc.dram_tensor("out_nodes", [P, BLOCKS, D], F32, kind="ExternalOutput").ap()
    build(nc, ins, out)
    result = run_bass_kernel_spmd(nc, [{f"in_{name}": a for name, a in arrays.items()}], core_ids=[0])
    nodes = result.results[0]["out_nodes"]
    return np.ascontiguousarray(nodes.transpose(1, 0, 2)).reshape(PADDED, D)[:NODES]
```

```python
from contextlib import ExitStack

import numpy as np

import concourse.bass as bass
from concourse import mybir

F32, BF16, I32, I16, U8 = (mybir.dt.float32, mybir.dt.bfloat16, mybir.dt.int32,
                           mybir.dt.int16, mybir.dt.uint8)
ALU = mybir.AluOpType
ACT = mybir.ActivationFunctionType
AX = mybir.AxisListType

P = 128
NODES, EDGES, D = 3125, 103125, 64
RELATIONS, HEADS, NODE_TYPES = 16, 4, 3
HD = HEADS * D
BLOCKS = -(-NODES // P)
PADDED = BLOCKS * P
TILES = -(-EDGES // P)
GROUP, RING = 4, 4
PAIRS = (TILES + BLOCKS - 1 + BLOCKS) // 2
FULL_ITEMS = 2 * PAIRS
ROUNDS = -(-FULL_ITEMS // (GROUP * RING))
ITEMS = ROUNDS * GROUP * RING
GROUPS = ITEMS // GROUP
NO_NODE = 4095
BANK = 512
LN_EPS = 1e-5
CHUNKS = [(c, min(c + BANK, PADDED)) for c in range(0, PADDED, BANK)]


class Chain:

    def __init__(self, engine, semaphore):
        self.engine, self.semaphore, self.count = engine, semaphore, 0

    def __call__(self, instruction):
        instruction.then_inc(self.semaphore, 1)
        self.count += 1
        self.engine.wait_ge(self.semaphore, self.count)


class Core:

    def __init__(self, nc, ctx, ins, out):
        self.nc, self.ctx, self.ins, self.out = nc, ctx, ins, out
        sb = self.sb
        self.counts = sb("counts", [P, BLOCKS, PADDED], BF16)
        self.mask = self.counts[:, 0:BLOCKS // 2 + 1, :].rearrange("p b s -> p (b s)")\
            [:, 0:BLOCKS * PADDED // 2].bitcast(U8).rearrange("p (b s) -> p b s", b=BLOCKS)
        self.words = sb("item_words", [P, ITEMS], I32)
        self.dloc = sb("item_dst", [P, ITEMS], F32)
        self.block_of = sb("block_of", [1, ITEMS], I32)
        self.bounds = sb("pair_bounds", [1, 32], I32)
        self.x = sb("x_nodes", [P, BLOCKS, D], F32)
        self.ident = sb("ident", [P, P], F32)
        self.ident16 = sb("ident16", [P, P], BF16)
        self.ones = sb("ones", [P, P], F32)
        self.ones16 = sb("ones16", [P, 1], BF16)
        self.iota = sb("iota128", [P, P], F32)
        self.eps = sb("eps", [P, 1], F32)
        self.deg = sb("deg", [P, BLOCKS, len(CHUNKS)], F32)
        self.stat = sb("stat", [P, 4, BLOCKS], F32)
        self.psum = ctx.enter_context(nc.psum_tensor("psum", [P, 8 * BANK], F32))

    def sb(self, name, shape, dtype, ctx=None):
        return (ctx or self.ctx).enter_context(self.nc.sbuf_tensor(name, shape, dtype))

    def tail_views(self, *wanted):
        flat = self.counts[:, :, :].rearrange("p b s -> p (b s)")
        at, views = BLOCKS * PADDED // 2, []
        for shape, dtype in wanted:
            size = int(np.prod(shape[1:]))
            cols = size * {F32: 4, I32: 4, BF16: 2}[dtype] // 2
            view = flat[:, at:at + cols].bitcast(dtype) if dtype is not BF16 else flat[:, at:at + cols]
            at += cols
            letters = "abc"[:len(shape) - 1]
            if len(letters) > 1:
                view = view.rearrange(f"p ({' '.join(letters)}) -> p {' '.join(letters)}",
                                      **dict(zip(letters[:-1], shape[1:-1])))
            views.append(view)
        assert at <= BLOCKS * PADDED
        return views

    def sem(self, name, ctx=None):
        return (ctx or self.ctx).enter_context(self.nc.semaphore(name))

    def bank(self, n, count=1):
        return self.psum[:, n * BANK:(n + count) * BANK]


def prepare(core):
    nc, ins = core.nc, core.ins
    with ExitStack() as stage:
        sb = lambda *a: core.sb(*a, stage)
        sem = lambda n: core.sem(n, stage)
        raw_src, raw_rel = (sb(n, [P, TILES], I32) for n in ("raw_src", "raw_rel"))
        raw_dst = sb("raw_dst", [P, 2 * TILES], I32)
        dst_f = core.counts[:, 0, 0:2 * TILES].bitcast(F32)
        below = core.counts[:, 1, 0:TILES]
        item_w = core.counts[:, 2, 0:2 * ITEMS].bitcast(F32)
        item_i = core.counts[:, 3, 0:2 * ITEMS].bitcast(I32)
        reached = core.counts[:, 4, 0:2 * ITEMS].bitcast(F32)
        block_f = core.counts[:, 5, 0:2 * ITEMS].bitcast(F32)
        flat = core.counts[:, 6:9, :].rearrange("p b s -> p (b s)")
        item_words = flat[:, 0:2 * (ITEMS + TILES)].bitcast(I32)
        as_i16 = lambda ap: ap.bitcast(I16)
        starts = sb("starts", [P, BLOCKS - 1], F32)
        tile_row, even_row = sb("tile_row", [1, BLOCKS + 1], I32), sb("even_row", [1, BLOCKS], I32)
        ones_row, first_row = sb("ones_row", [1, BLOCKS], F32), sb("first_row", [1, BLOCKS + 1], F32)
        first_item = sb("first_item", [1, BLOCKS + 1], I32)
        first_col = sb("first_col", [P, 1], F32)
        loaded, constant, step = sem("p_loaded"), sem("p_constant"), sem("p_step")
        counted, summed = sem("p_counted"), sem("p_summed")
        firsts_ready, turned, reach_ready, blocks_ready = sem("p_firsts"), sem("p_turned"), sem("p_reach"), sem("p_blocks")
        placed = sem("p_placed")
        with nc.Block() as block:
            @block.sync
            def _(sp):
                sp.dma_start(raw_dst[:, 0:TILES], ins["dst"]).then_inc(loaded, 16)
                sp.dma_start(raw_src[:, :], ins["src"]).then_inc(loaded, 16)
                sp.dma_start(raw_rel[:, :], ins["rel"]).then_inc(loaded, 16)
                sp.dma_start(core.x[:, :, :], ins["x"]).then_inc(loaded, 16)
                sp.wait_ge(loaded, 64)

            @block.gpsimd
            def _(pool):
                chain = Chain(pool, constant)
                chain(pool.memset(core.ident[:, :], 0.0))
                chain(pool.affine_select(out=core.ident[:, :], in_=core.ident[:, :], compare_op=ALU.not_equal,
                                         fill=1.0, base=0, pattern=[[-1, P]], channel_multiplier=1))
                pool.tensor_copy(core.ident16[:, :], core.ident[:, :]).then_inc(constant, 1)
                pool.memset(core.ones[:, :], 1.0).then_inc(constant, 1)
                pool.memset(core.ones16[:, :], 1.0).then_inc(constant, 1)
                pool.memset(core.eps[:, :], LN_EPS).then_inc(constant, 1)
                pool.memset(ones_row[:, :], 1.0).then_inc(constant, 1)
                for tile, pattern in ((core.iota[:, :], [[1, P]]), (item_w, [[1, ITEMS]])):
                    pool.iota(tile, pattern, base=0, channel_multiplier=0,
                              allow_small_or_imprecise_dtypes=True).then_inc(constant, 1)
                pool.memset(raw_dst[:, TILES:], NO_NODE << 16).then_inc(constant, 1)
                pool.memset(item_words, NO_NODE << 16).then_inc(constant, 1)

            @block.vector
            def _(dve):
                chain = Chain(dve, step)
                dve.wait_ge(loaded, 64)
                dve.wait_ge(constant, 11)
                chain(nc.vector.tensor_copy(dst_f, raw_dst[:, 0:TILES]))
                for k in range(BLOCKS - 1):
                    chain(nc.vector.tensor_scalar(below, dst_f, float(P * (k + 1)), 0.0, ALU.is_lt, ALU.add,
                                                  accum_out=starts[:, k:k + 1]))
                nc.vector.memset(tile_row[:, 0:1], 0).then_inc(counted, 1)
                chain(nc.vector.scalar_tensor_tensor(raw_src[:, :], raw_src[:, :], float(RELATIONS), raw_rel[:, :],
                                                     ALU.mult, ALU.add))
                words = raw_dst[:, 0:TILES]
                chain(nc.vector.tensor_scalar(words, words, 16, None, ALU.logical_shift_left))
                chain(nc.vector.tensor_tensor(words, words, raw_src[:, :], ALU.bitwise_or))
                dve.wait_ge(summed, 1)
                chain(nc.vector.tensor_copy(tile_row[:, 1:BLOCKS], core.psum[0:1, 0:BLOCKS - 1]))
                chain(nc.vector.tensor_scalar(tile_row[:, 1:BLOCKS], tile_row[:, 1:BLOCKS], 7, None,
                                              ALU.arith_shift_right))
                chain(nc.vector.memset(tile_row[:, BLOCKS:BLOCKS + 1], TILES - 1))
                chain(nc.vector.scalar_tensor_tensor(even_row[:, :], tile_row[:, 1:BLOCKS + 1], 2.0,
                                                     tile_row[:, 0:BLOCKS], ALU.add, ALU.subtract))
                chain(nc.vector.tensor_scalar(even_row[:, :], even_row[:, :], -2, None, ALU.bitwise_and))
                chain(nc.vector.memset(first_row[:, 0:1], 0.0))
                chain(nc.vector.tensor_tensor_scan(first_row[:, 1:BLOCKS + 1], ones_row[:, :], even_row[:, :], 0.0,
                                                   ALU.mult, ALU.add))
                nc.vector.tensor_copy(first_item[:, :], first_row[:, :]).then_inc(firsts_ready, 1)
                dve.wait_ge(firsts_ready, 1)
                chain(nc.vector.tensor_scalar(core.bounds[:, 0:BLOCKS], first_item[:, 0:BLOCKS], 1, None,
                                              ALU.arith_shift_right))
                chain(nc.vector.memset(core.bounds[:, BLOCKS:BLOCKS + 1], PAIRS))
                with dve.Fori(0, BLOCKS) as b:
                    to = dve.value_load(first_item[0:1, bass.ds(b, 1)], min_val=0, max_val=ITEMS)
                    of = dve.value_load(tile_row[0:1, bass.ds(b, 1)], min_val=0, max_val=TILES)
                    nc.vector.tensor_copy(as_i16(item_words)[:, bass.ds(to * 2, 2 * TILES)],
                                          as_i16(raw_dst[:, :])[:, bass.ds(of * 2, 2 * TILES)]).then_inc(placed, 1)
                    dve.wait_ge(placed, b + 1)
                dve.wait_ge(turned, 1)
                chain(nc.vector.tensor_copy(first_col[0:BLOCKS - 1, :], core.psum[0:BLOCKS - 1, BANK:BANK + 1]))
                nc.vector.tensor_scalar(reached[0:BLOCKS - 1, :], item_w[0:BLOCKS - 1, :],
                                        first_col[0:BLOCKS - 1, 0:1], None, ALU.is_ge).then_inc(reach_ready, 1)
                chain(nc.vector.tensor_scalar(core.words[:, :], item_words[:, 0:ITEMS], 0xFFFF, None, ALU.bitwise_and))
                chain(nc.vector.tensor_scalar(item_i, item_words[:, 0:ITEMS], 16, None, ALU.logical_shift_right))
                dve.wait_ge(blocks_ready, 1)
                chain(nc.vector.tensor_copy(block_f, core.psum[:, 2 * BANK:2 * BANK + ITEMS]))
                chain(nc.vector.tensor_copy(core.block_of[:, :], block_f[0:1, :]))
                chain(nc.vector.scalar_tensor_tensor(core.dloc[:, :], block_f, float(-P), item_i,
                                                     ALU.mult, ALU.add))

            @block.tensor
            def _(pe):
                pe.wait_ge(constant, 11)
                pe.wait_ge(counted, 1)
                nc.tensor.matmul(core.psum[0:1, 0:BLOCKS - 1], core.ones[:, 0:1], starts[:, :],
                                 start=True, stop=True).then_inc(summed, 1)
                pe.wait_ge(firsts_ready, 1)
                nc.tensor.matmul(core.psum[0:BLOCKS - 1, BANK:BANK + 1], first_row[:, 1:BLOCKS], core.ones[0:1, 0:1],
                                 start=True, stop=True).then_inc(turned, 1)
                pe.wait_ge(reach_ready, 1)
                for at in range(0, ITEMS, BANK):
                    end = min(at + BANK, ITEMS)
                    last = nc.tensor.matmul(core.psum[:, 2 * BANK + at:2 * BANK + end], core.ones[0:BLOCKS - 1, :],
                                            reached[0:BLOCKS - 1, at:end], start=True, stop=True)
                last.then_inc(blocks_ready, 1)


def count_edges(core):
    nc = core.nc
    with ExitStack() as stage:
        sb = lambda *a: core.sb(*a, stage)
        sem = lambda n: core.sem(n, stage)
        source_no = sb("source_no", [P, PADDED], I16)
        source = sb("item_source", [P, ITEMS], F32)
        src_hot = sb("src_hot", [P, 2, PADDED], BF16)
        dst_hot = sb("dst_hot", [P, 2, P], BF16)
        zeros = sb("zeros16", [P, BANK], BF16)
        iota_ready, source_ready = sem("c_iota"), sem("c_source")
        zeros_ready = sem("c_zeros")
        hots_ready, items_added, banks_stored = sem("c_hots"), sem("c_added"), sem("c_stored")
        banks = len(CHUNKS)
        with nc.Block() as block:
            @block.gpsimd
            def _(pool):
                pool.iota(source_no[:, :], [[1, PADDED]], base=0, channel_multiplier=0).then_inc(iota_ready, 1)
                pool.memset(zeros[:, :], 0.0).then_inc(zeros_ready, 1)

            @block.vector
            def _(dve):
                words = source[:, :].bitcast(I32)
                chain = Chain(dve, source_ready)
                chain(nc.vector.tensor_scalar(words, core.words[:, :], 4, None, ALU.logical_shift_right))
                chain(nc.vector.tensor_copy(source[:, :], words))
                dve.wait_ge(iota_ready, 1)

                def one_hots(slot, w):
                    col = slice(w, w + 1) if isinstance(w, int) else bass.ds(w, 1)
                    nc.vector.tensor_scalar(dst_hot[:, slot, :], core.iota[:, :], core.dloc[:, col], None,
                                            ALU.is_equal)
                    nc.vector.tensor_scalar(src_hot[:, slot, :], source_no[:, :], source[:, col], None,
                                            ALU.is_equal).then_inc(hots_ready, 1)

                one_hots(0, 0)
                one_hots(1, 1)
                with dve.Fori(1, PAIRS) as pair:
                    for slot in range(2):
                        dve.wait_ge(items_added, pair * 2 - 1 + slot)
                        one_hots(slot, pair * 2 + slot)

            @block.tensor
            def _(pe):
                pe.wait_ge(zeros_ready, 1)

                def block_counts(b):
                    first = pe.value_load(core.bounds[0:1, bass.ds(b, 1)], min_val=0, max_val=PAIRS - 1)
                    end = pe.value_load(core.bounds[0:1, bass.ds(b + 1, 1)], min_val=1, max_val=PAIRS)
                    for n, (lo, hi) in enumerate(CHUNKS):
                        if not isinstance(b, int):
                            pe.wait_ge(banks_stored, b * banks - (banks - 1 - n))
                        nc.tensor.matmul(core.psum[:, lo:hi], zeros[:, 0:P], zeros[:, 0:hi - lo],
                                         start=True, stop=True, skip_group_check=True)
                    with pe.Fori(first, end) as pair:
                        for slot in range(2):
                            pe.wait_ge(hots_ready, pair * 2 + (slot + 1))
                            for lo, hi in CHUNKS:
                                last = nc.tensor.matmul(core.psum[:, lo:hi], dst_hot[:, slot, :],
                                                        src_hot[:, slot, lo:hi],
                                                        start=False, stop=True, skip_group_check=True)
                            last.then_inc(items_added, 1)

                block_counts(0)
                with pe.Fori(1, BLOCKS) as b:
                    block_counts(b)

            @block.scalar
            def _(act):
                with act.Fori(0, BLOCKS) as b:
                    end = act.value_load(core.bounds[0:1, bass.ds(b + 1, 1)], min_val=1, max_val=PAIRS)
                    act.wait_ge(items_added, end * 2)
                    for n, (lo, hi) in enumerate(CHUNKS):
                        nc.scalar.activation(core.counts[:, bass.ds(b, 1), lo:hi], core.psum[:, lo:hi], ACT.Copy,
                                             accum_out=core.deg[:, bass.ds(b, 1), n:n + 1])\
                          .then_inc(banks_stored, 1)


def transposed_nodes(core, banks_ready, src, width, dst, copied, first_bank=0):
    nc = core.nc

    def on_tensor(pe):
        for b in range(BLOCKS):
            last = nc.tensor.transpose(core.psum[0:width, b * P:(b + 1) * P], src[:, b, :], core.ident[:, :])
            if b % 4 == 3 or b == BLOCKS - 1:
                last.then_inc(banks_ready, 1)

    def on_scalar(act):
        for n, (lo, hi) in enumerate(CHUNKS):
            act.wait_ge(banks_ready, n + 1)
            nc.scalar.activation(dst[0:width, lo:hi], core.psum[0:width, lo:hi], ACT.Copy).then_inc(copied, 1)

    return on_tensor, on_scalar


def bcast(ap, shape):
    return ap.to_broadcast(shape)


def layernorm(core, chain, act_turn, dve_turn, x, work, stat):
    nc = core.nc
    total, var = stat[:, 0, :], stat[:, 1, :]
    width = x.shape[2]
    chain(nc.vector.tensor_reduce(total, x, AX.X, ALU.add))
    chain(nc.vector.tensor_scalar(total, total, 1.0 / width, None, ALU.mult))
    chain(nc.vector.tensor_tensor(x, x, total.unsqueeze(2).to_broadcast(x.shape), ALU.subtract))
    chain(nc.vector.tensor_tensor(work, x, x, ALU.mult))
    nc.vector.tensor_reduce(var, work, AX.X, ALU.add).then_inc(dve_turn, 1)
    chain.engine.wait_ge(act_turn, 1)
    chain(nc.vector.reciprocal(total, stat[:, 2, :]))
    chain(nc.vector.tensor_tensor(x, x, total.unsqueeze(2).to_broadcast(x.shape), ALU.mult))


def layernorm_root(core, act, dve_turn, act_turn, stat, width):
    act.wait_ge(dve_turn, 1)
    core.nc.scalar.activation(stat[:, 2, :], stat[:, 1, :], ACT.Sqrt, bias=core.eps[:, 0:1],
                              scale=1.0 / width).then_inc(act_turn, 1)


def split_parts(nc, chain, value, parts):
    hi, mid, lo = (parts[:, :, k * D:(k + 1) * D] for k in range(3))
    chain(nc.vector.tensor_copy(hi, value))
    chain(nc.vector.tensor_tensor(value, value, hi, ALU.subtract))
    chain(nc.vector.tensor_copy(mid, value))
    chain(nc.vector.tensor_tensor(lo, value, mid, ALU.subtract))


def bilinear_layer(core):
    nc, ins = core.nc, core.ins
    with ExitStack() as stage:
        sb = lambda *a: core.sb(*a, stage)
        sem = lambda n: core.sem(n, stage)
        stack = sb("b_stack", [P, BLOCKS, 2 * D], F32)
        wide = sb("b_wide", [P, PADDED], F32)
        parts = wide[:, 0:BLOCKS * 3 * D // 2].bitcast(BF16).rearrange("p (b k) -> p b k", b=BLOCKS)
        turned = sb("b_turned", [P, 2, 7, P], BF16)
        weights = sb("b_weights", [P, D], F32)
        bias = sb("b_bias", [P, 2, D], F32)
        norm = core.stat[:, 3, :]
        loaded, step, root_of, rooted = sem("b_loaded"), sem("b_step"), sem("b_rootof"), sem("b_rooted")
        parts_ready, turned_in_psum, turned_ready = sem("b_parts"), sem("b_tpsum"), [sem("b_turned0"), sem("b_turned1")]
        turned_used, sums_stored = sem("b_used"), sem("b_sumstored")
        stack_ready, banks_ready, copied, products = sem("b_stack_s"), sem("b_banks"), sem("b_copied"), sem("b_prod")
        ln_var, ln_root = sem("b_lnvar"), sem("b_lnroot")
        groups = [range(0, 7), range(7, 13), range(13, 19), range(19, 25)]
        turned_psum = [core.bank(k).bitcast(BF16).rearrange("p (t d) -> p t d", d=P) for k in (0, 1)]
        sums = core.bank(2)[:, 0:3 * D]
        on_tensor, on_scalar = transposed_nodes(core, banks_ready, stack, P, wide, copied)
        with nc.Block() as block:
            @block.sync
            def _(sp):
                sp.dma_start(weights[0:D, :], ins["w_f"]).then_inc(loaded, 16)
                sp.dma_start(weights[D:P, :], ins["w_xf"]).then_inc(loaded, 16)
                for k, name in enumerate(("b_f", "b_xf")):
                    sp.dma_start(bias[:, k, :], ins[name].to_broadcast([P, D])).then_inc(loaded, 16)

            @block.vector
            def _(dve):
                chain = Chain(dve, step)
                dve.sem_inc(sums_stored, 1)
                chain(nc.vector.tensor_reduce(norm, core.deg[:, :, :], AX.X, ALU.add))
                nc.vector.tensor_scalar(norm, norm, 1.0, None, ALU.max).then_inc(root_of, 1)
                dve.wait_ge(rooted, 1)
                chain(nc.vector.reciprocal(norm, core.stat[:, 2, :]))
                value = stack[:, :, 0:D]
                per_node = norm.unsqueeze(2).to_broadcast([P, BLOCKS, D])
                chain(nc.vector.tensor_tensor(value, core.x[:, :, :], per_node, ALU.mult))
                split_parts(nc, chain, value, parts)
                nc.vector.memset(core.stat[:, 0, :], 0.0).then_inc(parts_ready, 1)
                with dve.Fori(0, BLOCKS) as b:
                    for n, group in enumerate(groups):
                        if n % 2:
                            dve.wait_ge(turned_in_psum, b * 4 + (n + 1))
                            dve.wait_ge(turned_used, b * 4 + (n + 1))
                            nc.vector.tensor_copy(turned[:, 1, 0:len(group), :],
                                                  turned_psum[1][:, 0:len(group), :]).then_inc(turned_ready[1], 1)
                    dve.wait_ge(turned_used, b * 4 + 6)
                    nc.vector.tensor_reduce(stack[:, bass.ds(b, 1), 0:D], sums.rearrange("p (k f) -> p f k", k=3),
                                            AX.X, ALU.add).then_inc(sums_stored, 1)
                dve.wait_ge(sums_stored, BLOCKS + 1)
                chain(nc.vector.tensor_tensor(value, value, per_node, ALU.mult))
                nc.vector.tensor_tensor(stack[:, :, D:2 * D], value, core.x[:, :, :], ALU.mult).then_inc(stack_ready, 1)
                dve.wait_ge(loaded, 64)
                chain(nc.vector.tensor_tensor(bias[:, 0, :], bias[:, 0, :], bias[:, 1, :], ALU.add))
                chain(nc.vector.tensor_tensor(core.x[:, :, :], core.x[:, :, :],
                                              bias[:, 0:1, :].to_broadcast([P, BLOCKS, D]), ALU.add))
                dve.wait_ge(products, 1)
                chain(nc.vector.tensor_tensor(core.x[:, :, :], core.x[:, :, :],
                                              core.psum[:, 0:BLOCKS * D].rearrange("p (b f) -> p b f", f=D), ALU.add))
                layernorm(core, chain, ln_root, ln_var, core.x[:, :, :], stack[:, :, 0:D], core.stat)

            @block.scalar
            def _(act):
                act.wait_ge(root_of, 1)
                nc.scalar.activation(core.stat[:, 2, :], norm, ACT.Sqrt).then_inc(rooted, 1)
                with act.Fori(0, BLOCKS) as b:
                    for n, group in enumerate(groups):
                        if n % 2 == 0:
                            act.wait_ge(turned_in_psum, b * 4 + (n + 1))
                            act.wait_ge(turned_used, b * 4 + (n + 1))
                            nc.scalar.activation(turned[:, 0, 0:len(group), :], turned_psum[0][:, 0:len(group), :],
                                                 ACT.Copy).then_inc(turned_ready[0], 1)
                on_scalar(act)
                layernorm_root(core, act, ln_var, ln_root, core.stat, D)

            @block.tensor
            def _(pe):
                pe.sem_inc(turned_used, 2)
                pe.wait_ge(parts_ready, 1)

                def turn(b, n):
                    for t, j in enumerate(groups[n]):
                        last = nc.tensor.transpose(turned_psum[n % 2][:, t, :],
                                                   core.counts[:, bass.ds(b, 1), j * P:(j + 1) * P],
                                                   core.ident16[:, :])
                    last.then_inc(turned_in_psum, 1)

                with pe.Fori(0, BLOCKS) as b:
                    turn(b, 0)
                    turn(b, 1)
                    pe.wait_ge(sums_stored, b + 1)
                    for n, group in enumerate(groups):
                        pe.wait_ge(turned_ready[n % 2], b * 2 + (n // 2 + 1))
                        for t, j in enumerate(group):
                            last = nc.tensor.matmul(sums, turned[:, n % 2, t, :], parts[:, j, :],
                                                    start=(j == 0), stop=(j == BLOCKS - 1))
                        last.then_inc(turned_used, 1)
                        if n < 2:
                            turn(b, n + 2)
                pe.wait_ge(stack_ready, 1)
                on_tensor(pe)
                pe.wait_ge(copied, len(CHUNKS))
                pe.wait_ge(loaded, 64)
                for b in range(BLOCKS):
                    last = nc.tensor.matmul(core.psum[:, b * D:(b + 1) * D], wide[:, b * P:(b + 1) * P],
                                            weights[:, :], start=True, stop=True)
                last.then_inc(products, 1)


def interaction_layer(core):
    nc, ins = core.nc, core.ins
    with ExitStack() as stage:
        sb = lambda *a: core.sb(*a, stage)
        sem = lambda n: core.sem(n, stage)
        stack = sb("i_stack", [P, BLOCKS, 2 * D], F32)
        wide = sb("i_wide", [P, PADDED], F32)
        parts = wide[:, 0:BLOCKS * 3 * D // 2].bitcast(BF16).rearrange("p (b k) -> p b k", b=BLOCKS)
        weights = sb("i_weights", [P, 2 * D], F32)
        bias = sb("i_bias", [P, 1, 2 * D], F32)
        norm, root = core.stat[:, 3, :], core.stat[:, 2, :]
        has_edges = core.stat[:, 0, :]
        loaded, cleared, step = sem("i_loaded"), sem("i_cleared"), sem("i_step")
        degrees, root_of, rooted = sem("i_degrees"), sem("i_rootof"), sem("i_rooted")
        norm_of, normed = sem("i_normof"), sem("i_normed")
        parts_ready, sums_ready, sums_stored = sem("i_parts"), sem("i_sums"), sem("i_stored")
        stack_ready, banks_ready, copied, products = sem("i_stack_s"), sem("i_banks"), sem("i_copied"), sem("i_prod")
        ln_var, ln_root = sem("i_lnvar"), sem("i_lnroot")
        sums = [core.bank(k)[:, 0:3 * D] for k in (0, 1)]
        on_tensor, on_scalar = transposed_nodes(core, banks_ready, stack, P, wide, copied)
        with nc.Block() as block:
            @block.gpsimd
            def _(pool):
                pool.memset(weights[:, :], 0.0).then_inc(cleared, 1)

            @block.sync
            def _(sp):
                sp.wait_ge(cleared, 1)
                sp.dma_start(weights[0:D, 0:D], ins["w_gcn"]).then_inc(loaded, 16)
                sp.dma_start(weights[D:P, D:2 * D], ins["w_int"]).then_inc(loaded, 16)
                sp.dma_start(bias[:, 0, 0:D], ins["b_gcn"].to_broadcast([P, D])).then_inc(loaded, 16)
                sp.dma_start(bias[:, 0, D:2 * D], ins["b_int"].to_broadcast([P, D])).then_inc(loaded, 16)

            @block.tensor
            def _(pe):
                with pe.Fori(0, BLOCKS) as j:
                    for b in range(BLOCKS):
                        last = nc.tensor.matmul(core.bank(7)[:, bass.ds(j, 1)],
                                                core.counts[:, b, bass.ds(j * P, P)], core.ones16[:, :],
                                                start=(b == 0), stop=(b == BLOCKS - 1))
                    last.then_inc(degrees, 1)
                pe.wait_ge(parts_ready, 1)

                def gather_sources(j, slot, turn):
                    pe.wait_ge(sums_stored, turn)
                    for b in range(BLOCKS):
                        last = nc.tensor.matmul(sums[slot], core.counts[:, b, bass.ds(j * P, P)], parts[:, b, :],
                                                start=(b == 0), stop=(b == BLOCKS - 1))
                    last.then_inc(sums_ready, 1)

                with pe.Fori(0, BLOCKS // 2) as pair:
                    for slot in range(2):
                        gather_sources(pair * 2 + slot, slot, pair * 2 + (slot + 1))
                gather_sources(BLOCKS - 1, 0, BLOCKS)
                pe.wait_ge(stack_ready, 1)
                on_tensor(pe)
                pe.wait_ge(copied, len(CHUNKS))
                pe.wait_ge(loaded, 64)
                for b in range(BLOCKS):
                    last = nc.tensor.matmul(core.psum[:, b * P:(b + 1) * P], wide[:, b * P:(b + 1) * P],
                                            weights[:, :], start=True, stop=True)
                last.then_inc(products, 1)

            @block.scalar
            def _(act):
                act.wait_ge(root_of, 1)
                nc.scalar.activation(root, norm, ACT.Sqrt).then_inc(rooted, 1)
                on_scalar(act)
                act.wait_ge(norm_of, 1)
                nc.scalar.activation(root, norm, ACT.Sqrt).then_inc(normed, 1)
                layernorm_root(core, act, ln_var, ln_root, core.stat, D)

            @block.vector
            def _(dve):
                chain = Chain(dve, step)
                dve.sem_inc(sums_stored, 2)
                dve.wait_ge(degrees, BLOCKS)
                degree = core.bank(7)[:, 0:BLOCKS]
                chain(nc.vector.tensor_scalar(has_edges, degree, 0.0, None, ALU.is_gt))
                nc.vector.tensor_scalar(norm, degree, 1.0, None, ALU.max).then_inc(root_of, 1)
                dve.wait_ge(rooted, 1)
                chain(nc.vector.reciprocal(norm, root))
                chain(nc.vector.tensor_tensor(norm, norm, has_edges, ALU.mult))
                value = stack[:, :, 0:D]
                per_node = norm.unsqueeze(2).to_broadcast([P, BLOCKS, D])
                chain(nc.vector.tensor_tensor(value, core.x[:, :, :], per_node, ALU.mult))
                split_parts(nc, chain, value, parts)
                nc.vector.memset(has_edges, 0.0).then_inc(parts_ready, 1)

                def store(j, slot, turn):
                    dve.wait_ge(sums_ready, turn)
                    nc.vector.tensor_reduce(stack[:, bass.ds(j, 1), 0:D],
                                            sums[slot].rearrange("p (k f) -> p f k", k=3),
                                            AX.X, ALU.add).then_inc(sums_stored, 1)

                with dve.Fori(0, BLOCKS // 2) as pair:
                    for slot in range(2):
                        store(pair * 2 + slot, slot, pair * 2 + (slot + 1))
                store(BLOCKS - 1, 0, BLOCKS)
                dve.wait_ge(sums_stored, BLOCKS + 2)
                chain(nc.vector.tensor_tensor(value, value, per_node, ALU.mult))
                nc.vector.tensor_tensor(stack[:, :, D:2 * D], value, core.x[:, :, :], ALU.mult).then_inc(stack_ready, 1)
                dve.wait_ge(loaded, 64)
                dve.wait_ge(products, 1)
                chain(nc.vector.tensor_tensor(stack[:, :, :], core.psum[:, 0:PADDED].rearrange("p (b f) -> p b f", f=P),
                                              bias[:, :, :].to_broadcast([P, BLOCKS, 2 * D]), ALU.add))
                chain(nc.vector.scalar_tensor_tensor(stack[:, :, :], stack[:, :, :], 0.2, stack[:, :, :],
                                                     ALU.mult, ALU.max))
                u, square = stack[:, :, 0:D], stack[:, :, D:2 * D]
                chain(nc.vector.tensor_tensor(u, u, square, ALU.add))
                chain(nc.vector.tensor_tensor(square, u, u, ALU.mult))
                chain(nc.vector.tensor_reduce(norm, square, AX.X, ALU.add))
                nc.vector.tensor_scalar(norm, norm, 1e-12, None, ALU.max).then_inc(norm_of, 1)
                dve.wait_ge(normed, 1)
                chain(nc.vector.reciprocal(norm, root))
                chain(nc.vector.tensor_tensor(u, u, per_node, ALU.mult))
                chain(nc.vector.tensor_tensor(core.x[:, :, :], core.x[:, :, :], u, ALU.add))
                layernorm(core, chain, ln_root, ln_var, core.x[:, :, :], u, core.stat)


def gather_rows(core, pool, table, index, staged, rows, used, staged_ready, started, gathered):
    nc = core.nc

    def group(r, slot):
        q = r * RING + slot
        if not isinstance(r, int):
            pool.wait_ge(used, (q - (RING - 1)) * GROUP)
        nc.gpsimd.tensor_copy(staged[:, slot, :], index[:, bass.ds(q * GROUP, GROUP)]).then_inc(staged_ready, 1)
        pool.wait_ge(staged_ready, q + 1)
        pool.sem_inc(started, 1)
        for u in range(GROUP):
            nc.gpsimd.indirect_dma_start(
                out=rows[:, slot, u, :], out_offset=None, in_=table,
                in_offset=bass.IndirectOffsetOnAxis(ap=staged[:, slot, u:u + 1], axis=0)).then_inc(gathered[slot], 16)

    for slot in range(RING):
        group(0, slot)
    with pool.Fori(1, ROUNDS) as r:
        for slot in range(RING):
            group(r, slot)


def destination_hots(core, hots, slot, q):
    return core.nc.vector.tensor_tensor(
        hots[:, slot, :, :], core.iota[:, :].unsqueeze(1).to_broadcast([P, GROUP, P]),
        core.dloc[:, bass.ds(q * GROUP, GROUP)].unsqueeze(2).to_broadcast([P, GROUP, P]), ALU.is_equal)


def blocks_of_group(core, engine, q):
    return [engine.value_load(core.block_of[0:1, bass.ds(q * GROUP + u, 1)], min_val=0, max_val=BLOCKS - 1)
            for u in range(GROUP)]


def relation_layer(core):
    nc, ins = core.nc, core.ins
    with ExitStack() as stage:
        sem = lambda n: core.sem(n, stage)
        weights, x_t, made, rows, hots, staged = core.tail_views(
            ([P, RELATIONS, D], F32), ([P, PADDED], F32), ([P, 2, RELATIONS * D], F32),
            ([P, RING, GROUP, D], F32), ([P, RING, GROUP, P], F32), ([P, RING, GROUP], I32))
        mask0 = core.sb("r_mask0", [P, PADDED], U8, stage)
        zeros = core.tail_views(([P, RELATIONS, D], F32), ([P, BANK], F32))[1]
        table = nc.dram_tensor("relation_table", [PADDED * RELATIONS, D], F32).ap()
        table_rows = table.rearrange("(n r) f -> n (r f)", r=RELATIONS)
        masked, loaded, step = sem("r_masked"), sem("r_loaded"), sem("r_step")
        banks_ready, copied = sem("r_banks"), sem("r_copied")
        multiplied, evacuated = sem("r_multiplied"), [sem("r_evac0"), sem("r_evac1")]
        written = [sem("r_written0"), sem("r_written1")]
        used, gathered = sem("r_used"), [sem(f"r_gathered{n}") for n in range(RING)]
        started = sem("r_started")
        staged_ready, hots_ready, zeros_ready = sem("r_staged"), sem("r_hots"), sem("r_zeros")
        summed, ln_var, ln_root = sem("r_summed"), sem("r_lnvar"), sem("r_lnroot")
        on_tensor, on_scalar = transposed_nodes(core, banks_ready, core.x, D, x_t, copied)
        sums = core.psum[:, 0:BLOCKS * D]
        with nc.Block() as block:
            @block.sync
            def _(sp):
                sp.wait_ge(masked, BLOCKS)
                sp.dma_start(weights[0:D, :, :], ins["w_rel"].rearrange("r i o -> i r o")).then_inc(loaded, 16)
                for b in range(BLOCKS):
                    sp.wait_ge(evacuated[b % 2], b // 2 + 1)
                    sp.dma_start(table_rows[b * P:(b + 1) * P, :], made[:, b % 2, :]).then_inc(written[b % 2], 16)

            @block.gpsimd
            def _(pool):
                pool.wait_ge(masked, BLOCKS)
                pool.wait_ge(written[0], 16 * (BLOCKS - BLOCKS // 2))
                pool.wait_ge(written[1], 16 * (BLOCKS // 2))
                gather_rows(core, pool, table, core.words, staged, rows, used, staged_ready, started, gathered)

            @block.vector
            def _(dve):
                for b in range(BLOCKS):
                    nc.vector.tensor_scalar(core.mask[:, b, :] if b else mask0[:, :], core.counts[:, b, :], 0.0, None,
                                            ALU.is_gt).then_inc(masked, 1)
                    dve.wait_ge(masked, b + 1)
                nc.vector.tensor_copy(core.mask[:, 0, :], mask0[:, :])
                for b in range(1, BLOCKS, 2):
                    dve.wait_ge(multiplied, b + 1)
                    if b > 2:
                        dve.wait_ge(written[1], 16 * (b // 2))
                    nc.vector.tensor_copy(made[:, 1, :], core.bank(2 * (b % 4), 2)).then_inc(evacuated[1], 1)
                dve.wait_ge(written[0], 16 * (BLOCKS - BLOCKS // 2))
                dve.wait_ge(copied, len(CHUNKS))
                dve.wait_ge(multiplied, BLOCKS)
                nc.vector.memset(zeros, 0.0).then_inc(zeros_ready, 1)
                for slot in range(RING):
                    destination_hots(core, hots, slot, slot).then_inc(hots_ready, 1)
                with dve.Fori(1, ROUNDS) as r:
                    for slot in range(RING):
                        dve.wait_ge(used, (r * RING + slot - (RING - 1)) * GROUP)
                        destination_hots(core, hots, slot, r * RING + slot).then_inc(hots_ready, 1)
                chain = Chain(dve, step)
                dve.wait_ge(summed, 1)
                chain(nc.vector.tensor_tensor(core.x[:, :, :], core.x[:, :, :],
                                              sums.rearrange("p (b f) -> p b f", f=D), ALU.add))
                chain(nc.vector.tensor_scalar(core.words[:, :], core.words[:, :], 4, None, ALU.logical_shift_right))
                work = x_t[:, 0:BLOCKS * D].rearrange("p (b f) -> p b f", f=D)
                layernorm(core, chain, ln_root, ln_var, core.x[:, :, :], work, core.stat)

            @block.scalar
            def _(act):
                act.wait_ge(masked, BLOCKS)
                on_scalar(act)
                for b in range(0, BLOCKS, 2):
                    act.wait_ge(multiplied, b + 1)
                    if b > 1:
                        act.wait_ge(written[0], 16 * (b // 2))
                    nc.scalar.activation(made[:, 0, :], core.bank(2 * (b % 4), 2), ACT.Copy)\
                      .then_inc(evacuated[0], 1)
                layernorm_root(core, act, ln_var, ln_root, core.stat, D)

            @block.tensor
            def _(pe):
                on_tensor(pe)
                pe.wait_ge(copied, len(CHUNKS))
                pe.wait_ge(loaded, 16)
                flat = weights[0:D, :, :].rearrange("p r f -> p (r f)")
                for b in range(BLOCKS):
                    if b >= 4:
                        pe.wait_ge(evacuated[b % 2], (b - 4) // 2 + 1)
                    for n in range(2):
                        last = nc.tensor.matmul(core.bank(2 * (b % 4) + n), x_t[0:D, b * P:(b + 1) * P],
                                                flat[:, n * BANK:(n + 1) * BANK], start=True, stop=True)
                    last.then_inc(multiplied, 1)
                pe.wait_ge(evacuated[0], BLOCKS - BLOCKS // 2)
                pe.wait_ge(evacuated[1], BLOCKS // 2)
                pe.wait_ge(zeros_ready, 1)
                for n in range(4):
                    nc.tensor.matmul(core.bank(n), zeros[:, 0:P], zeros, start=True, stop=True,
                                     skip_group_check=True)
                with pe.Fori(0, ROUNDS) as r:
                    for slot in range(RING):
                        q = r * RING + slot
                        blocks = blocks_of_group(core, pe, q)
                        pe.wait_ge(hots_ready, q + 1)
                        pe.wait_ge(gathered[slot], (r + 1) * (16 * GROUP))
                        for u, b in enumerate(blocks):
                            nc.tensor.matmul(core.psum[:, bass.ds(b * D, D)], hots[:, slot, u, :],
                                             rows[:, slot, u, :], start=False, stop=True,
                                             skip_group_check=True).then_inc(used, 1)
                pe.wait_ge(used, ITEMS)
                pe.sem_inc(summed, 1)


ROW = HD + HEADS
WIDE = HD + 2 * HEADS


def attention_layer(core, acc, layer):
    nc, ins = core.nc, core.ins
    depth = D if layer == 0 else HD
    halves = -(-depth // P)
    rows_used = min(depth, P)
    with ExitStack() as stage:
        sb = lambda *a: core.sb(*a, stage)
        sem = lambda n: core.sem(f"a{layer}_{n}", stage)
        weights, vectors, product, repeated, turned = core.tail_views(
            ([P, 2, WIDE], F32), ([P, 2, HD], F32), ([P, HD], F32), ([P, 2, HEADS, P], F32), ([P, 2, PADDED], F32))
        before = ([P, 2, WIDE], F32), ([P, 2, HD], F32), ([P, HD], F32), ([P, 2, HEADS, P], F32), ([P, 2, PADDED], F32)
        level, masked_out = core.tail_views(*before, ([P, 2, PADDED], F32), ([P, PADDED], BF16))[-2:]
        rows, hots, hots_t = core.tail_views(*before, ([P, RING, GROUP, ROW], F32), ([P, RING, GROUP, P], F32),
                                             ([P, 2, GROUP, P], F32))[-3:]
        logits = sb(f"a{layer}_logits", [P, 2, GROUP, HEADS], F32)
        staged = sb(f"a{layer}_staged", [P, RING, GROUP], I32)
        at_dst = sb(f"a{layer}_at_dst", [P, BLOCKS, 2 * HEADS], F32)
        own = sb(f"a{layer}_own", [P, BLOCKS, HEADS], F32)
        best = sb(f"a{layer}_best", [P, BLOCKS, HEADS], F32)
        least = sb(f"a{layer}_least", [P, HEADS], F32)
        table = nc.dram_tensor(f"attention_table{layer}", [PADDED, ROW], F32).ap()
        loaded, step = sem("loaded"), sem("step")
        weights_ready, projected, evacuated, written = (sem(n) for n in ("weights", "projected", "evac", "written"))
        levels_in_psum, levels_ready, level_used = sem("lpsum"), sem("levels"), sem("lused")
        node_logits, self_ready = sem("nlogits"), sem("self")
        self_of, pass_ready = sem("self_of"), sem("pass_ready")
        gathered = [sem(f"gathered{n}") for n in range(RING)]
        staged_ready, started, hots_ready = sem("staged_s"), sem("started"), sem("hots_s")
        turned_in_psum, turned_ready, fetched = sem("tpsum"), sem("turned"), sem("fetched")
        logits_ready, exps_ready, messages_ready = sem("logits_s"), sem("exps"), sem("messages")
        used, stored, logit_steps = sem("used"), sem("stored"), sem("lsteps")
        hots_psum = [core.bank(k)[:, 0:GROUP * P].rearrange("p (u e) -> p u e", u=GROUP) for k in (0, 1)]
        fetch_psum = [core.bank(k)[:, 0:GROUP * 2 * HEADS]
                      .rearrange("p (u h) -> p u h", u=GROUP) for k in (2, 7)]
        sums = [[core.bank(3 + k * (GROUP // 2) + pair)[:, 0:ROW] for pair in range(GROUP // 2)] for k in (0, 1)]
        with nc.Block() as block:
            @block.sync
            def _(sp):
                w = ins[f"w_gat{layer}"]
                for n in range(halves):
                    sp.dma_start(weights[0:rows_used, n, 0:HD], w[n * P:n * P + rows_used, :]).then_inc(loaded, 16)
                for n, name in enumerate(("att_src", "att_dst")):
                    sp.dma_start(vectors[:, n, :], ins[f"{name}{layer}"].to_broadcast([P, HD])).then_inc(loaded, 16)
                sp.wait_ge(evacuated, BLOCKS)
                sp.dma_start(table.rearrange("(b p) c -> p b c", p=P), acc[:, :, 0:ROW]).then_inc(written, 16)

            @block.gpsimd
            def _(pool):
                pool.wait_ge(written, 16)
                pool.wait_ge(pass_ready, 1)
                gather_rows(core, pool, table, core.words, staged, rows, used, staged_ready, started, gathered)

            @block.tensor
            def _(pe):
                pe.wait_ge(weights_ready, 1)
                for b in range(BLOCKS):
                    if b >= 8:
                        pe.wait_ge(evacuated, b - 7)
                    for n in range(halves):
                        last = nc.tensor.matmul(core.bank(b % 8)[:, 0:WIDE],
                                                turned[0:rows_used, n, b * P:(b + 1) * P], weights[0:rows_used, n, :],
                                                start=(n == 0), stop=(n == halves - 1))
                    last.then_inc(projected, 1)
                pe.wait_ge(evacuated, BLOCKS)
                for h in range(HEADS):
                    for c, (lo, hi) in enumerate(CHUNKS):
                        if h:
                            pe.wait_ge(levels_ready, (h - 1) * len(CHUNKS) + c + 1)
                        for n in range(halves):
                            last = nc.tensor.matmul(core.psum[:, lo:hi], repeated[0:rows_used, n, h, :],
                                                    turned[0:rows_used, n, lo:hi],
                                                    start=(n == 0), stop=(n == halves - 1))
                        last.then_inc(levels_in_psum, 1)
                pe.wait_ge(levels_ready, HEADS * len(CHUNKS))
                pe.wait_ge(pass_ready, 1)

                def turn_hots(q, slot):
                    pe.wait_ge(hots_ready, q + 1)
                    if not (isinstance(q, int) and q < 2):
                        pe.wait_ge(turned_ready, q - 1)
                    for u in range(GROUP):
                        last = nc.tensor.transpose(hots_psum[slot % 2][:, u, :], hots[:, slot, u, :], core.ident[:, :])
                    last.then_inc(turned_in_psum, 1)

                def fetch(q, slot):
                    blocks = blocks_of_group(core, pe, q)
                    pe.wait_ge(turned_ready, q + 1)
                    for u, b in enumerate(blocks):
                        last = nc.tensor.matmul(fetch_psum[slot % 2][:, u, :], hots_t[:, slot % 2, u, :],
                                                at_dst[:, bass.ds(b, 1), :], start=True, stop=True)
                    last.then_inc(fetched, 1)

                def add_up(q, slot, first):
                    pe.wait_ge(messages_ready, q + 1)
                    for pair in range(GROUP // 2):
                        if not first:
                            pe.wait_ge(stored, q * (GROUP // 2) + (pair + 1 - GROUP))
                        for u in (2 * pair, 2 * pair + 1):
                            nc.tensor.matmul(sums[slot % 2][pair], hots[:, slot, u, :], rows[:, slot, u, :],
                                             start=(u % 2 == 0), stop=(u % 2 == 1)).then_inc(used, 1)

                def turn(r, slot, first=False, left=2):
                    q = r * RING + slot
                    if left >= 1:
                        fetch(q + 1, (slot + 1) % RING)
                    if left >= 2:
                        turn_hots(q + 2, (slot + 2) % RING)
                    add_up(q, slot, first)

                turn_hots(0, 0)
                turn_hots(1, 1)
                fetch(0, 0)
                for slot in range(RING):
                    turn(0, slot, first=slot < 2)
                with pe.Fori(1, ROUNDS - 1) as r:
                    for slot in range(RING):
                        turn(r, slot)
                for slot in range(RING):
                    turn(ROUNDS - 1, slot, left=RING - 1 - slot)

            @block.scalar
            def _(act):
                for b in range(BLOCKS):
                    act.wait_ge(projected, b + 1)
                    nc.scalar.activation(acc[:, b, :], core.bank(b % 8)[:, 0:WIDE], ACT.Copy).then_inc(evacuated, 1)
                for h in range(HEADS):
                    if h >= 2:
                        act.wait_ge(level_used, h - 1)
                    for c, (lo, hi) in enumerate(CHUNKS):
                        act.wait_ge(levels_in_psum, h * len(CHUNKS) + c + 1)
                        nc.scalar.activation(level[:, h % 2, lo:hi], core.psum[:, lo:hi], ACT.Copy)\
                          .then_inc(levels_ready, 1)
                act.wait_ge(node_logits, 1)
                nc.scalar.activation(own[:, :, :], own[:, :, :], ACT.Exp).then_inc(self_ready, 1)
                act.wait_ge(pass_ready, 1)


                def keep_turned(q, slot):
                    act.wait_ge(turned_in_psum, q + 1)
                    if not (isinstance(q, int) and q < 2):
                        act.wait_ge(fetched, q - 1)
                    nc.scalar.activation(hots_t[:, slot % 2, :, :], hots_psum[slot % 2], ACT.Copy)\
                      .then_inc(turned_ready, 1)

                def weights_of(q, slot):
                    act.wait_ge(logits_ready, q + 1)
                    nc.scalar.activation(rows[:, slot, :, HD:ROW], logits[:, slot % 2, :, :], ACT.Exp)\
                      .then_inc(exps_ready, 1)

                def turn(r, slot, left=2):
                    q = r * RING + slot
                    if left >= 1:
                        weights_of(q + 1, (slot + 1) % RING)
                    if left >= 2:
                        keep_turned(q + 2, (slot + 2) % RING)

                keep_turned(0, 0)
                keep_turned(1, 1)
                weights_of(0, 0)
                for slot in range(RING):
                    turn(0, slot)
                with act.Fori(1, ROUNDS - 1) as r:
                    for slot in range(RING):
                        turn(r, slot)
                for slot in range(RING):
                    turn(ROUNDS - 1, slot, left=RING - 1 - slot)

            @block.vector
            def _(dve):
                chain = Chain(dve, step)
                dve.wait_ge(loaded, 16 * (halves + 2))
                for n in range(halves):
                    for which in range(2):
                        chain(nc.vector.tensor_tensor(product[0:rows_used, :], weights[0:rows_used, n, 0:HD],
                                                      vectors[0:rows_used, which, :], ALU.mult))
                        at = HD + which * HEADS
                        chain(nc.vector.tensor_reduce(weights[0:rows_used, n, at:at + HEADS],
                                                      product[0:rows_used, :].rearrange("p (h c) -> p h c", h=HEADS),
                                                      AX.X, ALU.add))
                    chain(nc.vector.tensor_copy(repeated[0:rows_used, n, :, :],
                                                weights[0:rows_used, n, HD:HD + HEADS].unsqueeze(2)
                                                .to_broadcast([rows_used, HEADS, P])))
                dve.sem_inc(weights_ready, 1)
                for h in range(HEADS):
                    dve.wait_ge(levels_ready, (h + 1) * len(CHUNKS))
                    chain(nc.vector.tensor_reduce(least[:, h:h + 1], level[:, h % 2, :], AX.X, ALU.min))
                    chain(nc.vector.tensor_scalar(level[:, h % 2, :], level[:, h % 2, :], least[:, h:h + 1], None,
                                                  ALU.subtract))
                    for b in range(BLOCKS):
                        chain(nc.vector.tensor_tensor_reduce(
                            out=masked_out, in0=core.mask[:, b, :], in1=level[:, h % 2, :], scale=1.0, scalar=0.0,
                            op0=ALU.mult, op1=ALU.max, accum_out=best[:, b, h:h + 1]))
                    dve.sem_inc(level_used, 1)
                a_src, a_dst = acc[:, :, HD:ROW], acc[:, :, ROW:WIDE]
                highest = at_dst[:, :, HEADS:2 * HEADS]
                chain(nc.vector.tensor_tensor(best[:, :, :], best[:, :, :],
                                              least[:, :].unsqueeze(1).to_broadcast([P, BLOCKS, HEADS]), ALU.add))
                chain(nc.vector.tensor_tensor(best[:, :, :], best[:, :, :], a_src, ALU.max))
                chain(nc.vector.tensor_tensor(best[:, :, :], best[:, :, :], a_dst, ALU.add))
                chain(nc.vector.scalar_tensor_tensor(highest, best[:, :, :], 0.2, best[:, :, :], ALU.mult, ALU.max))
                chain(nc.vector.tensor_copy(at_dst[:, :, 0:HEADS], a_dst))
                chain(nc.vector.tensor_tensor(own[:, :, :], a_src, a_dst, ALU.add))
                chain(nc.vector.scalar_tensor_tensor(own[:, :, :], own[:, :, :], 0.2, own[:, :, :],
                                                     ALU.mult, ALU.max))
                nc.vector.tensor_tensor(own[:, :, :], own[:, :, :], highest, ALU.subtract).then_inc(node_logits, 1)
                dve.wait_ge(self_ready, 1)
                dve.wait_ge(written, 16)
                by_head = acc[:, :, 0:HD].rearrange("p b (h c) -> p b h c", h=HEADS)
                chain(nc.vector.tensor_tensor(by_head, by_head,
                                              own[:, :, :].unsqueeze(3).to_broadcast([P, BLOCKS, HEADS, D]), ALU.mult))
                chain(nc.vector.tensor_copy(a_src, own[:, :, :]))
                dve.sem_inc(pass_ready, 1)

                def weigh_logits(q, slot):
                    dve.wait_ge(fetched, q + 1)
                    dve.wait_ge(gathered[slot], (q - slot + RING) * (16 * GROUP // RING))
                    e, of_dst = logits[:, slot % 2, :, :], fetch_psum[slot % 2]
                    nc.vector.tensor_tensor(e, rows[:, slot, :, HD:ROW], of_dst[:, :, 0:HEADS],
                                            ALU.add).then_inc(logit_steps, 1)
                    dve.wait_ge(logit_steps, q * 3 + 1)
                    nc.vector.scalar_tensor_tensor(e, e, 0.2, e, ALU.mult, ALU.max).then_inc(logit_steps, 1)
                    dve.wait_ge(logit_steps, q * 3 + 2)
                    nc.vector.tensor_tensor(e, e, of_dst[:, :, HEADS:2 * HEADS], ALU.subtract)\
                      .then_inc(logit_steps, 1)
                    dve.wait_ge(logit_steps, q * 3 + 3)
                    nc.vector.tensor_scalar(e, e, 0.0, None, ALU.min).then_inc(logits_ready, 1)

                def weigh_rows(q, slot):
                    dve.wait_ge(exps_ready, q + 1)
                    message = rows[:, slot, :, 0:HD].rearrange("p u (h c) -> p u h c", h=HEADS)
                    nc.vector.tensor_tensor(message, message,
                                            rows[:, slot, :, HD:ROW].unsqueeze(3).to_broadcast([P, GROUP, HEADS, D]),
                                            ALU.mult).then_inc(messages_ready, 1)

                def store(q, slot):
                    for pair in range(GROUP // 2):
                        b = dve.value_load(core.block_of[0:1, bass.ds(q * GROUP + 2 * pair, 1)],
                                           min_val=0, max_val=BLOCKS - 1)
                        dve.wait_ge(used, q * GROUP + 2 * (pair + 1))
                        if not (isinstance(q, int) and q == 0 and pair == 0):
                            dve.wait_ge(stored, q * (GROUP // 2) + pair)
                        nc.vector.tensor_tensor(acc[:, bass.ds(b, 1), 0:ROW], acc[:, bass.ds(b, 1), 0:ROW],
                                                sums[slot % 2][pair].unsqueeze(1), ALU.add).then_inc(stored, 1)

                def turn(r, slot, before=1, left=RING - 1):
                    q = r * RING + slot
                    weigh_rows(q, slot)
                    if left >= 1:
                        weigh_logits(q + 1, (slot + 1) % RING)
                    if before >= 1:
                        store(q - 1, (slot - 1) % RING)
                    if left >= RING - 1:
                        destination_hots(core, hots, (slot - 1) % RING, q + RING - 1).then_inc(hots_ready, 1)

                for slot in range(RING - 1):
                    destination_hots(core, hots, slot, slot).then_inc(hots_ready, 1)
                weigh_logits(0, 0)
                for slot in range(RING):
                    turn(0, slot, before=slot)
                with dve.Fori(1, ROUNDS - 1) as r:
                    for slot in range(RING):
                        turn(r, slot)
                for slot in range(RING):
                    turn(ROUNDS - 1, slot, left=RING - 1 - slot)
                store(GROUPS - 1, RING - 1)


def attention_layers(core):
    nc, ins = core.nc, core.ins
    before = ([P, 2, WIDE], F32), ([P, 2, HD], F32), ([P, HD], F32), ([P, 2, HEADS, P], F32)
    turned, across = core.tail_views(*before, ([P, 2, PADDED], F32), ([P, PADDED], F32))[-2:]
    acc = core.sb("acc", [P, BLOCKS, WIDE], F32)
    head_affine = core.sb("head_affine", [P, 3, HD], F32)
    with ExitStack() as stage:
        sem = lambda n: core.sem(n, stage)
        weights = core.sb("p_weights", [P, D], F32, stage)
        types, types_f = core.sb("type_of", [P, BLOCKS], I32, stage), core.sb("type_of_f", [P, BLOCKS], F32, stage)
        depth = D + NODE_TYPES + 1
        given, loaded, step = sem("j_given"), sem("j_loaded"), sem("j_step")
        banks_ready, copied, products, turned_out = sem("j_banks"), sem("j_copied"), sem("j_products"), sem("j_out")
        on_tensor, on_scalar = transposed_nodes(core, banks_ready, acc[:, :, 0:depth], depth, across, copied)
        with nc.Block() as block:
            @block.sync
            def _(sp):
                sp.dma_start(types[:, :], ins["types"]).then_inc(loaded, 16)
                sp.dma_start(weights[0:D, :], ins["w_proj"]).then_inc(loaded, 16)
                sp.dma_start(weights[D:D + NODE_TYPES, :], ins["type_emb"]).then_inc(loaded, 16)
                sp.dma_start(weights[depth - 1:depth, :], ins["b_proj"]).then_inc(loaded, 16)
                for n, name in enumerate(("bias0", "gain0", "shift0")):
                    sp.dma_start(head_affine[:, n, :], ins[name].to_broadcast([P, HD])).then_inc(loaded, 16)
                sp.wait_ge(loaded, 16 * 7)

            @block.vector
            def _(dve):
                chain = Chain(dve, step)
                chain(nc.vector.tensor_copy(acc[:, :, 0:D], core.x[:, :, :]))
                dve.wait_ge(loaded, 16 * 7)
                chain(nc.vector.tensor_copy(types_f[:, :], types[:, :]))
                for t in range(NODE_TYPES):
                    chain(nc.vector.tensor_scalar(acc[:, :, D + t:D + t + 1], types_f[:, :].unsqueeze(2), float(t),
                                                  None, ALU.is_equal))
                nc.vector.memset(acc[:, :, depth - 1:depth], 1.0).then_inc(given, 1)

            @block.tensor
            def _(pe):
                pe.wait_ge(given, 1)
                on_tensor(pe)
                pe.wait_ge(copied, len(CHUNKS))
                for lo, hi in CHUNKS:
                    nc.tensor.matmul(core.psum[0:D, lo:hi], weights[0:depth, :], across[0:depth, lo:hi],
                                     start=True, stop=True).then_inc(products, 1)

            @block.scalar
            def _(act):
                on_scalar(act)
                for n, (lo, hi) in enumerate(CHUNKS):
                    act.wait_ge(products, n + 1)
                    nc.scalar.activation(turned[0:D, 0, lo:hi], core.psum[0:D, lo:hi], ACT.Copy)\
                      .then_inc(turned_out, 1)
    attention_layer(core, acc, 0)

    with ExitStack() as stage:
        sem = lambda n: core.sem(n, stage)
        share = core.sb("m_share", [P, BLOCKS, HEADS], F32, stage)
        work = core.tail_views(([P, BLOCKS, HD], F32))[0]
        step, ln_var, ln_root, normed, relued = (sem(f"m_{n}") for n in ("step", "var", "root", "normed", "relued"))
        banks_ready, copied = sem("m_banks"), sem("m_copied")
        hidden = acc[:, :, 0:HD]
        by_head = hidden.rearrange("p b (h c) -> p b h c", h=HEADS)
        with nc.Block() as block:
            @block.vector
            def _(dve):
                chain = Chain(dve, step)
                chain(nc.vector.tensor_scalar(share[:, :, :], acc[:, :, HD:ROW], 1e-16, None, ALU.add))
                chain(nc.vector.reciprocal(share[:, :, :], share[:, :, :]))
                chain(nc.vector.tensor_tensor(by_head, by_head,
                                              share[:, :, :].unsqueeze(3).to_broadcast([P, BLOCKS, HEADS, D]), ALU.mult))
                rows = lambda n: head_affine[:, n:n + 1, :].to_broadcast([P, BLOCKS, HD])
                chain(nc.vector.tensor_tensor(hidden, hidden, rows(0), ALU.add))
                layernorm(core, chain, ln_root, ln_var, hidden, work, core.stat)
                chain(nc.vector.tensor_tensor(hidden, hidden, rows(1), ALU.mult))
                nc.vector.tensor_tensor(hidden, hidden, rows(2), ALU.add).then_inc(normed, 1)

            @block.scalar
            def _(act):
                layernorm_root(core, act, ln_var, ln_root, core.stat, HD)
                act.wait_ge(normed, 1)
                nc.scalar.activation(hidden, hidden, ACT.Relu).then_inc(relued, 1)
                for half in range(2):
                    for n, (lo, hi) in enumerate(CHUNKS):
                        act.wait_ge(banks_ready, half * len(CHUNKS) + n + 1)
                        nc.scalar.activation(turned[:, half, lo:hi], core.psum[:, lo:hi], ACT.Copy).then_inc(copied, 1)

            @block.tensor
            def _(pe):
                pe.wait_ge(relued, 1)
                for half in range(2):
                    for b in range(BLOCKS):
                        if half and b % 4 == 0:
                            pe.wait_ge(copied, b // 4 + 1)
                        last = nc.tensor.transpose(core.psum[:, b * P:(b + 1) * P],
                                                   acc[:, b, half * P:(half + 1) * P], core.ident[:, :])
                        if b % 4 == 3 or b == BLOCKS - 1:
                            last.then_inc(banks_ready, 1)
    attention_layer(core, acc, 1)

    with ExitStack() as stage:
        sem = lambda n: core.sem(n, stage)
        share = core.sb("f_share", [P, BLOCKS, HEADS], F32, stage)
        affine = core.sb("f_affine", [P, 3, D], F32, stage)
        work = core.tail_views(([P, BLOCKS, D], F32))[0]
        mean = acc[:, :, 0:D]
        loaded, step, done, stored = (sem(f"f_{n}") for n in ("loaded", "step", "done", "stored"))
        turns = [(sem(f"f_var{n}"), sem(f"f_root{n}")) for n in range(2)]
        hidden = acc[:, :, 0:HD]
        by_head = hidden.rearrange("p b (h c) -> p b h c", h=HEADS)
        with nc.Block() as block:
            @block.sync
            def _(sp):
                for n, name in enumerate(("bias1", "gain1", "shift1")):
                    sp.dma_start(affine[:, n, :], ins[name].to_broadcast([P, D])).then_inc(loaded, 16)
                sp.wait_ge(done, 1)
                sp.dma_start(core.out, core.x[:, :, :]).then_inc(stored, 16)
                sp.wait_ge(stored, 16)

            @block.vector
            def _(dve):
                chain = Chain(dve, step)
                chain(nc.vector.tensor_scalar(share[:, :, :], acc[:, :, HD:ROW], 1e-16, None, ALU.add))
                chain(nc.vector.reciprocal(share[:, :, :], share[:, :, :]))
                chain(nc.vector.tensor_tensor(by_head, by_head,
                                              share[:, :, :].unsqueeze(3).to_broadcast([P, BLOCKS, HEADS, D]), ALU.mult))
                for h in range(1, HEADS):
                    chain(nc.vector.tensor_tensor(mean, mean, acc[:, :, h * D:(h + 1) * D], ALU.add))
                rows = lambda n: affine[:, n:n + 1, :].to_broadcast([P, BLOCKS, D])
                dve.wait_ge(loaded, 48)
                chain(nc.vector.tensor_scalar(mean, mean, 1.0 / HEADS, None, ALU.mult))
                chain(nc.vector.tensor_tensor(mean, mean, rows(0), ALU.add))
                layernorm(core, chain, turns[0][1], turns[0][0], mean, work, core.stat)
                chain(nc.vector.tensor_tensor(mean, mean, rows(1), ALU.mult))
                chain(nc.vector.tensor_tensor(mean, mean, rows(2), ALU.add))
                chain(nc.vector.scalar_tensor_tensor(core.x[:, :, :], mean, 0.0, core.x[:, :, :], ALU.max, ALU.add))
                layernorm(core, chain, turns[1][1], turns[1][0], core.x[:, :, :], work, core.stat)
                dve.sem_inc(done, 1)

            @block.scalar
            def _(act):
                for variance, root in turns:
                    layernorm_root(core, act, variance, root, core.stat, D)


def build(nc, ins, out, debug=None):
    with ExitStack() as ctx:
        core = Core(nc, ctx, ins, out)
        prepare(core)
        count_edges(core)
        bilinear_layer(core)
        interaction_layer(core)
        relation_layer(core)
        attention_layers(core)
        if debug:
            debug(core)


_VECTORS = {"b_f": "L0_gnn_b1", "b_xf": "L0_gnn_b2", "b_gcn": "L1_gnn_b_gcn", "b_int": "L1_gnn_b_int",
            "b_proj": "L3_gnn_proj_b", "bias0": "L3_gnn_bias0", "gain0": "L3_gnn_ln0_g", "shift0": "L3_gnn_ln0_b",
            "bias1": "L3_gnn_bias1", "gain1": "L3_gnn_ln1_g", "shift1": "L3_gnn_ln1_b",
            "att_src0": "L3_gnn_att_src0", "att_dst0": "L3_gnn_att_dst0",
            "att_src1": "L3_gnn_att_src1", "att_dst1": "L3_gnn_att_dst1"}
_MATRICES = {"w_f": "L0_gnn_W1", "w_xf": "L0_gnn_W2", "w_gcn": "L1_gnn_W_gcn", "w_int": "L1_gnn_W_int",
             "w_rel": "L2_gnn_weight", "w_proj": "L3_gnn_proj_W", "type_emb": "L3_gnn_type_emb",
             "w_gat0": "L3_gnn_W0", "w_gat1": "L3_gnn_W1"}


def laid_out(inputs):
    def edges(name, fill):
        a = np.asarray(inputs[name])
        a = np.concatenate([a, np.full(TILES * P - a.size, fill, a.dtype)])
        return np.ascontiguousarray(a.reshape(TILES, P).T)

    x = np.asarray(inputs["x"])
    x = np.concatenate([x, np.zeros((PADDED - NODES, D), x.dtype)]).reshape(BLOCKS, P, D)
    types = np.asarray(inputs["node_type_3"])
    types = np.concatenate([types, np.zeros(PADDED - NODES, types.dtype)]).reshape(BLOCKS, P).T
    arrays = {"src": edges("src", 0), "dst": edges("dst", NO_NODE), "rel": edges("edge_type_16", 0),
              "x": np.ascontiguousarray(x.transpose(1, 0, 2)), "types": np.ascontiguousarray(types)}
    arrays |= {n: np.asarray(inputs[k]).reshape(1, -1) for n, k in _VECTORS.items()}
    arrays |= {n: np.asarray(inputs[k]) for n, k in _MATRICES.items()}
    return arrays


def kernel(**inputs):
    import concourse.bacc as bacc
    from concourse.bass_utils import run_bass_kernel_spmd

    nc = bacc.Bacc("TRN2", target_bir_lowering=False, num_devices=1)
    arrays = laid_out(inputs)
    ins = {name: nc.dram_tensor(f"in_{name}", a.shape, mybir.dt.from_np(a.dtype), kind="ExternalInput").ap()
           for name, a in arrays.items()}
    out = nc.dram_tensor("out_nodes", [P, BLOCKS, D], F32, kind="ExternalOutput").ap()
    build(nc, ins, out)
    result = run_bass_kernel_spmd(nc, [{f"in_{name}": a for name, a in arrays.items()}], core_ids=[0])
    nodes = result.results[0]["out_nodes"]
    return np.ascontiguousarray(nodes.transpose(1, 0, 2)).reshape(PADDED, D)[:NODES]
```

```python
from contextlib import ExitStack, nullcontext

import numpy as np

import concourse.bass as bass
from concourse import mybir

F32, BF16, I32, I16, U8 = (mybir.dt.float32, mybir.dt.bfloat16, mybir.dt.int32,
                           mybir.dt.int16, mybir.dt.uint8)
ALU = mybir.AluOpType
ACT = mybir.ActivationFunctionType
AX = mybir.AxisListType

P = 128
NODES, EDGES, D = 3125, 103125, 64
RELATIONS, HEADS, NODE_TYPES = 16, 4, 3
HD = HEADS * D
BLOCKS = -(-NODES // P)
PADDED = BLOCKS * P
TILES = -(-EDGES // P)
GROUP, RING = 4, 4
PAIRS = (TILES + BLOCKS - 1 + BLOCKS) // 2
FULL_ITEMS = 2 * PAIRS
ROUNDS = 2 * -(-FULL_ITEMS // (2 * GROUP * RING))
ITEMS = ROUNDS * GROUP * RING
GROUPS = ITEMS // GROUP
NO_NODE = 4095
BANK = 512
LN_EPS = 1e-5
EXACT = 256
CHUNKS = [(c, min(c + BANK, PADDED)) for c in range(0, PADDED, BANK)]
USED_CHUNKS = [(c, min(c + BANK, NODES)) for c in range(0, NODES, BANK)]


class Chain:

    def __init__(self, engine, semaphore, before=0):
        self.engine, self.semaphore, self.count = engine, semaphore, before

    def __call__(self, instruction):
        instruction.then_inc(self.semaphore, 1)
        self.count += 1
        self.engine.wait_ge(self.semaphore, self.count)

    def overlapped(self, instruction):
        instruction.then_inc(self.semaphore, 1)
        self.count += 1
        self.engine.wait_ge(self.semaphore, self.count - 1)


class Core:

    def __init__(self, nc, ctx, ins, out):
        self.nc, self.ctx, self.ins, self.out = nc, ctx, ins, out
        sb = self.sb
        self.counts = sb("counts", [P, BLOCKS, PADDED], BF16)
        self.mask = self.counts[:, 0:BLOCKS // 2 + 1, :].rearrange("p b s -> p (b s)")\
            [:, 0:BLOCKS * PADDED // 2].bitcast(U8).rearrange("p (b s) -> p b s", b=BLOCKS)
        self.words = sb("item_words", [P, ITEMS], I32)
        self.dloc = sb("item_dst", [P, ITEMS], F32)
        self.block_of = sb("block_of", [1, ITEMS], I32)
        self.bounds = sb("pair_bounds", [1, 32], I32)
        self.x = sb("x_nodes", [P, BLOCKS, D], F32)
        self.ident = sb("ident", [P, P], F32)
        self.ident16 = sb("ident16", [P, P], BF16)
        self.ones = sb("ones", [P, P], F32)
        self.ones16 = sb("ones16", [P, 1], BF16)
        self.iota = sb("iota128", [P, P], F32)
        self.eps = sb("eps", [P, 1], F32)
        self.deg = sb("deg", [P, BLOCKS, len(CHUNKS)], F32)
        self.stat = sb("stat", [P, 4, BLOCKS], F32)
        self.psum = ctx.enter_context(nc.psum_tensor("psum", [P, 8 * BANK], F32))
        self.rounded = sb("counts_rounded", [1, 1], I32)
        self.planes = [nc.dram_tensor(f"counts_{name}", [P, BLOCKS, PADDED], BF16).ap() for name in ("high", "low")]
        self.exchanged, self.exchanges = self.sem("planes_exchanged"), 0
        self.again_step, self.again_steps = self.sem("again_step"), 0
        self.steps = Chain(None, self.sem("vector_steps"))
        self.variances_ready, self.variances_taken = self.sem("variances_ready"), 0
        self.roots_ready, self.roots_taken = self.sem("roots_ready"), 0
        self.banks_turned, self.banks_copied, self.turns = self.sem("banks_turned"), self.sem("banks_copied"), 0

    def sb(self, name, shape, dtype, ctx=None):
        return (ctx or self.ctx).enter_context(self.nc.sbuf_tensor(name, shape, dtype))

    def where_rounded(self, engine):
        rounded = engine.value_load(self.rounded[0:1, 0:1], min_val=0, max_val=P)
        return engine.If(rounded > 0)

    def exchange(self, sp, to, of):
        self.exchanges += 1
        sp.dma_start(to, of).then_inc(self.exchanged, 16)
        sp.wait_ge(self.exchanged, 16 * self.exchanges)

    def over_low_plane(self, sp, finished, count):
        self.exchange(sp, self.counts[:, :, :], self.planes[1])
        sp.wait_ge(finished, count)
        self.exchange(sp, self.counts[:, :, :], self.planes[0])

    def steps_of(self, engine):
        self.steps.engine = engine
        return self.steps

    def tail_views(self, *wanted):
        flat = self.counts[:, :, :].rearrange("p b s -> p (b s)")
        at, views = BLOCKS * PADDED // 2, []
        for shape, dtype in wanted:
            size = int(np.prod(shape[1:]))
            cols = size * {F32: 4, I32: 4, BF16: 2}[dtype] // 2
            view = flat[:, at:at + cols].bitcast(dtype) if dtype is not BF16 else flat[:, at:at + cols]
            at += cols
            letters = "abc"[:len(shape) - 1]
            if len(letters) > 1:
                view = view.rearrange(f"p ({' '.join(letters)}) -> p {' '.join(letters)}",
                                      **dict(zip(letters[:-1], shape[1:-1])))
            views.append(view)
        assert at <= BLOCKS * PADDED
        return views

    def sem(self, name, ctx=None):
        return (ctx or self.ctx).enter_context(self.nc.semaphore(name))

    def bank(self, n, count=1):
        return self.psum[:, n * BANK:(n + count) * BANK]


PLACED = max(k for k in range(1, 9) if BLOCKS % k == 0)


ONE_ITEM = 1024


class Edges:

    def __init__(self, core, sb, sem):
        self.semaphores = [sem(f"e_{n}") for n in ("placed", "step", "reach", "blocks", "inside", "inside_added")]
        self.steps = 0
        counts = core.counts
        self.raw = sb("raw_dst", [P, ONE_ITEM + TILES], I32)
        self.words = self.raw[:, 0:TILES]
        self.item_no = counts[:, 2, 0:2 * ITEMS].bitcast(F32)
        self.item_dst = counts[:, 3, 0:2 * ITEMS].bitcast(I32)
        self.reached = counts[:, 4, 0:2 * ITEMS].bitcast(F32)
        self.item_block = counts[:, 5, 0:2 * ITEMS].bitcast(F32)
        flat = counts[:, 6:9, :].rearrange("p b s -> p (b s)")
        self.item_words = flat[:, 0:2 * (ITEMS + TILES)].bitcast(I32)
        self.scratch = [counts[:, 10 + k, 0:2 * TILES].bitcast(F32) for k in range(6)]
        self.tile_row = sb("tile_row", [1, BLOCKS + 1], I32)
        self.first_item = sb("first_item", [1, BLOCKS + 1], I32)
        self.moves = sb("moves", [1, BLOCKS], I32)
        self.first_col = sb("first_col", [P, 1], F32)
        self.place = sb("place_no", [P, 1], F32)
        self.missing = sb("missing", [1, 1], I32)


def place_edges(core, edges, turn):
    nc = core.nc
    placed, step, reach_ready, blocks_ready, inside_ready, inside_added = edges.semaphores
    as_i16 = lambda ap: ap.bitcast(I16)
    inside = edges.scratch[0][:, 0:2]

    def on_vector(dve):
        chain = Chain(dve, step, turn * edges.steps)
        with dve.Fori(0, BLOCKS // PLACED) as n:
            moves = [dve.value_load(edges.moves[0:1, bass.ds(n * PLACED + k, 1)], min_val=0,
                                    max_val=ITEMS * ONE_ITEM + TILES) for k in range(PLACED)]
            for k, move in enumerate(moves):
                to, of = move // ONE_ITEM, move % ONE_ITEM
                nc.vector.tensor_copy(as_i16(edges.item_words)[:, bass.ds(to * 2, 2 * TILES)],
                                      as_i16(edges.raw[:, :])[:, bass.ds(of * 2, 2 * TILES)]).then_inc(placed, 1)
                dve.wait_ge(placed, n * PLACED + (k + 1 + turn * BLOCKS))
        nc.vector.tensor_scalar(edges.reached[0:BLOCKS - 1, :], edges.item_no[0:BLOCKS - 1, :],
                                edges.first_col[0:BLOCKS - 1, 0:1], None, ALU.is_ge).then_inc(reach_ready, 1)
        words = edges.item_words[:, 0:ITEMS]
        chain(nc.vector.tensor_scalar(core.words[:, :], words, 0xFFFF, None, ALU.bitwise_and))
        chain(nc.vector.tensor_scalar(edges.item_dst, words, 16, None, ALU.logical_shift_right))
        dve.wait_ge(blocks_ready, turn + 1)
        chain(nc.vector.tensor_copy(edges.item_block, core.psum[:, 2 * BANK:2 * BANK + ITEMS]))
        chain(nc.vector.tensor_copy(core.block_of[:, :], edges.item_block[0:1, :]))
        chain(nc.vector.scalar_tensor_tensor(core.dloc[:, :], edges.item_block, float(-P), edges.item_dst,
                                             ALU.mult, ALU.add))
        for n, bound in enumerate((0, P)):
            chain(nc.vector.tensor_scalar(edges.item_block, core.dloc[:, :], float(bound), 0.0,
                                          ALU.is_ge, ALU.add, accum_out=inside[:, n:n + 1]))
        dve.sem_inc(inside_ready, 1)
        dve.wait_ge(inside_added, turn + 1)
        chain(nc.vector.tensor_copy(inside[0:1, :], core.psum[0:1, 0:2]))
        chain(nc.vector.tensor_tensor(inside[0:1, 0:1], inside[0:1, 0:1], inside[0:1, 1:2], ALU.subtract))
        chain(nc.vector.tensor_scalar(inside[0:1, 0:1], inside[0:1, 0:1], -1.0, float(EDGES), ALU.mult, ALU.add))
        chain(nc.vector.tensor_copy(edges.missing[:, :], inside[0:1, 0:1]))
        edges.steps = chain.count

    def on_tensor(pe):
        pe.wait_ge(reach_ready, turn + 1)
        for at in range(0, ITEMS, BANK):
            end = min(at + BANK, ITEMS)
            last = nc.tensor.matmul(core.psum[:, 2 * BANK + at:2 * BANK + end], core.ones[0:BLOCKS - 1, :],
                                    edges.reached[0:BLOCKS - 1, at:end], start=True, stop=True)
        last.then_inc(blocks_ready, 1)
        pe.wait_ge(inside_ready, turn + 1)
        nc.tensor.matmul(core.psum[0:1, 0:2], core.ones[:, 0:1], inside, start=True, stop=True)\
          .then_inc(inside_added, 1)

    return on_vector, on_tensor


def prepare(core):
    nc, ins = core.nc, core.ins
    with ExitStack() as stage:
        sb = lambda *a: core.sb(*a, stage)
        sem = lambda n: core.sem(n, stage)
        edges = Edges(core, sb, sem)
        raw_src, raw_rel = (sb(n, [P, TILES], I32) for n in ("raw_src", "raw_rel"))
        block_i = core.counts[:, 0, 0:2 * TILES].bitcast(I32)
        block_of_edge = core.counts[:, 9, 0:TILES]
        below = core.counts[:, 1, 0:TILES]
        starts = sb("starts", [P, BLOCKS - 1], F32)
        even_row, ones_row = sb("even_row", [1, BLOCKS], I32), sb("ones_row", [1, BLOCKS], F32)
        first_row = sb("first_row", [1, BLOCKS + 1], F32)
        tile_row, first_item = edges.tile_row, edges.first_item
        loaded, constant = sem("p_loaded"), sem("p_constant")
        counted, summed, firsts_ready, turned = sem("p_counted"), sem("p_summed"), sem("p_firsts"), sem("p_turned")
        place_on_vector, place_on_tensor = place_edges(core, edges, 0)
        with nc.Block() as block:
            @block.sync
            def _(sp):
                sp.dma_start(edges.words, ins["dst"]).then_inc(loaded, 16)
                sp.dma_start(raw_src[:, :], ins["src"]).then_inc(loaded, 16)
                sp.dma_start(raw_rel[:, :], ins["rel"]).then_inc(loaded, 16)
                sp.dma_start(core.x[:, :, :], ins["x"]).then_inc(loaded, 16)
                sp.wait_ge(loaded, 64)

            @block.gpsimd
            def _(pool):
                chain = Chain(pool, constant)
                chain(pool.memset(core.ident[:, :], 0.0))
                chain(pool.affine_select(out=core.ident[:, :], in_=core.ident[:, :], compare_op=ALU.not_equal,
                                         fill=1.0, base=0, pattern=[[-1, P]], channel_multiplier=1))
                pool.tensor_copy(core.ident16[:, :], core.ident[:, :]).then_inc(constant, 1)
                pool.memset(core.ones[:, :], 1.0).then_inc(constant, 1)
                pool.memset(core.ones16[:, :], 1.0).then_inc(constant, 1)
                pool.memset(core.eps[:, :], LN_EPS).then_inc(constant, 1)
                pool.memset(ones_row[:, :], 1.0).then_inc(constant, 1)
                for tile, pattern, down in ((core.iota[:, :], [[1, P]], 0), (edges.item_no, [[1, ITEMS]], 0),
                                            (edges.place[:, :], [[0, 1]], 1)):
                    pool.iota(tile, pattern, base=0, channel_multiplier=down,
                              allow_small_or_imprecise_dtypes=True).then_inc(constant, 1)
                pool.memset(edges.raw[:, TILES:], NO_NODE << 16).then_inc(constant, 1)
                pool.memset(edges.item_words, NO_NODE << 16).then_inc(constant, 1)

            @block.vector
            def _(dve):
                chain = core.steps_of(dve)
                dve.wait_ge(loaded, 64)
                dve.wait_ge(constant, 12)
                chain(nc.vector.tensor_scalar(block_i, edges.words, 7, None, ALU.arith_shift_right))
                chain(nc.vector.tensor_copy(block_of_edge, block_i))
                for k in range(BLOCKS - 1):
                    chain(nc.vector.tensor_scalar(below, block_of_edge, float(k), 0.0, ALU.is_le, ALU.add,
                                                  accum_out=starts[:, k:k + 1]))
                nc.vector.memset(tile_row[:, 0:1], 0).then_inc(counted, 1)
                chain(nc.vector.scalar_tensor_tensor(raw_src[:, :], raw_src[:, :], float(RELATIONS), raw_rel[:, :],
                                                     ALU.mult, ALU.add))
                chain(nc.vector.tensor_scalar(edges.words, edges.words, 16, None, ALU.logical_shift_left))
                chain(nc.vector.tensor_tensor(edges.words, edges.words, raw_src[:, :], ALU.bitwise_or))
                dve.wait_ge(summed, 1)
                chain(nc.vector.tensor_copy(tile_row[:, 1:BLOCKS], core.psum[0:1, 0:BLOCKS - 1]))
                chain(nc.vector.tensor_scalar(tile_row[:, 1:BLOCKS], tile_row[:, 1:BLOCKS], 7, None,
                                              ALU.arith_shift_right))
                chain(nc.vector.memset(tile_row[:, BLOCKS:BLOCKS + 1], TILES - 1))
                chain(nc.vector.scalar_tensor_tensor(even_row[:, :], tile_row[:, 1:BLOCKS + 1], 2.0,
                                                     tile_row[:, 0:BLOCKS], ALU.add, ALU.subtract))
                chain(nc.vector.tensor_scalar(even_row[:, :], even_row[:, :], -2, None, ALU.bitwise_and))
                chain(nc.vector.memset(first_row[:, 0:1], 0.0))
                chain(nc.vector.tensor_tensor_scan(first_row[:, 1:BLOCKS + 1], ones_row[:, :], even_row[:, :], 0.0,
                                                   ALU.mult, ALU.add))
                nc.vector.tensor_copy(first_item[:, :], first_row[:, :]).then_inc(firsts_ready, 1)
                dve.wait_ge(firsts_ready, 1)
                chain(nc.vector.tensor_scalar(core.bounds[:, 0:BLOCKS], first_item[:, 0:BLOCKS], 1, None,
                                              ALU.arith_shift_right))
                chain(nc.vector.memset(core.bounds[:, BLOCKS:BLOCKS + 1], PAIRS))
                chain(nc.vector.scalar_tensor_tensor(edges.moves[:, :], first_item[:, 0:BLOCKS], float(ONE_ITEM),
                                                     tile_row[:, 0:BLOCKS], ALU.mult, ALU.add))
                dve.wait_ge(turned, 1)
                chain(nc.vector.tensor_copy(edges.first_col[0:BLOCKS - 1, :], core.psum[0:BLOCKS - 1, BANK:BANK + 1]))
                place_on_vector(dve)

            @block.tensor
            def _(pe):
                pe.wait_ge(constant, 12)
                pe.wait_ge(counted, 1)
                nc.tensor.matmul(core.psum[0:1, 0:BLOCKS - 1], core.ones[:, 0:1], starts[:, :],
                                 start=True, stop=True).then_inc(summed, 1)
                pe.wait_ge(firsts_ready, 1)
                nc.tensor.matmul(core.psum[0:BLOCKS - 1, BANK:BANK + 1], first_row[:, 1:BLOCKS], core.ones[0:1, 0:1],
                                 start=True, stop=True).then_inc(turned, 1)
                place_on_tensor(pe)
        order_by_block(core, edges)


SCATTERS = max(k for k in range(1, 17) if TILES % k == 0)


def order_by_block(core, edges):
    nc = core.nc
    with ExitStack() as stage:
        sem = lambda n: core.sem(f"o_{n}", stage)
        block_of_edge, in_block, rank, places, ones, spare = edges.scratch
        addresses, tile_of = spare.bitcast(I32), rank.bitcast(I32)
        before = core.counts[:, 9, 0:2 * P].bitcast(F32)
        total, base = core.sb("o_total", [P, 1], F32, stage), core.sb("o_base", [P, 1], F32, stage)
        staged_words = core.sb("o_words", [P, SCATTERS], I32, stage)
        staged_at = core.sb("o_at", [P, SCATTERS], I32, stage)
        ordered = nc.dram_tensor("ordered_edges", [P * TILES, 1], I32).ap()
        step, rank_step, totals_ready, prefix_ready = sem("step"), sem("rank_step"), sem("totals"), sem("prefix")
        places_ready, staged, started, scattered, reloaded = (sem(n) for n in (
            "places", "staged", "started", "scattered", "reloaded"))
        place_on_vector, place_on_tensor = place_edges(core, edges, 1)
        STEPS = 7
        with nc.Block() as block:
            @block.vector
            def _(dve):
                missing = dve.value_load(edges.missing[0:1, 0:1], min_val=0, max_val=EDGES)
                with dve.If(missing > 0):
                    chain = Chain(dve, step)
                    chain(nc.vector.tensor_scalar(tile_of, edges.words, 16 + 7, None, ALU.logical_shift_right))
                    chain(nc.vector.tensor_scalar(block_of_edge, tile_of, float(BLOCKS), None, ALU.min))
                    chain(nc.vector.tensor_scalar(before, core.iota[:, :], edges.place[:, 0:1], None, ALU.is_gt))
                    chain(nc.vector.memset(ones, 1.0))
                    chain(nc.vector.memset(places, 0.0))
                    chain(nc.vector.memset(base[:, :], -1.0))
                    with dve.Fori(0, BLOCKS + 1) as b:
                        turn = Chain(dve, rank_step, b * STEPS)
                        turn(nc.vector.tensor_scalar(in_block, block_of_edge, core.iota[:, bass.ds(b, 1)], None,
                                                     ALU.is_equal))
                        turn(nc.vector.tensor_tensor_scan(rank, ones, in_block, 0.0, ALU.mult, ALU.add))
                        nc.vector.tensor_copy(total[:, :], rank[:, TILES - 1:TILES]).then_inc(totals_ready, 1)
                        dve.wait_ge(prefix_ready, b + 1)
                        turn(nc.vector.tensor_tensor(total[:, :], core.psum[:, 0:1], base[:, :], ALU.add))
                        turn(nc.vector.tensor_tensor(base[:, :], core.psum[:, BANK:BANK + 1], base[:, :], ALU.add))
                        turn(nc.vector.tensor_scalar(rank, rank, total[:, 0:1], None, ALU.add))
                        turn(nc.vector.tensor_tensor(rank, rank, in_block, ALU.mult))
                        turn(nc.vector.tensor_tensor(places, places, rank, ALU.add))
                    chain(nc.vector.tensor_copy(addresses, places))
                    chain(nc.vector.tensor_scalar(tile_of, addresses, 7, None, ALU.logical_shift_right))
                    chain(nc.vector.tensor_scalar(addresses, addresses, P - 1, None, ALU.bitwise_and))
                    nc.vector.scalar_tensor_tensor(addresses, addresses, float(TILES), tile_of,
                                                   ALU.mult, ALU.add).then_inc(places_ready, 1)
                    dve.wait_ge(reloaded, 16)
                    place_on_vector(dve)

            @block.tensor
            def _(pe):
                missing = pe.value_load(edges.missing[0:1, 0:1], min_val=0, max_val=EDGES)
                with pe.If(missing > 0):
                    with pe.Fori(0, BLOCKS + 1) as b:
                        pe.wait_ge(totals_ready, b + 1)
                        nc.tensor.matmul(core.psum[:, 0:1], before, total[:, :], start=True, stop=True)
                        nc.tensor.matmul(core.psum[:, BANK:BANK + 1], core.ones[:, :], total[:, :],
                                         start=True, stop=True).then_inc(prefix_ready, 1)
                    place_on_tensor(pe)

            @block.gpsimd
            def _(pool):
                missing = pool.value_load(edges.missing[0:1, 0:1], min_val=0, max_val=EDGES)
                with pool.If(missing > 0):
                    pool.wait_ge(places_ready, 1)
                    with pool.Fori(0, TILES // SCATTERS) as n:
                        for to, of in ((staged_words, edges.words), (staged_at, addresses)):
                            nc.gpsimd.tensor_copy(to[:, :].bitcast(I16),
                                                  of.bitcast(I16)[:, bass.ds(n * 2 * SCATTERS, 2 * SCATTERS)])\
                              .then_inc(staged, 1)
                        pool.wait_ge(staged, n * 2 + 2)
                        pool.sem_inc(started, 1)
                        for k in range(SCATTERS):
                            nc.gpsimd.indirect_dma_start(
                                out=ordered, out_offset=bass.IndirectOffsetOnAxis(ap=staged_at[:, k:k + 1], axis=0),
                                in_=staged_words[:, k:k + 1], in_offset=None).then_inc(scattered, 16)
                        pool.wait_ge(scattered, (n + 1) * (16 * SCATTERS))

            @block.sync
            def _(sp):
                missing = sp.value_load(edges.missing[0:1, 0:1], min_val=0, max_val=EDGES)
                with sp.If(missing > 0):
                    sp.wait_ge(scattered, 16 * TILES)
                    sp.dma_start(edges.words, ordered.rearrange("(p t) c -> p (t c)", p=P)).then_inc(reloaded, 16)
                    sp.wait_ge(reloaded, 16)


HOT_SPLIT = 4
HOT_PARTS = [(0, CHUNKS[HOT_SPLIT][0]), (CHUNKS[HOT_SPLIT][0], PADDED)]


def count_edges(core):
    nc = core.nc
    with ExitStack() as stage:
        sb = lambda *a: core.sb(*a, stage)
        sem = lambda n: core.sem(n, stage)
        source_no = sb("source_no", [P, PADDED], I16)
        source = sb("item_source", [P, ITEMS], F32)
        src_hot = sb("src_hot", [P, 2, PADDED], BF16)
        dst_hot = sb("dst_hot", [P, 2, P], BF16)
        zeros = sb("zeros16", [P, BANK], BF16)
        above = sb("above", [P, PADDED], BF16)
        aboves = sb("aboves", [P, BLOCKS], F32)
        allowed, high = sb("allowed", [P, 1], F32), sb("high", [P, 1], F32)
        warm, warmed = sb("warm", [P, 1], F32), sem("c_warmed")
        iota_ready, source_ready = sem("c_iota"), sem("c_source")
        zeros_ready, allowed_ready, aboves_ready = sem("c_zeros"), sem("c_allowed"), sem("c_aboves")
        high_ready, high_summed = sem("c_high"), sem("c_high_summed")
        hots_ready, items_added = sem("c_hots"), sem("c_added")
        stored = [sem("c_stored_even"), sem("c_stored_odd")]
        shared = [CHUNKS[0::2], CHUNKS[1::2]]
        flat = lambda ap: ap.rearrange("p b s -> p (b s)")

        def counts_of(b, n):
            lo, hi = CHUNKS[n]
            return (flat(core.counts[:, bass.ds(b, 1), lo:hi]), core.psum[:, lo:hi],
                    flat(core.deg[:, bass.ds(b, 1), n:n + 1]))

        def count(low):
            hots_before, added_before = (4 * PAIRS + 4, 4 * PAIRS) if low else (0, 0)
            stored_before = [BLOCKS * len(share) if low else 0 for share in shared]
            branch = core.where_rounded if low else lambda engine: nullcontext()
            with nc.Block() as block:
                @block.gpsimd
                def _(pool):
                    if low:
                        return
                    pool.iota(source_no[:, :], [[1, PADDED]], base=0, channel_multiplier=0).then_inc(iota_ready, 1)
                    pool.memset(zeros[:, :], 0.0).then_inc(zeros_ready, 1)
                    pool.memset(allowed[:, :], -(EXACT - 1.0)).then_inc(allowed_ready, 1)

                @block.sync
                def _(sp):
                    if low:
                        with branch(sp):
                            core.exchange(sp, core.planes[0], core.counts[:, :, :])
                            for which, share in enumerate(shared):
                                sp.wait_ge(stored[which], 2 * BLOCKS * len(share))
                            core.exchange(sp, core.planes[1], core.counts[:, :, :])
                            core.exchange(sp, core.counts[:, :, :], core.planes[0])

                @block.vector
                def _(dve):
                    def one_hots(slot, w, last=None):
                        col = slice(w, w + 1) if isinstance(w, int) else bass.ds(w, 1)
                        for part, (lo, hi) in enumerate(HOT_PARTS):
                            if last is not None and part == 0:
                                dve.wait_ge(items_added, last * 2 + (1 + added_before))
                            made = nc.vector.tensor_scalar(src_hot[:, slot, lo:hi], source_no[:, lo:hi],
                                                           source[:, col], None, ALU.is_equal)
                            if part == 0:
                                if last is not None:
                                    dve.wait_ge(items_added, last * 2 + (2 + added_before))
                                made = nc.vector.tensor_scalar(dst_hot[:, slot, :], core.iota[:, :],
                                                               core.dloc[:, col], None, ALU.is_equal)
                            made.then_inc(hots_ready, 1)

                    def store(b, n):
                        to, bank, degrees = counts_of(b, n)
                        if low:
                            nc.vector.tensor_reduce(degrees, bank, AX.X, ALU.add)
                            nc.vector.tensor_tensor(to, bank, to, ALU.subtract).then_inc(stored[n % 2], 1)
                        else:
                            nc.vector.tensor_scalar(to, bank, 1.0, 0.0, ALU.mult, ALU.add,
                                                    accum_out=degrees).then_inc(stored[1], 1)

                    with branch(dve):
                        if low:
                            dve.wait_ge(core.exchanged, 16)
                        else:
                            words = source[:, :].bitcast(I32)
                            chain = Chain(dve, source_ready)
                            chain(nc.vector.tensor_scalar(words, core.words[:, :], 4, None, ALU.logical_shift_right))
                            chain(nc.vector.tensor_copy(source[:, :], words))
                            dve.wait_ge(iota_ready, 1)
                        one_hots(0, 0)
                        one_hots(1, 1)
                        with dve.Fori(0, BLOCKS) as b:
                            first = dve.value_load(core.bounds[0:1, bass.ds(b, 1)], min_val=0, max_val=PAIRS - 1)
                            end = dve.value_load(core.bounds[0:1, bass.ds(b + 1, 1)], min_val=1, max_val=PAIRS)
                            with dve.Fori(first, end) as last_pair:
                                for slot in range(2):
                                    one_hots(slot, last_pair * 2 + (slot + 2), last_pair * 2 + slot)
                            dve.wait_ge(items_added, end * 4 + added_before)
                            for n in range(len(CHUNKS)) if low else range(1, len(CHUNKS), 2):
                                store(b, n)
                        if not low:
                            chain = core.steps_of(dve)
                            dve.wait_ge(aboves_ready, BLOCKS)
                            chain(nc.vector.tensor_reduce(high[:, :], aboves[:, :], AX.X, ALU.max))
                            nc.vector.tensor_scalar(high[:, :], high[:, :], 0.0, None, ALU.is_gt)\
                              .then_inc(high_ready, 1)
                            dve.wait_ge(high_summed, 1)
                            chain(nc.vector.tensor_copy(core.rounded[:, :], core.bank(7)[0:1, 0:1]))

                @block.tensor
                def _(pe):
                    def block_counts(b):
                        first = pe.value_load(core.bounds[0:1, bass.ds(b, 1)], min_val=0, max_val=PAIRS - 1)
                        end = pe.value_load(core.bounds[0:1, bass.ds(b + 1, 1)], min_val=1, max_val=PAIRS)
                        for n, (lo, hi) in enumerate(CHUNKS):
                            if not isinstance(b, int):
                                share = len(shared[n % 2])
                                pe.wait_ge(stored[n % 2], b * share + (stored_before[n % 2] - (share - 1 - n // 2)))
                            nc.tensor.matmul(core.psum[:, lo:hi], zeros[:, 0:P], zeros[:, 0:hi - lo],
                                             start=True, stop=True, skip_group_check=True)
                        with pe.Fori(first, end) as pair:
                            for slot in range(2):
                                for part, chunks in enumerate((USED_CHUNKS[:HOT_SPLIT], USED_CHUNKS[HOT_SPLIT:])):
                                    pe.wait_ge(hots_ready, pair * 4 + (2 * slot + part + 1 + hots_before))
                                    for lo, hi in chunks:
                                        last = nc.tensor.matmul(core.psum[:, lo:hi], dst_hot[:, slot, :],
                                                                src_hot[:, slot, lo:hi],
                                                                start=False, stop=True, skip_group_check=True)
                                    last.then_inc(items_added, 1)

                    with branch(pe):
                        pe.wait_ge(zeros_ready, 1)
                        block_counts(0)
                        with pe.Fori(1, BLOCKS) as b:
                            block_counts(b)
                        if not low:
                            pe.wait_ge(high_ready, 1)
                            nc.tensor.matmul(core.bank(7)[0:1, 0:1], core.ones[:, 0:1], high[:, :],
                                             start=True, stop=True).then_inc(high_summed, 1)

                @block.scalar
                def _(act):
                    if low:
                        return
                    nc.scalar.activation(warm[:, :], core.ones[:, 0:1], ACT.Copy).then_inc(warmed, 1)
                    act.wait_ge(warmed, 1)
                    act.wait_ge(allowed_ready, 1)
                    with act.Fori(0, BLOCKS) as b:
                        end = act.value_load(core.bounds[0:1, bass.ds(b + 1, 1)], min_val=1, max_val=PAIRS)
                        act.wait_ge(items_added, end * 4)
                        for n in range(0, len(CHUNKS), 2):
                            to, bank, degrees = counts_of(b, n)
                            nc.scalar.activation(to, bank, ACT.Copy, accum_out=degrees).then_inc(stored[0], 1)
                        for which, share in enumerate(shared):
                            act.wait_ge(stored[which], b * len(share) + len(share))
                        nc.scalar.activation(above[:, :], flat(core.counts[:, bass.ds(b, 1), :]), ACT.Relu,
                                             bias=allowed[:, 0:1], accum_out=aboves[:, bass.ds(b, 1)])\
                          .then_inc(aboves_ready, 1)
                        act.wait_ge(aboves_ready, b + 1)

        count(low=False)
        count(low=True)


def transposed_nodes(core, src, width, dst):
    nc = core.nc
    before = core.turns * len(CHUNKS)
    core.turns += 1

    def on_tensor(pe):
        for b in range(BLOCKS):
            last = nc.tensor.transpose(core.psum[0:width, b * P:(b + 1) * P], src[:, b, :], core.ident[:, :])
            if b % 4 == 3 or b == BLOCKS - 1:
                last.then_inc(core.banks_turned, 1)

    def on_scalar(act):
        for n, (lo, hi) in enumerate(CHUNKS):
            act.wait_ge(core.banks_turned, before + n + 1)
            nc.scalar.activation(dst[0:width, lo:hi], core.psum[0:width, lo:hi], ACT.Copy)\
              .then_inc(core.banks_copied, 1)

    return on_tensor, on_scalar, before + len(CHUNKS)


def layernorm(core, chain, x, work, stat):
    nc = core.nc
    total, var = stat[:, 0, :], stat[:, 1, :]
    width = x.shape[2]
    chain(nc.vector.tensor_reduce(total, x, AX.X, ALU.add))
    chain(nc.vector.tensor_scalar(total, total, 1.0 / width, None, ALU.mult))
    chain(nc.vector.tensor_tensor(x, x, total.unsqueeze(2).to_broadcast(x.shape), ALU.subtract))
    chain(nc.vector.tensor_tensor(work, x, x, ALU.mult))
    nc.vector.tensor_reduce(var, work, AX.X, ALU.add).then_inc(core.variances_ready, 1)
    core.roots_taken += 1
    chain.engine.wait_ge(core.roots_ready, core.roots_taken)
    chain(nc.vector.reciprocal(total, stat[:, 2, :]))
    chain(nc.vector.tensor_tensor(x, x, total.unsqueeze(2).to_broadcast(x.shape), ALU.mult))


def layernorm_root(core, act, stat, width):
    core.variances_taken += 1
    act.wait_ge(core.variances_ready, core.variances_taken)
    core.nc.scalar.activation(stat[:, 2, :], stat[:, 1, :], ACT.Sqrt, bias=core.eps[:, 0:1],
                              scale=1.0 / width).then_inc(core.roots_ready, 1)


def split_parts(nc, chain, value, parts):
    hi, mid, lo = (parts[:, :, k * D:(k + 1) * D] for k in range(3))
    chain(nc.vector.tensor_copy(hi, value))
    chain(nc.vector.tensor_tensor(value, value, hi, ALU.subtract))
    chain(nc.vector.tensor_copy(mid, value))
    chain(nc.vector.tensor_tensor(lo, value, mid, ALU.subtract))


def add_parts(core, dve, to, sums, extra, stored, free, done, low):
    nc = core.nc
    by_part = sums.rearrange("p (k f) -> p f k", k=3)
    if not low:
        nc.vector.tensor_reduce(to, by_part, AX.X, ALU.add).then_inc(stored, 1)
        return
    dve.wait_ge(stored, done + (free + BLOCKS))
    nc.vector.tensor_reduce(extra[:, :], by_part, AX.X, ALU.add).then_inc(core.again_step, 1)
    dve.wait_ge(core.again_step, done + (core.again_steps + 1))
    nc.vector.tensor_tensor(to, to, extra[:, :].unsqueeze(1), ALU.add).then_inc(stored, 1)


def bilinear_layer(core):
    nc, ins = core.nc, core.ins
    with ExitStack() as stage:
        sb = lambda *a: core.sb(*a, stage)
        sem = lambda n: core.sem(n, stage)
        stack = sb("b_stack", [P, BLOCKS, 2 * D], F32)
        wide = sb("b_wide", [P, PADDED], F32)
        parts = wide[:, 0:BLOCKS * 3 * D // 2].bitcast(BF16).rearrange("p (b k) -> p b k", b=BLOCKS)
        turned = sb("b_turned", [P, BLOCKS, P], BF16)
        weights = sb("b_weights", [P, D], F32)
        bias = sb("b_bias", [P, 2, D], F32)
        norm = core.stat[:, 3, :]
        loaded, root_of, rooted = sem("b_loaded"), sem("b_rootof"), sem("b_rooted")
        parts_ready, turned_in_psum, turned_ready = sem("b_parts"), sem("b_tpsum"), [sem("b_turned0"), sem("b_turned1")]
        turned_used, sums_stored = sem("b_used"), sem("b_sumstored")
        stack_ready, products = sem("b_stack_s"), sem("b_prod")
        groups = [range(0, 7), range(7, 13), range(13, 19), range(19, 25)]
        turned_psum = [core.bank(k).bitcast(BF16).rearrange("p (t d) -> p t d", d=P) for k in (0, 1, 3, 4)]
        sums = core.bank(2)[:, 0:3 * D]
        on_tensor, on_scalar, all_copied = transposed_nodes(core, stack, P, wide)
        value = stack[:, :, 0:D]
        per_node = norm.unsqueeze(2).to_broadcast([P, BLOCKS, D])
        extra = wide[:, BLOCKS * 3 * D // 2:BLOCKS * 3 * D // 2 + D]
        low_plane_in = 16 * (core.exchanges + 1)

        def out_of_psum(engine, b, n, before):
            engine.wait_ge(turned_in_psum, b * 4 + (n + 1 + before))
            engine.wait_ge(turned_used, b * 4 + (n + 1 + before))
            return turned[:, groups[n][0]:groups[n][-1] + 1, :], turned_psum[n][:, 0:len(groups[n]), :]

        def sum_on_vector(dve, low=False):
            before = 4 * BLOCKS if low else 0
            with dve.Fori(0, BLOCKS) as b:
                for n in (1, 3):
                    nc.vector.tensor_copy(*out_of_psum(dve, b, n, before)).then_inc(turned_ready[1], 1)
                dve.wait_ge(turned_used, b * 4 + (8 + before))
                add_parts(core, dve, stack[:, bass.ds(b, 1), 0:D], sums, extra, sums_stored, 1, b, low)

        def sum_on_scalar(act, low=False):
            before = 4 * BLOCKS if low else 0
            with act.Fori(0, BLOCKS) as b:
                for n in (0, 2):
                    nc.scalar.activation(*out_of_psum(act, b, n, before), ACT.Copy).then_inc(turned_ready[0], 1)

        def sum_on_tensor(pe, low=False):
            before = BLOCKS if low else 0

            def turn(b, n):
                for t, j in enumerate(groups[n]):
                    last = nc.tensor.transpose(turned_psum[n][:, t, :],
                                               core.counts[:, bass.ds(b, 1), j * P:(j + 1) * P],
                                               core.ident16[:, :])
                last.then_inc(turned_in_psum, 1)

            def block_sums(b, following):
                pe.wait_ge(sums_stored, b + (1 + before))
                for n, group in enumerate(groups):
                    pe.wait_ge(turned_ready[n % 2], b * 2 + (n // 2 + 1 + 2 * before))
                    for j in group:
                        last = nc.tensor.matmul(sums, turned[:, j, :], parts[:, j, :],
                                                start=(j == 0), stop=(j == BLOCKS - 1))
                    last.then_inc(turned_used, 1)
                    if following:
                        turn(b + 1, n)

            for n in range(len(groups)):
                turn(0, n)
            with pe.Fori(0, BLOCKS - 1) as b:
                block_sums(b, following=True)
            block_sums(BLOCKS - 1, following=False)

        with nc.Block() as block:
            @block.sync
            def _(sp):
                sp.dma_start(weights[0:D, :], ins["w_f"]).then_inc(loaded, 16)
                sp.dma_start(weights[D:P, :], ins["w_xf"]).then_inc(loaded, 16)
                for k, name in enumerate(("b_f", "b_xf")):
                    sp.dma_start(bias[:, k, :], ins[name].to_broadcast([P, D])).then_inc(loaded, 16)

            @block.vector
            def _(dve):
                chain = core.steps_of(dve)
                dve.sem_inc(sums_stored, 1)
                chain(nc.vector.tensor_reduce(norm, core.deg[:, :, :], AX.X, ALU.add))
                nc.vector.tensor_scalar(norm, norm, 1.0, None, ALU.max).then_inc(root_of, 1)
                dve.wait_ge(rooted, 1)
                chain(nc.vector.reciprocal(norm, core.stat[:, 2, :]))
                chain(nc.vector.tensor_tensor(value, core.x[:, :, :], per_node, ALU.mult))
                split_parts(nc, chain, value, parts)
                nc.vector.memset(core.stat[:, 0, :], 0.0).then_inc(parts_ready, 1)
                sum_on_vector(dve)

            @block.scalar
            def _(act):
                act.wait_ge(root_of, 1)
                nc.scalar.activation(core.stat[:, 2, :], norm, ACT.Sqrt).then_inc(rooted, 1)
                sum_on_scalar(act)

            @block.tensor
            def _(pe):
                pe.sem_inc(turned_used, 4)
                pe.wait_ge(parts_ready, 1)
                sum_on_tensor(pe)
        with nc.Block() as block:
            @block.sync
            def _(sp):
                with core.where_rounded(sp):
                    core.over_low_plane(sp, sums_stored, 2 * BLOCKS + 1)

            @block.vector
            def _(dve):
                with core.where_rounded(dve):
                    sum_on_vector(dve, low=True)
                    core.again_steps += BLOCKS

            @block.scalar
            def _(act):
                with core.where_rounded(act):
                    sum_on_scalar(act, low=True)

            @block.tensor
            def _(pe):
                with core.where_rounded(pe):
                    pe.wait_ge(core.exchanged, low_plane_in)
                    sum_on_tensor(pe, low=True)
        with nc.Block() as block:
            @block.vector
            def _(dve):
                chain = core.steps_of(dve)
                chain(nc.vector.tensor_tensor(value, value, per_node, ALU.mult))
                nc.vector.tensor_tensor(stack[:, :, D:2 * D], value, core.x[:, :, :], ALU.mult).then_inc(stack_ready, 1)
                dve.wait_ge(loaded, 64)
                chain(nc.vector.tensor_tensor(bias[:, 0, :], bias[:, 0, :], bias[:, 1, :], ALU.add))
                chain(nc.vector.tensor_tensor(core.x[:, :, :], core.x[:, :, :],
                                              bias[:, 0:1, :].to_broadcast([P, BLOCKS, D]), ALU.add))
                dve.wait_ge(products, 1)
                chain(nc.vector.tensor_tensor(core.x[:, :, :], core.x[:, :, :],
                                              core.psum[:, 0:BLOCKS * D].rearrange("p (b f) -> p b f", f=D), ALU.add))
                layernorm(core, chain, core.x[:, :, :], stack[:, :, 0:D], core.stat)

            @block.scalar
            def _(act):
                on_scalar(act)
                layernorm_root(core, act, core.stat, D)

            @block.tensor
            def _(pe):
                pe.wait_ge(stack_ready, 1)
                on_tensor(pe)
                pe.wait_ge(core.banks_copied, all_copied)
                pe.wait_ge(loaded, 64)
                for b in range(BLOCKS):
                    last = nc.tensor.matmul(core.psum[:, b * D:(b + 1) * D], wide[:, b * P:(b + 1) * P],
                                            weights[:, :], start=True, stop=True)
                last.then_inc(products, 1)


def interaction_layer(core):
    nc, ins = core.nc, core.ins
    with ExitStack() as stage:
        sb = lambda *a: core.sb(*a, stage)
        sem = lambda n: core.sem(n, stage)
        stack = sb("i_stack", [P, BLOCKS, 2 * D], F32)
        wide = sb("i_wide", [P, PADDED], F32)
        parts = wide[:, 0:BLOCKS * 3 * D // 2].bitcast(BF16).rearrange("p (b k) -> p b k", b=BLOCKS)
        weights = sb("i_weights", [P, 2 * D], F32)
        bias = sb("i_bias", [P, 1, 2 * D], F32)
        norm, root = core.stat[:, 3, :], core.stat[:, 2, :]
        has_edges = core.stat[:, 0, :]
        loaded, cleared = sem("i_loaded"), sem("i_cleared")
        degrees, root_of, rooted = sem("i_degrees"), sem("i_rootof"), sem("i_rooted")
        column_sums, row_ready = sem("i_columns"), sem("i_row")
        degree_row = wide[0:1, :]
        norm_of, normed = sem("i_normof"), sem("i_normed")
        parts_ready, sums_ready, sums_stored = sem("i_parts"), sem("i_sums"), sem("i_stored")
        stack_ready, products = sem("i_stack_s"), sem("i_prod")
        sums = [core.bank(k)[:, 0:3 * D] for k in (0, 1)]
        on_tensor, on_scalar, all_copied = transposed_nodes(core, stack, P, wide)
        value = stack[:, :, 0:D]
        per_node = norm.unsqueeze(2).to_broadcast([P, BLOCKS, D])
        extra = sb("i_extra", [P, D], F32)
        low_plane_in = 16 * (core.exchanges + 1)

        def column_sums_on_tensor(pe):
            for lo, hi in CHUNKS:
                for b in range(BLOCKS):
                    last = nc.tensor.matmul(core.psum[0:1, lo:hi], core.ones16[:, :], core.counts[:, b, lo:hi],
                                            start=(b == 0), stop=(b == BLOCKS - 1))
                last.then_inc(column_sums, 1)

        def sum_on_tensor(pe, low=False):
            before = BLOCKS if low else 0

            def gather_sources(j, slot, turn):
                pe.wait_ge(sums_stored, turn + before)
                for b in range(BLOCKS):
                    last = nc.tensor.matmul(sums[slot], core.counts[:, b, bass.ds(j * P, P)], parts[:, b, :],
                                            start=(b == 0), stop=(b == BLOCKS - 1))
                last.then_inc(sums_ready, 1)

            with pe.Fori(0, BLOCKS // 2) as pair:
                for slot in range(2):
                    gather_sources(pair * 2 + slot, slot, pair * 2 + (slot + 1))
            gather_sources(BLOCKS - 1, 0, BLOCKS)

        def sum_on_vector(dve, low=False):
            before = BLOCKS if low else 0

            def store(j, slot, turn):
                dve.wait_ge(sums_ready, turn + before)
                add_parts(core, dve, stack[:, bass.ds(j, 1), 0:D], sums[slot], extra, sums_stored, 2, j, low)

            with dve.Fori(0, BLOCKS // 2) as pair:
                for slot in range(2):
                    store(pair * 2 + slot, slot, pair * 2 + (slot + 1))
            store(BLOCKS - 1, 0, BLOCKS)

        with nc.Block() as block:
            @block.gpsimd
            def _(pool):
                pool.memset(weights[:, :], 0.0).then_inc(cleared, 1)

            @block.sync
            def _(sp):
                sp.wait_ge(cleared, 1)
                sp.dma_start(weights[0:D, 0:D], ins["w_gcn"]).then_inc(loaded, 16)
                sp.dma_start(weights[D:P, D:2 * D], ins["w_int"]).then_inc(loaded, 16)
                sp.dma_start(bias[:, 0, 0:D], ins["b_gcn"].to_broadcast([P, D])).then_inc(loaded, 16)
                sp.dma_start(bias[:, 0, D:2 * D], ins["b_int"].to_broadcast([P, D])).then_inc(loaded, 16)

            @block.tensor
            def _(pe):
                column_sums_on_tensor(pe)

            @block.scalar
            def _(act):
                for n, (lo, hi) in enumerate(CHUNKS):
                    act.wait_ge(column_sums, n + 1)
                    nc.scalar.activation(degree_row[0:1, lo:hi], core.psum[0:1, lo:hi], ACT.Copy)\
                      .then_inc(row_ready, 1)
        with nc.Block() as block:
            @block.sync
            def _(sp):
                with core.where_rounded(sp):
                    core.over_low_plane(sp, row_ready, 2 * len(CHUNKS))

            @block.tensor
            def _(pe):
                with core.where_rounded(pe):
                    pe.wait_ge(core.exchanged, low_plane_in)
                    column_sums_on_tensor(pe)

            @block.vector
            def _(dve):
                with core.where_rounded(dve):
                    for n, (lo, hi) in enumerate(CHUNKS):
                        dve.wait_ge(column_sums, len(CHUNKS) + n + 1)
                        nc.vector.tensor_tensor(degree_row[0:1, lo:hi], degree_row[0:1, lo:hi],
                                                core.psum[0:1, lo:hi], ALU.add).then_inc(row_ready, 1)
        low_plane_in_again = 16 * (core.exchanges + 1)
        with nc.Block() as block:
            @block.tensor
            def _(pe):
                for b in range(BLOCKS):
                    last = nc.tensor.matmul(core.bank(7)[:, b:b + 1], degree_row[0:1, b * P:(b + 1) * P],
                                            core.ones[0:1, 0:1], start=True, stop=True)
                last.then_inc(degrees, 1)
                pe.wait_ge(parts_ready, 1)
                sum_on_tensor(pe)

            @block.scalar
            def _(act):
                act.wait_ge(root_of, 1)
                nc.scalar.activation(root, norm, ACT.Sqrt).then_inc(rooted, 1)

            @block.vector
            def _(dve):
                chain = core.steps_of(dve)
                dve.sem_inc(sums_stored, 2)
                dve.wait_ge(degrees, 1)
                degree = core.bank(7)[:, 0:BLOCKS]
                chain(nc.vector.tensor_scalar(has_edges, degree, 0.0, None, ALU.is_gt))
                nc.vector.tensor_scalar(norm, degree, 1.0, None, ALU.max).then_inc(root_of, 1)
                dve.wait_ge(rooted, 1)
                chain(nc.vector.reciprocal(norm, root))
                chain(nc.vector.tensor_tensor(norm, norm, has_edges, ALU.mult))
                chain(nc.vector.tensor_tensor(value, core.x[:, :, :], per_node, ALU.mult))
                split_parts(nc, chain, value, parts)
                nc.vector.memset(has_edges, 0.0).then_inc(parts_ready, 1)
                sum_on_vector(dve)
        with nc.Block() as block:
            @block.sync
            def _(sp):
                with core.where_rounded(sp):
                    core.over_low_plane(sp, sums_stored, 2 * BLOCKS + 2)

            @block.tensor
            def _(pe):
                with core.where_rounded(pe):
                    pe.wait_ge(core.exchanged, low_plane_in_again)
                    sum_on_tensor(pe, low=True)

            @block.vector
            def _(dve):
                with core.where_rounded(dve):
                    sum_on_vector(dve, low=True)
        with nc.Block() as block:
            @block.tensor
            def _(pe):
                pe.wait_ge(stack_ready, 1)
                on_tensor(pe)
                pe.wait_ge(core.banks_copied, all_copied)
                pe.wait_ge(loaded, 64)
                for b in range(BLOCKS):
                    last = nc.tensor.matmul(core.psum[:, b * P:(b + 1) * P], wide[:, b * P:(b + 1) * P],
                                            weights[:, :], start=True, stop=True)
                last.then_inc(products, 1)

            @block.scalar
            def _(act):
                on_scalar(act)
                act.wait_ge(norm_of, 1)
                nc.scalar.activation(root, norm, ACT.Sqrt).then_inc(normed, 1)
                layernorm_root(core, act, core.stat, D)

            @block.vector
            def _(dve):
                chain = core.steps_of(dve)
                chain(nc.vector.tensor_tensor(value, value, per_node, ALU.mult))
                nc.vector.tensor_tensor(stack[:, :, D:2 * D], value, core.x[:, :, :], ALU.mult).then_inc(stack_ready, 1)
                dve.wait_ge(loaded, 64)
                dve.wait_ge(products, 1)
                chain(nc.vector.tensor_tensor(stack[:, :, :], core.psum[:, 0:PADDED].rearrange("p (b f) -> p b f", f=P),
                                              bias[:, :, :].to_broadcast([P, BLOCKS, 2 * D]), ALU.add))
                chain(nc.vector.scalar_tensor_tensor(stack[:, :, :], stack[:, :, :], 0.2, stack[:, :, :],
                                                     ALU.mult, ALU.max))
                u, square = stack[:, :, 0:D], stack[:, :, D:2 * D]
                chain(nc.vector.tensor_tensor(u, u, square, ALU.add))
                chain(nc.vector.tensor_tensor(square, u, u, ALU.mult))
                chain(nc.vector.tensor_reduce(norm, square, AX.X, ALU.add))
                nc.vector.tensor_scalar(norm, norm, 1e-12, None, ALU.max).then_inc(norm_of, 1)
                dve.wait_ge(normed, 1)
                chain(nc.vector.reciprocal(norm, root))
                chain(nc.vector.tensor_tensor(u, u, per_node, ALU.mult))
                chain(nc.vector.tensor_tensor(core.x[:, :, :], core.x[:, :, :], u, ALU.add))
                layernorm(core, chain, core.x[:, :, :], u, core.stat)


def gather_rows(core, pool, table, index, staged, rows, used, staged_ready, started, gathered):
    nc = core.nc

    def round_of_groups(r, half):
        for slot in range(RING):
            q = r * RING + slot
            if not (isinstance(r, int) and r == 0):
                pool.wait_ge(used, (q - (RING - 1)) * GROUP)
            if slot == 0:
                nc.gpsimd.tensor_copy(staged[:, half, :], index[:, bass.ds(q * GROUP, RING * GROUP)])\
                  .then_inc(staged_ready, 1)
                pool.wait_ge(staged_ready, r + 1)
            pool.sem_inc(started, 1)
            for u in range(GROUP):
                at = slot * GROUP + u
                nc.gpsimd.indirect_dma_start(
                    out=rows[:, slot, u, :], out_offset=None, in_=table,
                    in_offset=bass.IndirectOffsetOnAxis(ap=staged[:, half, at:at + 1], axis=0))\
                  .then_inc(gathered[slot], 16)

    round_of_groups(0, 0)
    round_of_groups(1, 1)
    with pool.Fori(1, ROUNDS // 2) as two:
        for half in range(2):
            round_of_groups(two * 2 + half, half)


def destination_hots(core, hots, slot, q):
    return core.nc.vector.tensor_tensor(
        hots[:, slot, :, :], core.iota[:, :].unsqueeze(1).to_broadcast([P, GROUP, P]),
        core.dloc[:, bass.ds(q * GROUP, GROUP)].unsqueeze(2).to_broadcast([P, GROUP, P]), ALU.is_equal)


def blocks_of_group(core, engine, q):
    return [engine.value_load(core.block_of[0:1, bass.ds(q * GROUP + u, 1)], min_val=0, max_val=BLOCKS - 1)
            for u in range(0, GROUP, 2)]


def relation_layer(core):
    nc, ins = core.nc, core.ins
    with ExitStack() as stage:
        sem = lambda n: core.sem(n, stage)
        rows, hots, staged, zeros = core.tail_views(
            ([P, RING, GROUP, D], F32), ([P, RING, GROUP, P], F32), ([P, 2, RING * GROUP], I32), ([P, BANK], F32))
        MADE = 3
        weights, x_t = core.sb("r_weights", [P, RELATIONS, D], F32, stage), core.sb("r_x_t", [P, PADDED], F32, stage)
        made = core.sb("r_made", [P, MADE, RELATIONS * D], F32, stage)
        mask0 = core.sb("r_mask0", [P, PADDED], U8, stage)
        table = nc.dram_tensor("relation_table", [PADDED * RELATIONS, D], F32).ap()
        table_rows = table.rearrange("(n r) f -> n (r f)", r=RELATIONS)
        masked, loaded = sem("r_masked"), sem("r_loaded")
        multiplied, evacuated = sem("r_multiplied"), sem("r_evacuated")
        written = [sem(f"r_written{n}") for n in range(MADE)]
        used, gathered = sem("r_used"), [sem(f"r_gathered{n}") for n in range(RING)]
        started = sem("r_started")
        staged_ready, hots_ready, zeros_ready = sem("r_staged"), sem("r_hots"), sem("r_zeros")
        summed = sem("r_summed")
        on_tensor, on_scalar, all_copied = transposed_nodes(core, core.x, D, x_t)
        sums = core.psum[:, 0:BLOCKS * D]
        with nc.Block() as block:
            @block.sync
            def _(sp):
                sp.dma_start(weights[0:D, :, :], ins["w_rel"].rearrange("r i o -> i r o")).then_inc(loaded, 16)
                for b in range(BLOCKS):
                    sp.wait_ge(evacuated, b + 1)
                    sp.dma_start(table_rows[b * P:(b + 1) * P, :], made[:, b % MADE, :])\
                      .then_inc(written[b % MADE], 16)

            @block.gpsimd
            def _(pool):
                pool.wait_ge(masked, BLOCKS)
                for n in range(MADE):
                    pool.wait_ge(written[n], 16 * len(range(n, BLOCKS, MADE)))
                gather_rows(core, pool, table, core.words, staged, rows, used, staged_ready, started, gathered)

            @block.vector
            def _(dve):
                for b in range(BLOCKS):
                    nc.vector.tensor_scalar(core.mask[:, b, :] if b else mask0[:, :], core.counts[:, b, :], 0.0, None,
                                            ALU.is_gt).then_inc(masked, 1)
                    dve.wait_ge(masked, b + 1)
                nc.vector.tensor_copy(core.mask[:, 0, :], mask0[:, :])
                nc.vector.memset(zeros, 0.0).then_inc(zeros_ready, 1)
                for slot in range(RING):
                    destination_hots(core, hots, slot, slot).then_inc(hots_ready, 1)
                with dve.Fori(1, ROUNDS) as r:
                    for slot in range(RING):
                        dve.wait_ge(used, (r * RING + slot - (RING - 1)) * GROUP)
                        destination_hots(core, hots, slot, r * RING + slot).then_inc(hots_ready, 1)
                chain = core.steps_of(dve)
                dve.wait_ge(summed, 1)
                chain(nc.vector.tensor_tensor(core.x[:, :, :], core.x[:, :, :],
                                              sums.rearrange("p (b f) -> p b f", f=D), ALU.add))
                chain(nc.vector.tensor_scalar(core.words[:, :], core.words[:, :], 4, None, ALU.logical_shift_right))
                work = x_t[:, 0:BLOCKS * D].rearrange("p (b f) -> p b f", f=D)
                layernorm(core, chain, core.x[:, :, :], work, core.stat)

            @block.scalar
            def _(act):
                on_scalar(act)
                for b in range(BLOCKS):
                    act.wait_ge(multiplied, b + 1)
                    if b >= MADE:
                        act.wait_ge(written[b % MADE], 16 * (b // MADE))
                    nc.scalar.activation(made[:, b % MADE, :], core.bank(2 * (b % 4), 2), ACT.Copy)\
                      .then_inc(evacuated, 1)
                layernorm_root(core, act, core.stat, D)

            @block.tensor
            def _(pe):
                on_tensor(pe)
                pe.wait_ge(core.banks_copied, all_copied)
                pe.wait_ge(loaded, 16)
                flat = weights[0:D, :, :].rearrange("p r f -> p (r f)")
                for b in range(BLOCKS):
                    if b >= 4:
                        pe.wait_ge(evacuated, b - 3)
                    for n in range(2):
                        last = nc.tensor.matmul(core.bank(2 * (b % 4) + n), x_t[0:D, b * P:(b + 1) * P],
                                                flat[:, n * BANK:(n + 1) * BANK], start=True, stop=True)
                    last.then_inc(multiplied, 1)
                pe.wait_ge(evacuated, BLOCKS)
                pe.wait_ge(zeros_ready, 1)
                for n in range(4):
                    nc.tensor.matmul(core.bank(n), zeros[:, 0:P], zeros, start=True, stop=True,
                                     skip_group_check=True)
                with pe.Fori(0, ROUNDS) as r:
                    for slot in range(RING):
                        q = r * RING + slot
                        blocks = blocks_of_group(core, pe, q)
                        pe.wait_ge(hots_ready, q + 1)
                        pe.wait_ge(gathered[slot], (r + 1) * (16 * GROUP))
                        for u in range(GROUP):
                            b = blocks[u // 2]
                            nc.tensor.matmul(core.psum[:, bass.ds(b * D, D)], hots[:, slot, u, :],
                                             rows[:, slot, u, :], start=False, stop=True,
                                             skip_group_check=True).then_inc(used, 1)
                pe.wait_ge(used, ITEMS)
                pe.sem_inc(summed, 1)


ROW = HD + HEADS
WIDE = HD + 2 * HEADS


ATTENTION_VIEWS = (([P, 2, WIDE], F32), ([P, 2, HD], F32), ([P, HD], F32), ([P, 2, HEADS, P], F32),
                   ([P, 2, PADDED], F32))


def attention_weights(core, layer, sem):
    nc, ins = core.nc, core.ins
    depth = D if layer == 0 else HD
    halves, rows_used = -(-depth // P), min(depth, P)
    weights, vectors, product, repeated = core.tail_views(*ATTENTION_VIEWS)[:4]
    loaded = sem("weights_loaded")

    def on_sync(sp):
        w = ins[f"w_gat{layer}"]
        for n in range(halves):
            sp.dma_start(weights[0:rows_used, n, 0:HD], w[n * P:n * P + rows_used, :]).then_inc(loaded, 16)
        for n, name in enumerate(("att_src", "att_dst")):
            sp.dma_start(vectors[:, n, :], ins[f"{name}{layer}"].to_broadcast([P, HD])).then_inc(loaded, 16)

    def on_vector(dve):
        chain = core.steps_of(dve)
        dve.wait_ge(loaded, 16 * (halves + 2))
        for n in range(halves):
            for which in range(2):
                chain(nc.vector.tensor_tensor(product[0:rows_used, :], weights[0:rows_used, n, 0:HD],
                                              vectors[0:rows_used, which, :], ALU.mult))
                at = HD + which * HEADS
                chain(nc.vector.tensor_reduce(weights[0:rows_used, n, at:at + HEADS],
                                              product[0:rows_used, :].rearrange("p (h c) -> p h c", h=HEADS),
                                              AX.X, ALU.add))
            chain(nc.vector.tensor_copy(repeated[0:rows_used, n, :, :],
                                        weights[0:rows_used, n, HD:HD + HEADS].unsqueeze(2)
                                        .to_broadcast([rows_used, HEADS, P])))

    return on_sync, on_vector


def attention_layer(core, acc, layer):
    nc = core.nc
    depth = D if layer == 0 else HD
    halves = -(-depth // P)
    rows_used = min(depth, P)
    with ExitStack() as stage:
        sb = lambda *a: core.sb(*a, stage)
        sem = lambda n: core.sem(f"a{layer}_{n}", stage)
        weights, _, _, repeated, turned = core.tail_views(*ATTENTION_VIEWS)
        level, masked_out = core.tail_views(*ATTENTION_VIEWS, ([P, 2, PADDED], F32), ([P, 2, PADDED], BF16))[-2:]
        rows, hots, hots_t = core.tail_views(*ATTENTION_VIEWS, ([P, RING, GROUP, ROW], F32),
                                             ([P, RING, GROUP, P], F32), ([P, 2, GROUP, P], F32))[-3:]
        logits = sb(f"a{layer}_logits", [P, 2, GROUP, HEADS], F32)
        staged = sb(f"a{layer}_staged", [P, 2, RING * GROUP], I32)
        at_dst = sb(f"a{layer}_at_dst", [P, BLOCKS, 2 * HEADS], F32)
        at_block = sb(f"a{layer}_at_block", [P, 2, GROUP // 2, 2 * HEADS], F32)
        own = sb(f"a{layer}_own", [P, BLOCKS, HEADS], F32)
        best = sb(f"a{layer}_best", [P, BLOCKS, HEADS], F32)
        least = sb(f"a{layer}_least", [P, HEADS], F32)
        table = nc.dram_tensor(f"attention_table{layer}", [PADDED, ROW], F32).ap()
        projected, evacuated, written = (sem(n) for n in ("projected", "evac", "written"))
        levels_in_psum, levels_ready, level_used = sem("lpsum"), sem("levels"), sem("lused")
        node_logits, self_ready = sem("nlogits"), sem("self")
        self_of, pass_ready = sem("self_of"), sem("pass_ready")
        gathered = [sem(f"gathered{n}") for n in range(RING)]
        staged_ready, started, hots_ready = sem("staged_s"), sem("started"), sem("hots_s")
        turned_in_psum, turned_ready, fetched = sem("tpsum"), sem("turned"), sem("fetched")
        picked = sem("picked")
        logits_ready, exps_ready, messages_ready = sem("logits_s"), sem("exps"), sem("messages")
        used, stored, logit_steps = sem("used"), sem("stored"), sem("lsteps")
        hots_psum = [core.bank(k)[:, 0:GROUP * P].rearrange("p (u e) -> p u e", u=GROUP) for k in (0, 1)]
        fetch_psum = [core.bank(k)[:, 0:GROUP * 2 * HEADS]
                      .rearrange("p (u h) -> p u h", u=GROUP) for k in (2, 7)]
        sums = [[core.bank(3 + k * (GROUP // 2) + pair)[:, 0:ROW] for pair in range(GROUP // 2)] for k in (0, 1)]

        def levels_of(pe, h):
            for c, (lo, hi) in enumerate(CHUNKS):
                if h > 1:
                    pe.wait_ge(levels_ready, (h - 1) * len(CHUNKS) + c + 1)
                for n in range(halves):
                    last = nc.tensor.matmul(core.psum[:, lo:hi], repeated[0:rows_used, n, h, :],
                                            turned[0:rows_used, n, lo:hi],
                                            start=(n == 0), stop=(n == halves - 1))
                last.then_inc(levels_in_psum, 1)

        def keep_levels(act, h):
            if h >= 2:
                act.wait_ge(level_used, h - 1)
            for c, (lo, hi) in enumerate(CHUNKS):
                act.wait_ge(levels_in_psum, h * len(CHUNKS) + c + 1)
                nc.scalar.activation(level[:, h % 2, lo:hi], core.psum[:, lo:hi], ACT.Copy).then_inc(levels_ready, 1)

        with nc.Block() as block:
            @block.sync
            def _(sp):
                sp.wait_ge(evacuated, BLOCKS)
                sp.dma_start(table.rearrange("(b p) c -> p b c", p=P), acc[:, :, 0:ROW]).then_inc(written, 16)

            @block.gpsimd
            def _(pool):
                pool.wait_ge(written, 16)
                pool.wait_ge(pass_ready, 1)
                gather_rows(core, pool, table, core.words, staged, rows, used, staged_ready, started, gathered)

            @block.tensor
            def _(pe):
                levels_of(pe, 0)
                pe.wait_ge(levels_ready, len(CHUNKS))
                for b in range(BLOCKS):
                    if b >= 8:
                        pe.wait_ge(evacuated, b - 7)
                    for n in range(halves):
                        last = nc.tensor.matmul(core.bank(b % 8)[:, 0:WIDE],
                                                turned[0:rows_used, n, b * P:(b + 1) * P], weights[0:rows_used, n, :],
                                                start=(n == 0), stop=(n == halves - 1))
                    last.then_inc(projected, 1)
                pe.wait_ge(evacuated, BLOCKS)
                for h in range(1, HEADS):
                    levels_of(pe, h)
                pe.wait_ge(levels_ready, HEADS * len(CHUNKS))
                pe.wait_ge(pass_ready, 1)

                def turn_hots(q, slot):
                    pe.wait_ge(hots_ready, q + 1)
                    if not (isinstance(q, int) and q < 2):
                        pe.wait_ge(turned_ready, q - 1)
                    for u in range(GROUP):
                        last = nc.tensor.transpose(hots_psum[slot % 2][:, u, :], hots[:, slot, u, :], core.ident[:, :])
                    last.then_inc(turned_in_psum, 1)

                def fetch(q, slot):
                    pe.wait_ge(turned_ready, q + 1)
                    pe.wait_ge(picked, (q + 1) * (GROUP // 2))
                    for u in range(GROUP):
                        last = nc.tensor.matmul(fetch_psum[slot % 2][:, u, :], hots_t[:, slot % 2, u, :],
                                                at_block[:, slot % 2, u // 2, :], start=True, stop=True)
                    last.then_inc(fetched, 1)

                def add_up(q, slot, first):
                    pe.wait_ge(messages_ready, q + 1)
                    for pair in range(GROUP // 2):
                        if not first:
                            pe.wait_ge(stored, q * (GROUP // 2) + (pair + 1 - GROUP))
                        for u in (2 * pair, 2 * pair + 1):
                            nc.tensor.matmul(sums[slot % 2][pair], hots[:, slot, u, :], rows[:, slot, u, :],
                                             start=(u % 2 == 0), stop=(u % 2 == 1)).then_inc(used, 1)

                def turn(r, slot, first=False, left=2):
                    q = r * RING + slot
                    if left >= 1:
                        fetch(q + 1, (slot + 1) % RING)
                    if left >= 2:
                        turn_hots(q + 2, (slot + 2) % RING)
                    add_up(q, slot, first)

                turn_hots(0, 0)
                turn_hots(1, 1)
                fetch(0, 0)
                for slot in range(RING):
                    turn(0, slot, first=slot < 2)
                with pe.Fori(1, ROUNDS - 1) as r:
                    for slot in range(RING):
                        turn(r, slot)
                for slot in range(RING):
                    turn(ROUNDS - 1, slot, left=RING - 1 - slot)

            @block.scalar
            def _(act):
                keep_levels(act, 0)
                for b in range(BLOCKS):
                    act.wait_ge(projected, b + 1)
                    nc.scalar.activation(acc[:, b, :], core.bank(b % 8)[:, 0:WIDE], ACT.Copy).then_inc(evacuated, 1)
                for h in range(1, HEADS):
                    keep_levels(act, h)
                act.wait_ge(node_logits, 1)
                nc.scalar.activation(own[:, :, :], own[:, :, :], ACT.Exp).then_inc(self_ready, 1)
                act.wait_ge(pass_ready, 1)

                def pick_blocks(q, slot):
                    if not (isinstance(q, int) and q < 2):
                        act.wait_ge(fetched, q - 1)
                    for pair, b in enumerate(blocks_of_group(core, act, q)):
                        nc.scalar.activation(at_block[:, slot % 2, pair, :], at_dst[:, bass.ds(b, 1), :]
                                             .rearrange("p b h -> p (b h)"), ACT.Copy).then_inc(picked, 1)

                def keep_turned(q, slot):
                    act.wait_ge(turned_in_psum, q + 1)
                    nc.scalar.activation(hots_t[:, slot % 2, :, :], hots_psum[slot % 2], ACT.Copy)\
                      .then_inc(turned_ready, 1)

                def weights_of(q, slot):
                    act.wait_ge(logits_ready, q + 1)
                    nc.scalar.activation(rows[:, slot, :, HD:ROW], logits[:, slot % 2, :, :], ACT.Exp)\
                      .then_inc(exps_ready, 1)

                def turn(r, slot, left=2):
                    q = r * RING + slot
                    if left >= 2:
                        pick_blocks(q + 2, (slot + 2) % RING)
                    if left >= 1:
                        weights_of(q + 1, (slot + 1) % RING)
                    if left >= 2:
                        keep_turned(q + 2, (slot + 2) % RING)

                pick_blocks(0, 0)
                pick_blocks(1, 1)
                keep_turned(0, 0)
                keep_turned(1, 1)
                weights_of(0, 0)
                for slot in range(RING):
                    turn(0, slot)
                with act.Fori(1, ROUNDS - 1) as r:
                    for slot in range(RING):
                        turn(r, slot)
                for slot in range(RING):
                    turn(ROUNDS - 1, slot, left=RING - 1 - slot)

            @block.vector
            def _(dve):
                chain = core.steps_of(dve)
                for h in range(HEADS):
                    dve.wait_ge(levels_ready, (h + 1) * len(CHUNKS))
                    of_head = level[:, h % 2, 0:NODES]
                    chain(nc.vector.tensor_reduce(least[:, h:h + 1], of_head, AX.X, ALU.min))
                    chain(nc.vector.tensor_scalar(of_head, of_head, least[:, h:h + 1], None,
                                                  ALU.subtract))
                    for b in range(BLOCKS):
                        chain.overlapped(nc.vector.tensor_tensor_reduce(
                            out=masked_out[:, b % 2, 0:NODES], in0=core.mask[:, b, 0:NODES],
                            in1=of_head, scale=1.0, scalar=0.0,
                            op0=ALU.mult, op1=ALU.max, accum_out=best[:, b, h:h + 1]))
                    dve.wait_ge(chain.semaphore, chain.count)
                    dve.sem_inc(level_used, 1)
                a_src, a_dst = acc[:, :, HD:ROW], acc[:, :, ROW:WIDE]
                dve.wait_ge(evacuated, BLOCKS)
                highest = at_dst[:, :, HEADS:2 * HEADS]
                chain(nc.vector.tensor_tensor(best[:, :, :], best[:, :, :],
                                              least[:, :].unsqueeze(1).to_broadcast([P, BLOCKS, HEADS]), ALU.add))
                chain(nc.vector.tensor_tensor(best[:, :, :], best[:, :, :], a_src, ALU.max))
                chain(nc.vector.tensor_tensor(best[:, :, :], best[:, :, :], a_dst, ALU.add))
                chain(nc.vector.scalar_tensor_tensor(highest, best[:, :, :], 0.2, best[:, :, :], ALU.mult, ALU.max))
                chain(nc.vector.tensor_copy(at_dst[:, :, 0:HEADS], a_dst))
                chain(nc.vector.tensor_tensor(own[:, :, :], a_src, a_dst, ALU.add))
                chain(nc.vector.scalar_tensor_tensor(own[:, :, :], own[:, :, :], 0.2, own[:, :, :],
                                                     ALU.mult, ALU.max))
                nc.vector.tensor_tensor(own[:, :, :], own[:, :, :], highest, ALU.subtract).then_inc(node_logits, 1)
                dve.wait_ge(self_ready, 1)
                dve.wait_ge(written, 16)
                by_head = acc[:, :, 0:HD].rearrange("p b (h c) -> p b h c", h=HEADS)
                chain(nc.vector.tensor_tensor(by_head, by_head,
                                              own[:, :, :].unsqueeze(3).to_broadcast([P, BLOCKS, HEADS, D]), ALU.mult))
                chain(nc.vector.tensor_copy(a_src, own[:, :, :]))
                dve.sem_inc(pass_ready, 1)

                def weigh_logits(q, slot):
                    e, of_dst = logits[:, slot % 2, :, :], fetch_psum[slot % 2]
                    dve.wait_ge(fetched, q + 1)
                    dve.wait_ge(gathered[slot], (q - slot + RING) * (16 * GROUP // RING))
                    nc.vector.tensor_tensor(e, rows[:, slot, :, HD:ROW], of_dst[:, :, 0:HEADS],
                                            ALU.add).then_inc(logit_steps, 1)
                    yield
                    dve.wait_ge(logit_steps, q * 3 + 1)
                    nc.vector.scalar_tensor_tensor(e, e, 0.2, e, ALU.mult, ALU.max).then_inc(logit_steps, 1)
                    yield
                    dve.wait_ge(logit_steps, q * 3 + 2)
                    nc.vector.tensor_tensor(e, e, of_dst[:, :, HEADS:2 * HEADS], ALU.subtract)\
                      .then_inc(logit_steps, 1)
                    yield
                    dve.wait_ge(logit_steps, q * 3 + 3)
                    nc.vector.tensor_scalar(e, e, 0.0, None, ALU.min).then_inc(logits_ready, 1)

                def weigh_rows(q, slot):
                    dve.wait_ge(exps_ready, q + 1)
                    message = rows[:, slot, :, 0:HD].rearrange("p u (h c) -> p u h c", h=HEADS)
                    nc.vector.tensor_tensor(message, message,
                                            rows[:, slot, :, HD:ROW].unsqueeze(3).to_broadcast([P, GROUP, HEADS, D]),
                                            ALU.mult).then_inc(messages_ready, 1)

                def store(q, slot, pair, b):
                    dve.wait_ge(used, q * GROUP + 2 * (pair + 1))
                    if not (isinstance(q, int) and q == 0 and pair == 0):
                        dve.wait_ge(stored, q * (GROUP // 2) + pair)
                    nc.vector.tensor_tensor(acc[:, bass.ds(b, 1), 0:ROW], acc[:, bass.ds(b, 1), 0:ROW],
                                            sums[slot % 2][pair].unsqueeze(1), ALU.add).then_inc(stored, 1)

                def turn(r, slot, before=1, left=RING - 1):
                    q = r * RING + slot
                    blocks = blocks_of_group(core, dve, q - 1) if before else None
                    weigh_rows(q, slot)
                    steps = weigh_logits(q + 1, (slot + 1) % RING) if left >= 1 else iter(())
                    for pair in range(GROUP // 2):
                        next(steps, None)
                        if before:
                            store(q - 1, (slot - 1) % RING, pair, blocks[pair])
                    next(steps, None)
                    if left >= RING - 1:
                        destination_hots(core, hots, (slot - 1) % RING, q + RING - 1).then_inc(hots_ready, 1)
                    next(steps, None)

                for slot in range(RING - 1):
                    destination_hots(core, hots, slot, slot).then_inc(hots_ready, 1)
                for _ in weigh_logits(0, 0):
                    pass
                for slot in range(RING):
                    turn(0, slot, before=slot)
                with dve.Fori(1, ROUNDS - 1) as r:
                    for slot in range(RING):
                        turn(r, slot)
                for slot in range(RING):
                    turn(ROUNDS - 1, slot, left=RING - 1 - slot)
                for pair, b in enumerate(blocks_of_group(core, dve, GROUPS - 1)):
                    store(GROUPS - 1, RING - 1, pair, b)


def attention_layers(core):
    nc, ins = core.nc, core.ins
    turned, across = core.tail_views(*ATTENTION_VIEWS, ([P, PADDED], F32))[-2:]
    acc = core.sb("acc", [P, BLOCKS, WIDE], F32)
    head_bias, head_affine = core.sb("head_bias", [P, 1, HD], F32), core.sb("head_affine", [P, 2, HD // P], F32)
    with ExitStack() as stage:
        sem = lambda n: core.sem(n, stage)
        weights = core.sb("p_weights", [P, D], F32, stage)
        types, types_f = core.sb("type_of", [P, BLOCKS], I32, stage), core.sb("type_of_f", [P, BLOCKS], F32, stage)
        depth = D + NODE_TYPES + 1
        given, loaded = sem("j_given"), sem("j_loaded")
        weights_on_sync, weights_on_vector = attention_weights(core, 0, lambda n: sem(f"j_{n}"))
        products, turned_out = sem("j_products"), sem("j_out")
        on_tensor, on_scalar, all_copied = transposed_nodes(core, acc[:, :, 0:depth], depth, across)
        with nc.Block() as block:
            @block.sync
            def _(sp):
                sp.dma_start(types[:, :], ins["types"]).then_inc(loaded, 16)
                sp.dma_start(weights[0:D, :], ins["w_proj"]).then_inc(loaded, 16)
                sp.dma_start(weights[D:D + NODE_TYPES, :], ins["type_emb"]).then_inc(loaded, 16)
                sp.dma_start(weights[depth - 1:depth, :], ins["b_proj"]).then_inc(loaded, 16)
                sp.dma_start(head_bias[:, 0, :], ins["bias0"].to_broadcast([P, HD])).then_inc(loaded, 16)
                for n, name in enumerate(("gain0", "shift0")):
                    sp.dma_start(head_affine[:, n, :], ins[name]).then_inc(loaded, 16)
                weights_on_sync(sp)
                sp.wait_ge(loaded, 16 * 7)

            @block.vector
            def _(dve):
                chain = core.steps_of(dve)
                chain(nc.vector.tensor_copy(acc[:, :, 0:D], core.x[:, :, :]))
                dve.wait_ge(loaded, 16 * 7)
                chain(nc.vector.tensor_copy(types_f[:, :], types[:, :]))
                for t in range(NODE_TYPES):
                    chain(nc.vector.tensor_scalar(acc[:, :, D + t:D + t + 1], types_f[:, :].unsqueeze(2), float(t),
                                                  None, ALU.is_equal))
                nc.vector.memset(acc[:, :, depth - 1:depth], 1.0).then_inc(given, 1)
                weights_on_vector(dve)

            @block.tensor
            def _(pe):
                pe.wait_ge(given, 1)
                on_tensor(pe)
                pe.wait_ge(core.banks_copied, all_copied)
                for lo, hi in CHUNKS:
                    nc.tensor.matmul(core.psum[0:D, lo:hi], weights[0:depth, :], across[0:depth, lo:hi],
                                     start=True, stop=True).then_inc(products, 1)

            @block.scalar
            def _(act):
                on_scalar(act)
                for n, (lo, hi) in enumerate(CHUNKS):
                    act.wait_ge(products, n + 1)
                    nc.scalar.activation(turned[0:D, 0, lo:hi], core.psum[0:D, lo:hi], ACT.Copy)\
                      .then_inc(turned_out, 1)
    attention_layer(core, acc, 0)

    with ExitStack() as stage:
        sem = lambda n: core.sem(n, stage)
        share = core.sb("m_share", [P, BLOCKS, HEADS], F32, stage)
        work = core.tail_views(*ATTENTION_VIEWS, ([P, BLOCKS, HD], F32))[-1]
        weights_on_sync, weights_on_vector = attention_weights(core, 1, lambda n: sem(f"m_{n}"))
        normed = sem("m_normed")
        banks_ready, copied = sem("m_banks"), sem("m_copied")
        hidden = acc[:, :, 0:HD]
        by_head = hidden.rearrange("p b (h c) -> p b h c", h=HEADS)
        with nc.Block() as block:
            @block.sync
            def _(sp):
                weights_on_sync(sp)

            @block.vector
            def _(dve):
                chain = core.steps_of(dve)
                chain(nc.vector.tensor_scalar(share[:, :, :], acc[:, :, HD:ROW], 1e-16, None, ALU.add))
                chain(nc.vector.reciprocal(share[:, :, :], share[:, :, :]))
                chain(nc.vector.tensor_tensor(by_head, by_head,
                                              share[:, :, :].unsqueeze(3).to_broadcast([P, BLOCKS, HEADS, D]), ALU.mult))
                chain(nc.vector.tensor_tensor(hidden, hidden, head_bias[:, :, :].to_broadcast([P, BLOCKS, HD]),
                                              ALU.add))
                layernorm(core, chain, hidden, work, core.stat)
                dve.sem_inc(normed, 1)
                weights_on_vector(dve)

            @block.scalar
            def _(act):
                layernorm_root(core, act, core.stat, HD)
                for half in range(2):
                    for n, (lo, hi) in enumerate(CHUNKS):
                        act.wait_ge(banks_ready, half * len(CHUNKS) + n + 1)
                        nc.scalar.activation(turned[:, half, lo:hi], core.psum[:, lo:hi], ACT.Relu,
                                             bias=head_affine[:, 1, half:half + 1],
                                             scale=head_affine[:, 0, half:half + 1]).then_inc(copied, 1)

            @block.tensor
            def _(pe):
                pe.wait_ge(normed, 1)
                for half in range(2):
                    for b in range(BLOCKS):
                        if half and b % 4 == 0:
                            pe.wait_ge(copied, b // 4 + 1)
                        last = nc.tensor.transpose(core.psum[:, b * P:(b + 1) * P],
                                                   acc[:, b, half * P:(half + 1) * P], core.ident[:, :])
                        if b % 4 == 3 or b == BLOCKS - 1:
                            last.then_inc(banks_ready, 1)
    attention_layer(core, acc, 1)

    with ExitStack() as stage:
        sem = lambda n: core.sem(n, stage)
        share = core.sb("f_share", [P, BLOCKS, HEADS], F32, stage)
        affine = core.sb("f_affine", [P, 3, D], F32, stage)
        work = core.tail_views(([P, BLOCKS, D], F32))[0]
        mean = acc[:, :, 0:D]
        loaded, done, stored = (sem(f"f_{n}") for n in ("loaded", "done", "stored"))
        hidden = acc[:, :, 0:HD]
        by_head = hidden.rearrange("p b (h c) -> p b h c", h=HEADS)
        with nc.Block() as block:
            @block.sync
            def _(sp):
                for n, name in enumerate(("bias1", "gain1", "shift1")):
                    sp.dma_start(affine[:, n, :], ins[name].to_broadcast([P, D])).then_inc(loaded, 16)
                sp.wait_ge(done, 1)
                sp.dma_start(core.out, core.x[:, :, :]).then_inc(stored, 16)
                sp.wait_ge(stored, 16)

            @block.vector
            def _(dve):
                chain = core.steps_of(dve)
                chain(nc.vector.tensor_scalar(share[:, :, :], acc[:, :, HD:ROW], 1e-16, None, ALU.add))
                chain(nc.vector.reciprocal(share[:, :, :], share[:, :, :]))
                chain(nc.vector.tensor_tensor(by_head, by_head,
                                              share[:, :, :].unsqueeze(3).to_broadcast([P, BLOCKS, HEADS, D]), ALU.mult))
                for h in range(1, HEADS):
                    chain(nc.vector.tensor_tensor(mean, mean, acc[:, :, h * D:(h + 1) * D], ALU.add))
                rows = lambda n: affine[:, n:n + 1, :].to_broadcast([P, BLOCKS, D])
                dve.wait_ge(loaded, 48)
                chain(nc.vector.tensor_scalar(mean, mean, 1.0 / HEADS, None, ALU.mult))
                chain(nc.vector.tensor_tensor(mean, mean, rows(0), ALU.add))
                layernorm(core, chain, mean, work, core.stat)
                chain(nc.vector.tensor_tensor(mean, mean, rows(1), ALU.mult))
                chain(nc.vector.tensor_tensor(mean, mean, rows(2), ALU.add))
                chain(nc.vector.scalar_tensor_tensor(core.x[:, :, :], mean, 0.0, core.x[:, :, :], ALU.max, ALU.add))
                layernorm(core, chain, core.x[:, :, :], work, core.stat)
                dve.sem_inc(done, 1)

            @block.scalar
            def _(act):
                for _ in range(2):
                    layernorm_root(core, act, core.stat, D)


def build(nc, ins, out, debug=None):
    with ExitStack() as ctx:
        core = Core(nc, ctx, ins, out)
        prepare(core)
        count_edges(core)
        bilinear_layer(core)
        interaction_layer(core)
        relation_layer(core)
        attention_layers(core)
        if debug:
            debug(core)


_VECTORS = {"b_f": "L0_gnn_b1", "b_xf": "L0_gnn_b2", "b_gcn": "L1_gnn_b_gcn", "b_int": "L1_gnn_b_int",
            "b_proj": "L3_gnn_proj_b", "bias0": "L3_gnn_bias0", "gain0": "L3_gnn_ln0_g", "shift0": "L3_gnn_ln0_b",
            "bias1": "L3_gnn_bias1", "gain1": "L3_gnn_ln1_g", "shift1": "L3_gnn_ln1_b",
            "att_src0": "L3_gnn_att_src0", "att_dst0": "L3_gnn_att_dst0",
            "att_src1": "L3_gnn_att_src1", "att_dst1": "L3_gnn_att_dst1"}
_MATRICES = {"w_f": "L0_gnn_W1", "w_xf": "L0_gnn_W2", "w_gcn": "L1_gnn_W_gcn", "w_int": "L1_gnn_W_int",
             "w_rel": "L2_gnn_weight", "w_proj": "L3_gnn_proj_W", "type_emb": "L3_gnn_type_emb",
             "w_gat0": "L3_gnn_W0", "w_gat1": "L3_gnn_W1"}


def laid_out(inputs):
    def edges(name, fill):
        a = np.asarray(inputs[name])
        a = np.concatenate([a, np.full(TILES * P - a.size, fill, a.dtype)])
        return np.ascontiguousarray(a.reshape(TILES, P).T)

    x = np.asarray(inputs["x"])
    x = np.concatenate([x, np.zeros((PADDED - NODES, D), x.dtype)]).reshape(BLOCKS, P, D)
    types = np.asarray(inputs["node_type_3"])
    types = np.concatenate([types, np.zeros(PADDED - NODES, types.dtype)]).reshape(BLOCKS, P).T
    arrays = {"src": edges("src", 0), "dst": edges("dst", NO_NODE), "rel": edges("edge_type_16", 0),
              "x": np.ascontiguousarray(x.transpose(1, 0, 2)), "types": np.ascontiguousarray(types)}
    arrays |= {n: np.asarray(inputs[k]).reshape(1, -1) for n, k in _VECTORS.items()}
    arrays |= {n: np.asarray(inputs[k]) for n, k in _MATRICES.items()}
    for n in ("gain0", "shift0"):
        arrays[n] = np.ascontiguousarray(arrays[n].reshape(HD // P, P).T)
    return arrays


def kernel(**inputs):
    import concourse.bacc as bacc
    from concourse.bass_utils import run_bass_kernel_spmd

    nc = bacc.Bacc("TRN2", target_bir_lowering=False, num_devices=1)
    arrays = laid_out(inputs)
    ins = {name: nc.dram_tensor(f"in_{name}", a.shape, mybir.dt.from_np(a.dtype), kind="ExternalInput").ap()
           for name, a in arrays.items()}
    out = nc.dram_tensor("out_nodes", [P, BLOCKS, D], F32, kind="ExternalOutput").ap()
    build(nc, ins, out)
    result = run_bass_kernel_spmd(nc, [{f"in_{name}": a for name, a in arrays.items()}], core_ids=[0])
    nodes = result.results[0]["out_nodes"]
    return np.ascontiguousarray(nodes.transpose(1, 0, 2)).reshape(PADDED, D)[:NODES]
```
